# Optimizing a Trainium2 kernel written in Bass

```python
import numpy as np
import jax
import jax.numpy as jnp

def _softmax(x, axis=-1):
    return jax.nn.softmax(x, axis=axis)

def _gelu(x):
    return jax.nn.gelu(x, approximate=True)

def _silu(x):
    return jax.nn.silu(x)

def _sigmoid(x):
    return jax.nn.sigmoid(x)

def _layernorm(x, axis=-1, eps=1e-05):
    m = jnp.mean(x, axis=axis, keepdims=True)
    v = jnp.var(x, axis=axis, keepdims=True)
    return (x - m) / jnp.sqrt(v + eps)

def _scatter_add(tgt, idx, src, axis=0):
    return tgt.at[idx].add(src)

def _segment_sum(src, seg, n):
    return jax.ops.segment_sum(src, seg, n)
kernel_name = 'mk_vit_tower_cls_d2_tok_img768_r4_fc6875'

def setup_inputs(seed: int=0):
    np.random.seed(seed)
    _w = jnp.asarray

    def _rec_inputs():
        import jax
        import jax.numpy as jnp
        _rk = jax.random.key(seed)
        x = -0.000125008 + 0.999885 * jax.random.normal(jax.random.fold_in(_rk, 1), (8, 1, 256, 256), jnp.float32)
        cls_tok = 0.02 * jax.random.normal(jax.random.fold_in(_rk, 5), (1, 1, 192), jnp.float32)
        return (x, cls_tok)
    x, cls_tok = _rec_inputs()

    def _L0_tok_setup():
        import jax, jax.numpy as jnp
        import numpy as np
        C, H, W = (1, 256, 256)
        P = 32
        D_TOK = 192
        B = 32
        D_PATCH = C * P * P

        def _patchify(x):
            Bx = x.shape[0]
            x = x.reshape(Bx, C, H // P, P, W // P, P)
            x = x.transpose(0, 2, 4, 1, 3, 5)
            return x.reshape(Bx, H // P * (W // P), D_PATCH)
        key = jax.random.key(seed)
        k_x, k_w, k_b = jax.random.split(key, 3)
        x = jax.random.normal(k_x, (B, C, H, W), dtype=jnp.float32)
        bound = 1.0 / np.sqrt(D_PATCH)
        w = jax.random.uniform(k_w, (D_TOK, D_PATCH), jnp.float32, -bound, bound)
        b = jax.random.uniform(k_b, (D_TOK,), jnp.float32, -bound, bound)
        return {'x': x, 'w': w, 'b': b}
    _L0_tok_all = _L0_tok_setup()
    _L0_tok_in = {k: v for k, v in _L0_tok_all.items() if k in ('w', 'b')}
    del _L0_tok_all

    def _L0_attn_setup():
        import jax, jax.numpy as jnp
        import numpy as np
        B, S, D = (2, 1024, 192)
        key = jax.random.key(seed)
        kx, kq, kk, kv, ko = jax.random.split(key, 5)
        x = jax.random.normal(kx, (B, S, D), dtype=jnp.float32)
        Wq = 0.01 * jax.random.normal(kq, (D, D), dtype=jnp.float32)
        Wk = 0.01 * jax.random.normal(kk, (D, D), dtype=jnp.float32)
        Wv = 0.01 * jax.random.normal(kv, (D, D), dtype=jnp.float32)
        Wo = 0.01 * jax.random.normal(ko, (D, D), dtype=jnp.float32)
        return {'x': x, 'Wq': Wq, 'Wk': Wk, 'Wv': Wv, 'Wo': Wo}
    _L0_attn_all = _L0_attn_setup()
    _L0_attn_in = {k: v for k, v in _L0_attn_all.items() if k in ('Wq', 'Wk', 'Wv', 'Wo')}
    del _L0_attn_all

    def _L0_ffn_setup():
        import jax, jax.numpy as jnp
        import numpy as np
        B, T, C = (2, 256, 192)
        H, NE, K = (768, 8, 2)
        key = jax.random.key(seed)
        k1, k2, k3, k4 = jax.random.split(key, 4)
        x = jax.random.normal(k1, (B, T, C), dtype=jnp.float32)
        w_fc = jax.random.normal(k2, (C, H * NE), dtype=jnp.float32) * 0.02
        w_proj = jax.random.normal(k3, (H * NE, C), dtype=jnp.float32) * (0.02 * (2 * 12) ** (-0.5))
        w_gate = jax.random.normal(k4, (C, NE), dtype=jnp.float32) * 0.02
        return {'x': x, 'w_fc': w_fc, 'w_proj': w_proj, 'w_gate': w_gate}
    _L0_ffn_all = _L0_ffn_setup()
    _L0_ffn_in = {k: v for k, v in _L0_ffn_all.items() if k in ('w_fc', 'w_proj', 'w_gate')}
    del _L0_ffn_all

    def _L1_attn_setup():
        import jax, jax.numpy as jnp
        import numpy as np
        NUM_HEADS = 12
        ACT_BITS = 8
        W_BITS = 8
        EXP_COEF = (0.35815147, 0.96963238, 1.0)
        LN2 = 0.6931471805599453
        N_EXP = 30

        def ste_round(x):
            return x + jax.lax.stop_gradient(jnp.round(x) - x)

        def fq_act(x, bits=ACT_BITS):
            mn = jax.lax.stop_gradient(jnp.min(x))
            mx = jax.lax.stop_gradient(jnp.max(x))
            qmax = 2.0 ** bits - 1.0
            scale = jnp.maximum((mx - mn) / qmax, 1e-08)
            zero = jnp.round(-mn / scale)
            q = jnp.clip(ste_round(x / scale) + zero, 0.0, qmax)
            return ((q - zero) * scale, scale)

        def fq_weight(w, bits=W_BITS):
            amax = jax.lax.stop_gradient(jnp.max(jnp.abs(w), axis=1, keepdims=True))
            qmax = 2.0 ** (bits - 1) - 1.0
            scale = jnp.maximum(amax / qmax, 1e-08)
            q = jnp.clip(ste_round(w / scale), -qmax - 1.0, qmax)
            return q * scale

        def int_softmax(x, scale):
            a, b, c = EXP_COEF
            x_int = ste_round(x / scale)
            x_int = x_int - jnp.max(x_int, axis=-1, keepdims=True)
            x0_int = jnp.floor(-LN2 / scale)
            x_int = jnp.maximum(x_int, N_EXP * x0_int)
            qexp = jnp.floor(x_int / x0_int)
            r = x_int - x0_int * qexp
            b_int = jnp.floor(b / a / scale)
            c_int = jnp.floor(c / a / (scale * scale))
            p_int = r * (r + b_int) + c_int
            e = p_int * jnp.exp2(-qexp) * (a * scale * scale)
            return e / jnp.sum(e, axis=-1, keepdims=True)
        key = jax.random.key(seed)
        ks = jax.random.split(key, 5)
        B, N, C = (64, 197, 192)
        x = jax.random.normal(ks[0], (B, N, C), dtype=jnp.float32)
        w_qkv = jax.random.normal(ks[1], (3 * C, C), dtype=jnp.float32) * 0.02
        b_qkv = jax.random.normal(ks[2], (3 * C,), dtype=jnp.float32) * 0.02
        w_proj = jax.random.normal(ks[3], (C, C), dtype=jnp.float32) * 0.02
        b_proj = jax.random.normal(ks[4], (C,), dtype=jnp.float32) * 0.02
        return {'x': x, 'w_qkv': w_qkv, 'b_qkv': b_qkv, 'w_proj': w_proj, 'b_proj': b_proj}
    _L1_attn_all = _L1_attn_setup()
    _L1_attn_in = {k: v for k, v in _L1_attn_all.items() if k in ('w_qkv', 'b_qkv', 'w_proj', 'b_proj')}
    del _L1_attn_all

    def _L1_ffn_setup():
        import jax, jax.numpy as jnp
        import numpy as np
        N_EMBD = 192
        EXPERT_SIZES = [(8, 128), (8, 256)]
        TOP_K = 8
        NORM_TOPK_PROB = True
        EXPERT_WIDTHS = []
        for cnt, w in EXPERT_SIZES:
            EXPERT_WIDTHS += [w] * cnt
        EXPERT_OFFSETS = np.concatenate([[0], np.cumsum(EXPERT_WIDTHS)]).astype(np.int64)
        NUM_EXPERTS = len(EXPERT_WIDTHS)
        TOTAL_WIDTH = int(EXPERT_OFFSETS[-1])
        key = jax.random.key(seed)
        k1, k2, k3, k4 = jax.random.split(key, 4)
        x = jax.random.normal(k1, (1, 512, N_EMBD), dtype=jnp.float32)
        router_w = jax.random.normal(k2, (NUM_EXPERTS, N_EMBD), dtype=jnp.float32) * 0.02
        w1 = jnp.clip(jax.random.normal(k3, (N_EMBD, TOTAL_WIDTH), dtype=jnp.float32) * 0.02, -0.06, 0.06)
        w2 = jnp.clip(jax.random.normal(k4, (TOTAL_WIDTH, N_EMBD), dtype=jnp.float32) * 0.02, -0.06, 0.06)
        return {'x': x, 'router_w': router_w, 'w1': w1, 'w2': w2}
    _L1_ffn_all = _L1_ffn_setup()
    _L1_ffn_in = {k: v for k, v in _L1_ffn_all.items() if k in ('router_w', 'w1', 'w2')}
    del _L1_ffn_all
    return {'x': x, 'cls_tok': cls_tok, 'L0_tok_w': _L0_tok_in['w'], 'L0_tok_b': _L0_tok_in['b'], 'L0_attn_Wq': _L0_attn_in['Wq'], 'L0_attn_Wk': _L0_attn_in['Wk'], 'L0_attn_Wv': _L0_attn_in['Wv'], 'L0_attn_Wo': _L0_attn_in['Wo'], 'L0_ffn_w_fc': _L0_ffn_in['w_fc'], 'L0_ffn_w_proj': _L0_ffn_in['w_proj'], 'L0_ffn_w_gate': _L0_ffn_in['w_gate'], 'L1_attn_w_qkv': _L1_attn_in['w_qkv'], 'L1_attn_b_qkv': _L1_attn_in['b_qkv'], 'L1_attn_w_proj': _L1_attn_in['w_proj'], 'L1_attn_b_proj': _L1_attn_in['b_proj'], 'L1_ffn_router_w': _L1_ffn_in['router_w'], 'L1_ffn_w1': _L1_ffn_in['w1'], 'L1_ffn_w2': _L1_ffn_in['w2']}

def reference(x, cls_tok, L0_tok_w, L0_tok_b, L0_attn_Wq, L0_attn_Wk, L0_attn_Wv, L0_attn_Wo, L0_ffn_w_fc, L0_ffn_w_proj, L0_ffn_w_gate, L1_attn_w_qkv, L1_attn_b_qkv, L1_attn_w_proj, L1_attn_b_proj, L1_ffn_router_w, L1_ffn_w1, L1_ffn_w2):
    import jax
    import jax.numpy as jnp

    def _L0_tok_ref(x, w, b):
        import jax, jax.numpy as jnp
        import numpy as np
        C, H, W = (1, 256, 256)
        P = 32
        D_TOK = 192
        B = 32
        D_PATCH = C * P * P

        def _patchify(x):
            Bx = x.shape[0]
            x = x.reshape(Bx, C, H // P, P, W // P, P)
            x = x.transpose(0, 2, 4, 1, 3, 5)
            return x.reshape(Bx, H // P * (W // P), D_PATCH)
        patches = _patchify(x)
        return jnp.einsum('bld,td->blt', patches, w) + b

    def _L0_attn_ref(x, Wq, Wk, Wv, Wo):
        import jax, jax.numpy as jnp
        import numpy as np
        B, S, D = (2, 1024, 192)
        q = jnp.einsum('bsd,ed->bse', x, Wq) * 0.1
        k = jnp.einsum('bsd,ed->bse', x, Wk) * 0.1
        v = jnp.einsum('bsd,ed->bse', x, Wv)
        attn = jnp.einsum('bqd,bkd->bqk', q, k) * 0.1
        attn = attn * attn + attn
        attn_out = jnp.einsum('bqk,bkd->bqd', attn, v)
        out = jnp.einsum('bsd,ed->bse', attn_out, Wo) * 0.1
        return out

    def _L0_ffn_ref(x, w_fc, w_proj, w_gate):
        import jax, jax.numpy as jnp
        import numpy as np
        B, T, C = (2, 256, 192)
        H, NE, K = (768, 8, 2)
        router_logits = jnp.einsum('btc,ce->bte', x, w_gate)
        router_probs = jax.nn.softmax(router_logits, axis=-1)
        top_p, top_i = jax.lax.top_k(router_probs, K)
        top_p = top_p / jnp.sum(top_p, axis=-1, keepdims=True)
        wf = w_fc.reshape(C, H, NE)
        h_all = jnp.einsum('btc,che->bthe', x, wf)
        h = jnp.take_along_axis(h_all, top_i[:, :, None, :], axis=-1)
        h = jax.nn.gelu(h, approximate=True)
        wp = w_proj.reshape(H, C, NE)
        o_all = jnp.einsum('bthk,hce->btcke', h, wp)
        o = jnp.take_along_axis(o_all, top_i[:, :, None, :, None], axis=-1)[..., 0]
        o = jnp.einsum('btck,btk->btc', o, top_p)
        return o

    def _L1_attn_ref(x, w_qkv, b_qkv, w_proj, b_proj):
        import jax, jax.numpy as jnp
        import numpy as np
        NUM_HEADS = 12
        ACT_BITS = 8
        W_BITS = 8
        EXP_COEF = (0.35815147, 0.96963238, 1.0)
        LN2 = 0.6931471805599453
        N_EXP = 30

        def ste_round(x):
            return x + jax.lax.stop_gradient(jnp.round(x) - x)

        def fq_act(x, bits=ACT_BITS):
            mn = jax.lax.stop_gradient(jnp.min(x))
            mx = jax.lax.stop_gradient(jnp.max(x))
            qmax = 2.0 ** bits - 1.0
            scale = jnp.maximum((mx - mn) / qmax, 1e-08)
            zero = jnp.round(-mn / scale)
            q = jnp.clip(ste_round(x / scale) + zero, 0.0, qmax)
            return ((q - zero) * scale, scale)

        def fq_weight(w, bits=W_BITS):
            amax = jax.lax.stop_gradient(jnp.max(jnp.abs(w), axis=1, keepdims=True))
            qmax = 2.0 ** (bits - 1) - 1.0
            scale = jnp.maximum(amax / qmax, 1e-08)
            q = jnp.clip(ste_round(w / scale), -qmax - 1.0, qmax)
            return q * scale

        def int_softmax(x, scale):
            a, b, c = EXP_COEF
            x_int = ste_round(x / scale)
            x_int = x_int - jnp.max(x_int, axis=-1, keepdims=True)
            x0_int = jnp.floor(-LN2 / scale)
            x_int = jnp.maximum(x_int, N_EXP * x0_int)
            qexp = jnp.floor(x_int / x0_int)
            r = x_int - x0_int * qexp
            b_int = jnp.floor(b / a / scale)
            c_int = jnp.floor(c / a / (scale * scale))
            p_int = r * (r + b_int) + c_int
            e = p_int * jnp.exp2(-qexp) * (a * scale * scale)
            return e / jnp.sum(e, axis=-1, keepdims=True)
        B, N, C = x.shape
        H = NUM_HEADS
        D = C // H
        attn_scale = D ** (-0.5)
        qkv = jnp.einsum('bnc,oc->bno', x, fq_weight(w_qkv)) + b_qkv
        qkv, _ = fq_act(qkv)
        q, _ = fq_act(qkv[:, :, :C])
        k, _ = fq_act(qkv[:, :, C:2 * C])
        v, _ = fq_act(qkv[:, :, 2 * C:])
        q = q.reshape(B, N, H, D).transpose(0, 2, 1, 3)
        k = k.reshape(B, N, H, D).transpose(0, 2, 1, 3)
        v = v.reshape(B, N, H, D).transpose(0, 2, 1, 3)
        attn = jnp.einsum('bhnd,bhmd->bhnm', q, k) * attn_scale
        attn, kv_scale = fq_act(attn)
        attn = int_softmax(attn, kv_scale)
        out = jnp.einsum('bhnm,bhmd->bhnd', attn, v)
        out = out.transpose(0, 2, 1, 3).reshape(B, N, C)
        out, _ = fq_act(out)
        out = jnp.einsum('bnc,oc->bno', out, fq_weight(w_proj)) + b_proj
        out, _ = fq_act(out)
        return out

    def _L1_ffn_ref(x, router_w, w1, w2):
        import jax, jax.numpy as jnp
        import numpy as np
        N_EMBD = 192
        EXPERT_SIZES = [(8, 128), (8, 256)]
        TOP_K = 8
        NORM_TOPK_PROB = True
        EXPERT_WIDTHS = []
        for cnt, w in EXPERT_SIZES:
            EXPERT_WIDTHS += [w] * cnt
        EXPERT_OFFSETS = np.concatenate([[0], np.cumsum(EXPERT_WIDTHS)]).astype(np.int64)
        NUM_EXPERTS = len(EXPERT_WIDTHS)
        TOTAL_WIDTH = int(EXPERT_OFFSETS[-1])
        B, S, D = x.shape
        xt = x.reshape(-1, D)
        T = xt.shape[0]
        logits = jnp.einsum('td,ed->te', xt, router_w)
        probs = jax.nn.softmax(logits, axis=-1)
        topk_w, topk_idx = jax.lax.top_k(probs, TOP_K)
        if NORM_TOPK_PROB:
            topk_w = topk_w / jnp.sum(topk_w, axis=-1, keepdims=True)
        comb = jnp.zeros((T, NUM_EXPERTS), dtype=xt.dtype)
        comb = comb.at[jnp.arange(T)[:, None], topk_idx].add(topk_w)
        out = jnp.zeros_like(xt)
        for e in range(NUM_EXPERTS):
            off = int(EXPERT_OFFSETS[e])
            wd = EXPERT_WIDTHS[e]
            h = jax.nn.gelu(xt @ w1[:, off:off + wd])
            out = out + comb[:, e:e + 1] * (h @ w2[off:off + wd, :])
        return out.reshape(B, S, D)
    h = _L0_tok_ref(x, L0_tok_w, L0_tok_b)
    h = jnp.concatenate([jnp.broadcast_to(cls_tok, (h.shape[0], 1, h.shape[2])), h], axis=1)
    h = h + _L0_attn_ref(_layernorm(h, axis=-1), L0_attn_Wq, L0_attn_Wk, L0_attn_Wv, L0_attn_Wo)
    h = h + _L0_ffn_ref(_layernorm(h, axis=-1), L0_ffn_w_fc, L0_ffn_w_proj, L0_ffn_w_gate)
    h = h + _L1_attn_ref(_layernorm(h, axis=-1), L1_attn_w_qkv, L1_attn_b_qkv, L1_attn_w_proj, L1_attn_b_proj)
    h = h + _L1_ffn_ref(_layernorm(h, axis=-1), L1_ffn_router_w, L1_ffn_w1, L1_ffn_w2)
    return h

_drawn_inputs = setup_inputs


def setup_inputs(seed=0):
    import zlib

    import numpy as np

    out = dict(_drawn_inputs(seed))
    spreads = {}
    factors = {'cls_tok': 8.0,
     'L0_attn_Wq': 8.0,
     'L0_attn_Wk': 8.0,
     'L0_attn_Wv': 8.0,
     'L0_attn_Wo': 8.0,
     'L0_ffn_w_fc': 2.765,
     'L0_ffn_w_proj': 2.701,
     'L0_ffn_w_gate': 3.117,
     'L1_attn_w_qkv': 3.241,
     'L1_attn_b_qkv': 6.027,
     'L1_attn_w_proj': 2.896,
     'L1_ffn_router_w': 3.134}
    for name, (base, spread) in spreads.items():
        noise = np.random.default_rng([zlib.crc32(name.encode()), seed]).standard_normal(out[name].shape)
        drawn = base * np.exp(spread * noise) if base else spread * noise
        out[name] = jnp.asarray(drawn.astype(out[name].dtype))
    for name, factor in factors.items():
        out[name] = (out[name] * factor).astype(out[name].dtype)
    return out
```

```python
from contextlib import ExitStack

import concourse.bass as bass
from concourse import mybir

F32 = mybir.dt.float32
BF16 = mybir.dt.bfloat16
I32 = mybir.dt.int32
ALU = mybir.AluOpType
ACT = mybir.ActivationFunctionType
X = mybir.AxisListType.X
XY = mybir.AxisListType.XY

B, D, PATCH = 8, 192, 64
S = PATCH + 1
KC, DC = 2, 96
NT = 5
HALF = 4 * S
NH, HD, HC = 12, 16, 6
TOKK = 8
EPS = 1e-5
MAGIC = 12582912.0
QMAX, SMIN = 255.0, 1e-8
LN2, EXP_A, EXP_B, EXP_C, N_EXP = 0.6931471805599453, 0.35815147, 0.96963238, 1.0, 30
E0, T0 = 8, 6
E1 = 16
ROWS = 50
GROUPS = 13
SLOT = 32


def build(nc, t):
    with ExitStack() as ctx:
        def sb(name, shape, dt=F32):
            return ctx.enter_context(nc.sbuf_tensor(name, shape, dt))

        def sem(name):
            return ctx.enter_context(nc.semaphore(name))

        PB = [ctx.enter_context(nc.psum_tensor(f"bank{i}", [128, 512], F32)) for i in range(8)]

        class Area:
            def __init__(self, name, words):
                self.raw, self.at, self.words = sb(name, [128, words]), 0, words

            def take(self, p, shape):
                n = 1
                for d in shape:
                    n *= d
                assert self.at + n <= self.words
                flat = self.raw[0:p, self.at:self.at + n]
                self.at += n
                names = "abcd"[:len(shape)]
                return flat.rearrange(f"p ({' '.join(names)}) -> p {' '.join(names)}", **dict(zip(names[1:], shape[1:])))

            def again(self):
                self.at = 0

        embed_area = Area("embed_area", TOKK * (B * PATCH + D))
        patches = embed_area.take(128, [TOKK, B * PATCH])
        w_tok = embed_area.take(128, [TOKK, D])
        tok_bias = sb("tok_bias", [128, D])
        layer0_area = Area("layer0_area", 4 * KC * D + 2 * KC * T0 * 128 + 2 * T0 * D)
        w_l0 = layer0_area.take(DC, [4, KC, D])
        w_gate0 = sb("w_gate0", [DC, KC, E0])
        w_gate1 = sb("w_gate1", [DC, KC, E1])
        ident = sb("ident", [128, 128])
        ident_bf = sb("ident_bf", [128, 128], BF16)
        head_mask = sb("head_mask", [DC, HC])
        cls_mask = sb("cls_mask", [DC, KC, SLOT])
        before = sb("before", [128, E0, E0])
        h = sb("h", [128, NT, D])
        xn = sb("xn", [128, NT, D])
        xt = sb("xt", [DC, KC, B * S])
        bn6 = sb("bn6", [128, NT, 6])
        mv = sb("mv", [128, NT, 2])
        var_eps = sb("var_eps", [128, NT])
        std = sb("std", [128, NT])
        rstd = sb("rstd", [128, NT])
        newton = sb("newton", [128, NT])
        eps_c = sb("eps_c", [128, 1])
        attn0_area = Area("attn0_area", 3 * KC * B * S + B * D + 2 * B * S)
        q0, k0, o0 = (attn0_area.take(DC, [KC, B, S]) for _ in range(3))
        v0 = attn0_area.take(S, [B, D])
        s0, a0 = (attn0_area.take(S, [B, S]) for _ in range(2))
        logits = sb("logits", [128, NT, E1])
        probs = sb("probs", [128, NT, E1])
        rmax = sb("rmax", [128, NT])
        rsum = sb("rsum", [128, NT])
        rinv = sb("rinv", [128, NT])
        cmp_a = sb("cmp_a", [128, E0, E0])
        cmp_b = sb("cmp_b", [128, E0, E0])
        rank = sb("rank", [128, NT, E0])
        top8 = sb("top8", [128, NT, 8])
        left = sb("left", [128, NT, E1])
        chosen = sb("chosen", [128, NT, E1])
        comb0 = sb("comb0", [128, NT, E0])
        comb1 = sb("comb1", [128, NT, E1])
        fc0 = layer0_area.take(DC, [2, KC, T0 * 128])
        pj0 = layer0_area.take(128, [2, T0, D])
        fc1 = sb("fc1", [DC, 2, KC, 512])
        pj1 = sb("pj1", [128, 2, 4, D])
        o0_cls = sb("o0_cls", [DC, KC, B])
        hid = sb("hid", [128, 2, 2 * HALF])
        wq_raw = sb("wq_raw", [DC, 8, D])
        wq_amax = sb("wq_amax", [DC, 8])
        wq_scale = sb("wq_scale", [DC, 8])
        wq_inv = sb("wq_inv", [DC, 8])
        wq_int = sb("wq_int", [DC, 8, D])
        w_qkv_t = sb("w_qkv_t", [DC, KC, 6 * DC])
        w_proj_t = sb("w_proj_t", [DC, KC, D], BF16)
        b_qkv = sb("b_qkv", [DC, 6])
        b_proj = sb("b_proj", [128, D])
        proj_scale = sb("proj_scale", [128, D])
        qkv = sb("qkv", [DC, 6, B, S])
        qkv_int = sb("qkv_int", [DC, 6, B, S], BF16)
        k_heads = sb("k_heads", [DC, KC, B, HC, S], BF16)
        q_cls = sb("q_cls", [DC, KC, B, SLOT], BF16)
        v1 = sb("v1", [S, B, NH, HD + 1])
        sc = sb("sc", [128, ROWS, S])
        v1_flat = sb("v1_flat", [S, B, D])
        for area in (embed_area, layer0_area, attn0_area):
            area.again()
        qexp = sb("qexp", [128, ROWS, S])
        rem = embed_area.take(128, [ROWS, S])
        pow2 = attn0_area.take(128, [ROWS, S])
        row_hi = sb("row_hi", [128, ROWS])
        row_lo = sb("row_lo", [128, ROWS])
        cls_sum = sb("cls_sum", [128, 2])
        e_t = layer0_area.take(S, [4 * GROUPS, 128])
        o_inv = sb("o_inv", [128, 4, NH])
        o1 = sb("o1", [128, 4, NH, HD])
        o1_int = sb("o1_int", [128, 4, NH * HD], BF16)
        o_cls_m = sb("o_cls_m", [DC, B * KC, NH])
        o_cls = sb("o_cls", [DC, B * KC])
        o1_t = sb("o1_t", [DC, KC, B * S], BF16)
        y1 = sb("y1", [128, NT, D])
        stat_q = sb("stat_q", [DC, 2, 6])
        stat_s = sb("stat_s", [128, 2])
        stat_o = sb("stat_o", [128, 4])
        stat_y = sb("stat_y", [128, 4])
        red = sb("red", [12, 4])
        g_q = sb("g_q", [128, 12])
        g_s = sb("g_s", [128, 2])
        g_o = sb("g_o", [128, 4])
        g_y = sb("g_y", [128, 4])
        ext = sb("ext", [128, 6])
        ext_t = sb("ext_t", [128, 6])
        ext_c = sb("ext_c", [128, 6])
        ext_q = sb("ext_q", [128, 6])
        c = sb("consts", [128, 64])
        columns = {}

        def col(name, n=1):
            if name not in columns:
                columns[name] = (sum(w for _, w in columns.values()), n)
                assert sum(w for _, w in columns.values()) <= 64
            at, w = columns[name]
            return c[:, at:at + w]

        def colp(name, p, i=0):
            at, _ = columns[name]
            return c[0:p, at + i:at + i + 1]

        tok_in = [sem(f"tok_in{k}") for k in range(TOKK)]
        bias_in = sem("bias_in")
        w_l0_in = sem("w_l0_in")
        consts_in = sem("consts_in")
        gates_in = sem("gates_in")
        wq_in = sem("wq_in")
        bq_in = sem("bq_in")
        fc0_in = [sem(f"fc0_in{s}") for s in range(2)]
        pj0_in = [sem(f"pj0_in{s}") for s in range(2)]
        fc1_in = [sem(f"fc1_in{s}") for s in range(2)]
        pj1_in = [sem(f"pj1_in{s}") for s in range(2)]
        dve_done = sem("dve_done")
        act_done = sem("act_done")
        tok_mm = sem("tok_mm")
        ident_ready = sem("ident_ready")
        mv_ready = sem("mv_ready")
        eps_ready = sem("eps_ready")
        std_ready = sem("std_ready")
        xn_ready = sem("xn_ready")
        xt_mm = sem("xt_mm")
        xt_act = sem("xt_act")
        xt_dve = sem("xt_dve")
        q0_mm = sem("q0_mm")
        k0_mm = sem("k0_mm")
        q0_ready = sem("q0_ready")
        k0_ready = sem("k0_ready")
        v0_mm = sem("v0_mm")
        v0_ready = sem("v0_ready")
        s0_mm = sem("s0_mm")
        s0_ready = sem("s0_ready")
        a0_ready = sem("a0_ready")
        o0_mm = sem("o0_mm")
        o0_ready = sem("o0_ready")
        y0_mm = sem("y0_mm")
        gate_mm = sem("gate_mm")
        soft_in = sem("soft_in")
        soft_exp = sem("soft_exp")
        fc_mm = [sem(f"fc_mm{n}") for n in range(3)]
        gelu_done = [sem(f"gelu_done{n}") for n in range(3)]
        pj_mm = [sem(f"pj_mm{n}") for n in range(3)]
        acc_done = [sem(f"acc_done{n}") for n in range(3)]
        wint_ready = sem("wint_ready")
        wint_t_mm = sem("wint_t_mm")
        wint_t_ready = sem("wint_t_ready")
        pscale_mm = sem("pscale_mm")
        qkv_mm = sem("qkv_mm")
        qkv_ready = sem("qkv_ready")
        stat_ready = sem("stat_ready")
        stat_t = sem("stat_t")
        red_ready = sem("red_ready")
        stat_b = sem("stat_b")
        v_int_ready = sem("v_int_ready")
        qk_ready = sem("qk_ready")
        v1_mm = sem("v1_mm")
        v1_ready = sem("v1_ready")
        sc_mm = sem("sc_mm")
        sc_ready = sem("sc_ready")
        x_ready = sem("x_ready")
        y_ready = sem("y_ready")
        qexp_ready = sem("qexp_ready")
        pow2_ready = sem("pow2_ready")
        rem_ready = sem("rem_ready")
        sq_ready = sem("sq_ready")
        e_ready = sem("e_ready")
        et_mm = sem("et_mm")
        et_act = sem("et_act")
        et_dve = sem("et_dve")
        pv_mm = sem("pv_mm")
        pvc_mm = sem("pvc_mm")
        o1_ready = sem("o1_ready")
        o1t_mm = sem("o1t_mm")
        o1t_ready = sem("o1t_ready")
        ocls_ready = sem("ocls_ready")
        y1_mm = sem("y1_mm")
        h_ready = sem("h_ready")
        out_done = sem("out_done")

        def tile_tokens(fm, kc, i):
            return fm[:, kc, i * 128:i * 128 + rows(i)]

        def pairs(cols):
            return cols.rearrange("p (i q) -> p i q", q=2 * S)

        def cls_cols(cols):
            return pairs(cols)[:, :, 0:2 * S:2 * S - 1]

        def patch_at(b):
            return 1 if b % 2 == 0 else 0

        def half(fm, kc, n):
            return fm[:, kc, 4 * n:4 * n + 4, :]

        def xt_half(kc, n):
            return xt[:, kc, n * HALF:(n + 1) * HALF]

        def xt_patches(r, j, i):
            if r % 2 == 0:
                return pairs(xt[:, j, :])[:, i:i + 2, 1:129]
            return xt[:, j, i * 128:(i + 2) * 128].rearrange("p (i q) -> p i q", i=2)

        def rows(i):
            return 128 if i < 4 else B

        CHUNKS = [(0, 26), (26, 50)]
        RUNS = [(2 * T0, T0, E0 // 2, 0), (8, 1, 1, 0), (8, 2, 2, 8)]
        LATER = [3, 4, 5]
        FCB = [(0, 1), (6, 7)]

        block = ctx.enter_context(nc.Block())

        @block.sync
        def _(sp):
            for k in range(TOKK):
                sp.dma_start(patches[:, k, :], t["patches"][k]).then_inc(tok_in[k], 16)
                sp.dma_start(w_tok[:, k, :], t["w_tok"][k]).then_inc(tok_in[k], 16)
            sp.dma_start(w_l0[:], t["w_l0"]).then_inc(w_l0_in, 16)
            for s in range(2):
                sp.dma_start(fc0[:, s], t["fc0"][s]).then_inc(fc0_in[s], 16)
                sp.dma_start(pj0[:, s], t["pj0"][s]).then_inc(pj0_in[s], 16)
            for s in range(2):
                sp.dma_start(fc1[:, s], t["fc1"][s]).then_inc(fc1_in[s], 16)
                sp.dma_start(pj1[:, s], t["pj1"][s]).then_inc(pj1_in[s], 16)
            with sp.Fori(1, E0 // 2) as it:
                for s in range(2):
                    sp.wait_ge(pj_mm[0], it * (2 * T0) + (s - 1) * T0)
                    sp.dma_start(fc0[:, s], t["fc0"][bass.ds(it * 2 + s, 1)].squeeze(0)).then_inc(fc0_in[s], 16)
                    sp.dma_start(pj0[:, s], t["pj0"][bass.ds(it * 2 + s, 1)].squeeze(0)).then_inc(pj0_in[s], 16)
            for s in range(2):
                sp.wait_ge(pj_mm[1], 4 * (s + 1))
                sp.dma_start(fc1[:, s], t["fc1"][2 + s]).then_inc(fc1_in[s], 16)
                sp.dma_start(pj1[:, s], t["pj1"][2 + s]).then_inc(pj1_in[s], 16)
            for s in range(2):
                sp.wait_ge(pj_mm[2], 4 * (s + 1))
                sp.dma_start(fc1[:, s], t["fc1"][4 + s]).then_inc(fc1_in[s], 16)
                sp.dma_start(pj1[:, s], t["pj1"][4 + s]).then_inc(pj1_in[s], 16)
            sp.wait_ge(acc_done[2], NT * 8)
            for b in range(B):
                lo = (b % 2) * PATCH
                sp.dma_start(t["out"][b, 1:S, :], h[lo:lo + PATCH, b // 2, :]).then_inc(out_done, 16)
            sp.dma_start(t["out"][:, 0, :], h[0:B, 4, :]).then_inc(out_done, 16)
            sp.wait_ge(out_done, 16 * (B + 1))

        @block.gpsimd
        def _(pool):
            pool.dma_start(ident[:], t["ident"]).then_inc(consts_in, 16)
            pool.dma_start(head_mask[:], t["head_mask"]).then_inc(consts_in, 16)
            pool.dma_start(cls_mask[:], t["cls_mask"]).then_inc(consts_in, 16)
            pool.dma_start(before[:], t["before"]).then_inc(consts_in, 16)
            pool.dma_start(tok_bias[:], t["tok_bias"].partition_broadcast(128)).then_inc(bias_in, 16)
            pool.dma_start(h[0:B, 4, :], t["cls_tok"].partition_broadcast(B)).then_inc(bias_in, 16)
            pool.dma_start(w_gate0[:], t["w_gate0"]).then_inc(gates_in, 16)
            pool.dma_start(w_gate1[:], t["w_gate1"]).then_inc(gates_in, 16)
            pool.dma_start(wq_raw[:, 0:6, :], t["w_qkv"]).then_inc(wq_in, 16)
            pool.dma_start(wq_raw[:, 6:8, :], t["w_proj"]).then_inc(wq_in, 16)
            pool.dma_start(b_qkv[:], t["b_qkv"]).then_inc(bq_in, 16)
            pool.dma_start(b_proj[:], t["b_proj"].partition_broadcast(128)).then_inc(bq_in, 16)

        @block.tensor
        def _(pe):
            def wait_xt(r):
                pe.wait_ge(xt_act, 4 * (r + 1))
                pe.wait_ge(xt_dve, 2 * (r + 1))

            def transpose_x(r):
                for i in range(NT):
                    pe.wait_ge(xn_ready, NT * r + i + 1)
                    n = rows(i)
                    for j in range(KC):
                        at = (i % 2) * 256 + j * 128 if i < 4 else j * B
                        last = pe.transpose(PB[i // 2][0:DC, at:at + n], xn[0:n, i, j * DC:(j + 1) * DC],
                                            ident[0:n, 0:n])
                    last.then_inc(xt_mm, 1)

            def mm_kc(out, lhs, rhs, n=KC):
                for kc in range(n):
                    last = pe.matmul(out, lhs(kc), rhs(kc), start=(kc == 0), stop=(kc == n - 1))
                return last

            def gate(r, w, n):
                wait_xt(r)
                pe.wait_ge(gates_in, 32)
                for i in range(NT):
                    last = mm_kc(PB[3][0:rows(i), i * n:(i + 1) * n],
                                 lambda kc: tile_tokens(xt, kc, i), lambda kc: w[:, kc, :])
                last.then_inc(gate_mm, 1)

            def ffn(run, fc, pj, fc_in, pj_in, loaded):
                tiles, per, iters, _ = RUNS[run]
                uw = tiles // 2

                def hidden(it, g):
                    s, j = g // uw, g % uw
                    if j == 0:
                        pe.wait_ge(fc_in[s], it * 16 + 16 * loaded)
                    for n in range(2):
                        if g >= 2:
                            pe.wait_ge(gelu_done[run], it * (2 * tiles) + 2 * g - 3 + n)
                        mm_kc(PB[FCB[g % 2][n]][:, 0:HALF], lambda kc: fc[:, s, kc, j * 128:(j + 1) * 128],
                              lambda kc: xt_half(kc, n)).then_inc(fc_mm[run], 1)

                def project(it, g):
                    s, j = g // uw, g % uw
                    first, last = g % per == 0, g % per == per - 1
                    pe.wait_ge(gelu_done[run], it * (2 * tiles) + 2 * g + 2)
                    if j == 0:
                        pe.wait_ge(pj_in[s], it * 16 + 16 * loaded)
                    if first and g:
                        pe.wait_ge(acc_done[run], it * (NT * tiles // per) + NT * (g // per))
                    for i in range(NT):
                        mm = pe.matmul(PB[LATER[i // 2]][0:rows(i), (i % 2) * D:(i % 2 + 1) * D],
                                       hid[:, g % 2, i * 128:i * 128 + rows(i)], pj[:, s, j, :],
                                       start=first and i % 2 == 0, stop=last, skip_group_check=True)
                    mm.then_inc(pj_mm[run], 1)

                def iteration(it):
                    hidden(it, 0)
                    for g in range(1, tiles):
                        hidden(it, g)
                        project(it, g - 1)
                    project(it, tiles - 1)

                return iteration

            def run_ffn(run, *a):
                tiles, per, iters, _ = RUNS[run]
                body = ffn(run, *a)
                if iters == 1:
                    body(0)
                    return
                with pe.Fori(0, iters) as it:
                    pe.wait_ge(acc_done[run], it * (NT * tiles // per))
                    body(it)

            def statistics(r, stat, n, p, out_cols):
                pe.wait_ge(stat_ready, r + 1)
                pe.transpose(PB[6][0:n, 0:p], stat, ident[0:p, 0:p]).then_inc(stat_t, 1)
                pe.wait_ge(red_ready, r + 1)
                pe.matmul(PB[7][:, 0:n], red[0:n, r:r + 1].broadcast_to([n, 128]), ident[0:n, 0:n],
                          start=True, stop=True).then_inc(stat_b, 1)

            for k in range(TOKK):
                pe.wait_ge(tok_in[k], 32)
                for i in range(4):
                    mm = pe.matmul(PB[i][:, 0:D], patches[:, k, i * 128:(i + 1) * 128], w_tok[:, k, :],
                                   start=(k == 0), stop=(k == TOKK - 1))
                    if k == TOKK - 1:
                        mm.then_inc(tok_mm, 1)
            pe.wait_ge(consts_in, 64)
            transpose_x(0)
            wait_xt(0)
            pe.wait_ge(w_l0_in, 16)
            for w, done in ((0, q0_mm), (1, k0_mm)):
                for j in range(KC):
                    for n in range(2):
                        mm_kc(PB[4 * w + 2 * j + n][0:DC, 0:HALF], lambda kc: w_l0[:, w, kc, j * DC:(j + 1) * DC],
                              lambda kc: xt_half(kc, n)).then_inc(done, 1)
            for b in range(B):
                if b % 2 == 0:
                    pe.wait_ge(q0_ready, b // 2 + 1)
                last = mm_kc(PB[b // 2][0:S, (b % 2) * D:(b % 2 + 1) * D], lambda kc: xt[:, kc, b * S:(b + 1) * S],
                             lambda kc: w_l0[:, 2, kc, :])
                if b % 2:
                    last.then_inc(v0_mm, 1)
            pe.wait_ge(q0_ready, 4)
            pe.wait_ge(k0_ready, 4)
            for b in range(B):
                last = mm_kc(PB[4 + b // 4][0:S, (b % 4) * S:(b % 4 + 1) * S], lambda kc: k0[:, kc, b, :],
                             lambda kc: q0[:, kc, b, :])
                if b % 4 == 3:
                    last.then_inc(s0_mm, 1)
            pe.wait_ge(v0_ready, 4)
            for n in range(2):
                pe.wait_ge(a0_ready, n + 1)
                for j in range(KC):
                    bank = PB[(6, 0)[n] + j]
                    for b in range(4 * n, 4 * n + 4):
                        last = pe.matmul(bank[0:DC, (b % 4) * S:(b % 4 + 1) * S], v0[:, b, j * DC:(j + 1) * DC],
                                         a0[:, b, :], start=True, stop=True)
                    last.then_inc(o0_mm, 1)
            pe.wait_ge(o0_ready, 5)
            o0_cols = o0.rearrange("p j b s -> p j (b s)")
            for i in range(NT):
                lhs = o0_cols[:, :, 2 * S * i + 1:2 * S * i + 129] if i < 4 else o0_cls
                last = mm_kc(PB[2 + i // 2][0:rows(i), (i % 2) * D:(i % 2 + 1) * D],
                             lambda kc: lhs[:, kc, :], lambda kc: w_l0[:, 3, kc, :])
                if i % 2 or i == 4:
                    last.then_inc(y0_mm, 1)
            transpose_x(1)
            gate(1, w_gate0, E0)
            pe.wait_ge(wint_ready, 1)
            for half_rows in range(2):
                for kc in range(KC):
                    for j in range(4):
                        last = pe.transpose(PB[4 + 2 * half_rows + kc][0:DC, j * DC:(j + 1) * DC],
                                            wq_int[:, 4 * half_rows + j, kc * DC:(kc + 1) * DC], ident[0:DC, 0:DC])
                    last.then_inc(wint_t_mm, 1)
            for j in range(KC):
                last = pe.matmul(PB[2][:, j * DC:(j + 1) * DC], wq_scale[:, 6 + j:7 + j].broadcast_to([DC, 128]),
                                 ident[0:DC, 0:DC], start=True, stop=True)
            last.then_inc(pscale_mm, 1)
            pe.wait_ge(wint_t_ready, 5)
            pe.wait_ge(soft_in, 1)
            run_ffn(0, fc0, pj0, fc0_in, pj0_in, 1)
            transpose_x(2)
            wait_xt(2)
            for j in range(6):
                for n in range(2):
                    g = 2 * j + n
                    if g >= 8:
                        pe.wait_ge(qkv_ready, g - 7)
                    mm_kc(PB[g % 8][0:DC, 0:HALF], lambda kc: w_qkv_t[:, kc, j * DC:(j + 1) * DC],
                          lambda kc: xt_half(kc, n)).then_inc(qkv_mm, 1)
            statistics(0, stat_q[:].rearrange("p a j -> p (a j)"), 12, DC, 12)
            pe.wait_ge(v_int_ready, 1)
            pe.wait_ge(ident_ready, 1)
            for b in range(B):
                for kc in range(KC):
                    out = PB[b // 4][:, :].bitcast(BF16)[0:S, (b % 4) * D + kc * DC:(b % 4) * D + (kc + 1) * DC]
                    last = pe.transpose(out, qkv_int[:, 4 + kc, b, :], ident_bf[0:DC, 0:DC])
                if b % 4 == 3:
                    last.then_inc(v1_mm, 1)
            pe.wait_ge(qk_ready, 1)
            for i in range(4):
                for kc in range(KC):
                    g = 2 * i + kc
                    if g >= 6:
                        pe.wait_ge(sc_ready, g - 5)
                    bank = PB[2 + g % 6]
                    for b in (2 * i, 2 * i + 1):
                        lo = (b % 2) * PATCH
                        last = pe.matmul(bank[lo:lo + PATCH, 0:HC * S], qkv_int[:, kc, b, patch_at(b):patch_at(b) + PATCH],
                                         k_heads[:, kc, b, :, :], start=True, stop=True)
                    last.then_inc(sc_mm, 1)
            pe.wait_ge(sc_ready, 3)
            for b in range(B):
                lo = SLOT * (b % 4)
                last = mm_kc(PB[4][lo:lo + SLOT, (b // 4) * S:(b // 4 + 1) * S], lambda kc: q_cls[:, kc, b, :],
                             lambda kc: qkv_int[:, 2 + kc, b, :])
            last.then_inc(sc_mm, 1)
            pe.wait_ge(sc_ready, 9)
            statistics(1, stat_s[:], 2, 128, 2)
            for g in range(GROUPS):
                n = min(4, ROWS - 4 * g)
                pe.wait_ge(e_ready, 1 if 4 * g + n <= CHUNKS[0][1] else 2)
                if g >= 6:
                    pe.wait_ge(et_dve if g % 2 else et_act, (g - 6) // 2 + 1)
                for r in range(4 * g, 4 * g + n):
                    last = pe.transpose(PB[g % 6][0:S, (r % 4) * 128:(r % 4 + 1) * 128], sc[:, r, :], ident[:])
                last.then_inc(et_mm, 1)
            pe.wait_ge(v1_ready, 4)
            for i in range(4):
                for head in range(NH):
                    r = i * NH + head
                    pe.wait_ge(et_dve if (r // 4) % 2 else et_act, (r // 4) // 2 + 1)
                    for b in (2 * i, 2 * i + 1):
                        lo = (b % 2) * PATCH
                        at = (i % 2) * NH * (HD + 1) + head * (HD + 1)
                        last = pe.matmul(PB[6 + i // 2][lo:lo + PATCH, at:at + HD + 1], e_t[:, r, lo:lo + PATCH],
                                         v1[:, b, head, :], start=True, stop=True)
                if i % 2:
                    last.then_inc(pv_mm, 1)
            pe.wait_ge(et_act, 7)
            for b in range(B):
                for kc in range(KC):
                    at = (2 * b + kc) * NH
                    last = pe.matmul(PB[0][0:DC, at:at + NH], v1_flat[:, b, kc * DC:(kc + 1) * DC],
                                     e_t[:, 48 + b // 4, SLOT * (b % 4):SLOT * (b % 4) + NH], start=True, stop=True)
            last.then_inc(pvc_mm, 1)
            statistics(2, stat_o[:], 4, 128, 4)
            pe.wait_ge(o1_ready, 1)
            for i in range(4):
                for kc in range(KC):
                    at = (i % 2) * 256 + kc * 128
                    last = pe.transpose(PB[1 + i // 2][:, :].bitcast(BF16)[0:DC, at:at + 128],
                                        o1_int[:, i, kc * DC:(kc + 1) * DC], ident_bf[:])
                if i % 2:
                    last.then_inc(o1t_mm, 1)
            pe.wait_ge(o1t_ready, 2)
            pe.wait_ge(ocls_ready, 1)
            for i in range(NT):
                last = mm_kc(PB[3 + i // 2][0:rows(i), (i % 2) * D:(i % 2 + 1) * D],
                             lambda kc: tile_tokens(o1_t, kc, i), lambda kc: w_proj_t[:, kc, :])
                if i % 2 or i == 4:
                    last.then_inc(y1_mm, 1)
            statistics(3, stat_y[:], 4, 128, 4)
            transpose_x(3)
            gate(3, w_gate1, E1)
            pe.wait_ge(soft_in, 2)
            run_ffn(1, fc1, pj1, fc1_in, pj1_in, 1)
            pe.wait_ge(acc_done[1], NT * 8)
            run_ffn(2, fc1, pj1, fc1_in, pj1_in, 2)

        @block.scalar
        def _(act):
            def layernorm(r):
                act.wait_ge(mv_ready, r + 1)
                if r == 0:
                    act.wait_ge(eps_ready, 1)
                act.activation(std[:], mv[:, :, 1], ACT.Sqrt, bias=eps_c[:]).then_inc(std_ready, 1)
                act.wait_ge(xt_mm, NT * r + 2)
                for j in range(KC):
                    src = PB[0][0:DC, :].rearrange("p (i j q) -> p i j q", i=2, j=2)[:, :, j]
                    act.activation(xt_patches(r, j, 0), src, ACT.Copy).then_inc(xt_act, 1)
                act.wait_ge(xt_mm, NT * r + 5)
                for j in range(KC):
                    to = xt[:, j, 512:520].rearrange("p (i b) -> p i b", b=2) if r % 2 else cls_cols(xt[:, j, :])
                    act.activation(to, PB[2][0:DC, j * B:(j + 1) * B].rearrange("p (i b) -> p i b", b=2),
                                   ACT.Copy).then_inc(xt_act, 1)

            def softmax_exp(r, n):
                act.wait_ge(soft_in, r + 1)
                act.activation(probs[:, :, 0:n], logits[:, :, 0:n], ACT.Exp).then_inc(soft_exp, 1)

            def ffn(run):
                tiles, per, iters, _ = RUNS[run]

                def body(it):
                    for g in range(tiles):
                        if g >= 2:
                            act.wait_ge(pj_mm[run], it * tiles + g - 1)
                        for n in range(2):
                            act.wait_ge(fc_mm[run], it * (2 * tiles) + 2 * g + n + 1)
                            act.activation(hid[:, g % 2, n * HALF:(n + 1) * HALF], PB[FCB[g % 2][n]][:, 0:HALF],
                                           ACT.Gelu_apprx_tanh).then_inc(gelu_done[run], 1)

                if iters == 1:
                    body(0)
                else:
                    with act.Fori(0, iters) as it:
                        body(it)

            layernorm(0)
            for j in range(KC):
                for n in range(2):
                    act.wait_ge(q0_mm, 2 * j + n + 1)
                    act.activation(half(q0, j, n), PB[2 * j + n][0:DC, 0:HALF].rearrange("p (b s) -> p b s", s=S),
                                   ACT.Copy, scale=0.1).then_inc(q0_ready, 1)
            for g in range(4):
                act.wait_ge(v0_mm, g + 1)
                act.activation(v0[:, 2 * g:2 * g + 2, :], PB[g][0:S, 0:2 * D].rearrange("p (b d) -> p b d", d=D),
                               ACT.Copy).then_inc(v0_ready, 1)
            for n in range(2):
                act.wait_ge(s0_mm, n + 1)
                act.activation(s0[:, 4 * n:4 * n + 4, :], PB[4 + n][0:S, 0:HALF].rearrange("p (b s) -> p b s", s=S),
                               ACT.Copy, scale=0.1).then_inc(s0_ready, 1)
            for n in range(2):
                for j in range(KC):
                    act.wait_ge(o0_mm, 2 * n + j + 1)
                    act.activation(half(o0, j, n), PB[(6, 0)[n] + j][0:DC, 0:HALF].rearrange("p (b s) -> p b s", s=S),
                                   ACT.Copy).then_inc(o0_ready, 1)
            act.wait_ge(o0_ready, 4)
            for j in range(KC):
                last = act.activation(o0_cls[:, j, :].rearrange("p (i b) -> p i b", b=2),
                                      cls_cols(o0[:, j].rearrange("p b s -> p (b s)")), ACT.Copy)
                if j == 0:
                    last.then_inc(act_done, 1)
            act.wait_ge(act_done, 1)
            last.then_inc(o0_ready, 1)
            layernorm(1)
            softmax_exp(0, E0)
            for hr in range(2):
                for kc in range(KC):
                    act.wait_ge(wint_t_mm, 2 * hr + kc + 1)
                    n = 4 * DC if hr == 0 else 2 * DC
                    act.activation(w_qkv_t[:, kc, hr * 4 * DC:hr * 4 * DC + n], PB[4 + 2 * hr + kc][0:DC, 0:n],
                                   ACT.Copy).then_inc(act_done, 1)
                    if hr == 1:
                        act.activation(w_proj_t[:, kc, :], PB[6 + kc][0:DC, 2 * DC:4 * DC],
                                       ACT.Copy).then_inc(wint_t_ready, 1)
            act.wait_ge(act_done, 5)
            act.wait_ge(pscale_mm, 1)
            act.activation(proj_scale[:], PB[2][:, 0:D], ACT.Copy).then_inc(wint_t_ready, 3)
            ffn(0)
            layernorm(2)
            act.wait_ge(bq_in, 32)
            for j in range(6):
                for n in range(2):
                    g = 2 * j + n
                    act.wait_ge(qkv_mm, g + 1)
                    act.activation(half(qkv, j, n), PB[g % 8][0:DC, 0:HALF].rearrange("p (b s) -> p b s", s=S),
                                   ACT.Identity, scale=wq_scale[:, j:j + 1], bias=b_qkv[:, j:j + 1]).then_inc(qkv_ready, 1)
            for n in range(2):
                act.wait_ge(v1_mm, n + 1)
                src = PB[n][:, :].bitcast(BF16)[0:S, 0:4 * D].rearrange("p (b h d) -> p b h d", b=4, h=NH)
                act.activation(v1[:, 4 * n:4 * n + 4, :, 0:HD], src, ACT.Copy).then_inc(v1_ready, 1)
                act.activation(v1_flat[:, 4 * n:4 * n + 4, :].rearrange("p b (h d) -> p b h d", h=NH), src,
                               ACT.Copy).then_inc(v1_ready, 1)
            for g in range(8):
                act.wait_ge(sc_mm, g + 1)
                act.activation(sc[:, HC * g:HC * (g + 1), :], PB[2 + g % 6][:, 0:HC * S].rearrange("p (h s) -> p h s", s=S),
                               ACT.Copy).then_inc(sc_ready, 1)
            act.wait_ge(sc_mm, 9)
            act.activation(sc[:, 48:50, :], PB[4][:, 0:2 * S].rearrange("p (h s) -> p h s", s=S),
                           ACT.Copy).then_inc(sc_ready, 1)
            for n, (a, z) in enumerate(CHUNKS):
                act.wait_ge(x_ready, n + 1)
                act.activation(qexp[:, a:z, :], sc[:, a:z, :], ACT.Identity, scale=col("inv_x0"),
                               bias=col("floor_shift")).then_inc(y_ready, 1)
            for n, (a, z) in enumerate(CHUNKS):
                act.wait_ge(qexp_ready, n + 1)
                act.activation(pow2[:, a:z, :], qexp[:, a:z, :], ACT.Exp, scale=-LN2).then_inc(pow2_ready, 1)
                act.wait_ge(rem_ready, n + 1)
                act.activation(sc[:, a:z, :], rem[:, a:z, :], ACT.Square, bias=col("neg_half_b")).then_inc(sq_ready, 1)
            for g in range(0, GROUPS, 2):
                n = min(4, ROWS - 4 * g)
                act.wait_ge(et_mm, g + 1)
                act.activation(e_t[:, 4 * g:4 * g + n, :], PB[g % 6][0:S, 0:n * 128].rearrange("p (r q) -> p r q", q=128),
                               ACT.Copy).then_inc(et_act, 1)
            for g in range(2):
                act.wait_ge(o1t_mm, g + 1)
                src = PB[1 + g][:, :].bitcast(BF16)[0:DC, 0:512].rearrange("p (i j q) -> p i j q", i=2, j=2)
                for kc in range(KC):
                    last = act.activation(o1_t[:, kc, 256 * g:256 * (g + 1)].rearrange("p (i q) -> p i q", i=2),
                                          src[:, :, kc], ACT.Copy)
                    if kc == 0:
                        last.then_inc(act_done, 1)
                act.wait_ge(act_done, 6 + g)
                last.then_inc(o1t_ready, 1)
            layernorm(3)
            softmax_exp(1, E1)
            ffn(1)
            ffn(2)

        @block.vector
        def _(dve):
            steps = [0]

            def then(ins):
                steps[0] += 1
                ins.then_inc(dve_done, 1)
                dve.wait_ge(dve_done, steps[0])

            def settle(ins):
                steps[0] += 1
                ins.then_inc(dve_done, 1)

            def layernorm(r):
                for i in range(NT):
                    settle(dve.bn_stats(bn6[0:rows(i), i, :], h[0:rows(i), i, :]))
                dve.wait_ge(dve_done, steps[0])
                for i in range(NT):
                    last = dve.bn_aggr(mv[0:rows(i), i, :], bn6[0:rows(i), i, :])
                    if i < NT - 1:
                        settle(last)
                dve.wait_ge(dve_done, steps[0])
                last.then_inc(mv_ready, 1)
                dve.wait_ge(mv_ready, r + 1)
                then(dve.tensor_scalar(var_eps[:], mv[:, :, 1], EPS, None, ALU.add))
                dve.wait_ge(std_ready, r + 1)
                then(dve.reciprocal(rstd[:], std[:]))
                then(dve.tensor_tensor(newton[:], rstd[:], rstd[:], ALU.mult))
                then(dve.tensor_tensor(newton[:], newton[:], var_eps[:], ALU.mult))
                then(dve.tensor_scalar(newton[:], newton[:], -0.5, 1.5, ALU.mult, ALU.add))
                then(dve.tensor_tensor(rstd[:], rstd[:], newton[:], ALU.mult))
                for i in range(NT):
                    n = rows(i)
                    dve.tensor_scalar(xn[0:n, i, :], h[0:n, i, :], mv[0:n, i, 0:1], rstd[0:n, i:i + 1],
                                      ALU.subtract, ALU.mult).then_inc(xn_ready, 1)
                dve.wait_ge(xt_mm, NT * r + 4)
                for j in range(KC):
                    src = PB[1][0:DC, :].rearrange("p (i j q) -> p i j q", i=2, j=2)[:, :, j]
                    dve.tensor_copy(xt_patches(r, j, 2), src).then_inc(xt_dve, 1)

            def softmax(r, n):
                dve.wait_ge(gate_mm, r + 1)
                settle(dve.tensor_copy(logits[:, 0:4, 0:n], PB[3][:, 0:4 * n].rearrange("p (i e) -> p i e", e=n)))
                then(dve.tensor_copy(logits[0:B, 4, 0:n], PB[3][0:B, 4 * n:5 * n]))
                lg, pr = logits[:, :, 0:n], probs[:, :, 0:n]
                then(dve.tensor_reduce(rmax[:], lg, X, ALU.max))
                dve.tensor_tensor(lg, lg, rmax[:].unsqueeze(2).broadcast_to([128, NT, n]), ALU.subtract).then_inc(soft_in, 1)
                dve.wait_ge(soft_exp, r + 1)
                then(dve.tensor_reduce(rsum[:], pr, X, ALU.add))
                then(dve.reciprocal(rinv[:], rsum[:]))
                then(dve.tensor_tensor(pr, pr, rinv[:].unsqueeze(2).broadcast_to([128, NT, n]), ALU.mult))

            def combine(out, n):
                pr, ch = probs[:, :, 0:n], chosen[:, :, 0:n]
                then(dve.tensor_tensor(ch, ch, pr, ALU.mult))
                then(dve.tensor_reduce(rsum[:], ch, X, ALU.add))
                then(dve.reciprocal(rinv[:], rsum[:]))
                then(dve.tensor_tensor(out[:], ch, rinv[:].unsqueeze(2).broadcast_to([128, NT, n]), ALU.mult))

            def ffn(run, comb):
                tiles, per, iters, e0 = RUNS[run]
                experts = tiles // per

                def body(it):
                    for e in range(experts):
                        dve.wait_ge(pj_mm[run], it * tiles + per * (e + 1))
                        if e:
                            dve.wait_ge(acc_done[run], it * (NT * experts) + NT * e)
                        for i in range(NT):
                            n = rows(i)
                            w = comb[0:n, i, bass.ds(it * experts + (e0 + e), 1)]
                            dve.scalar_tensor_tensor(h[0:n, i, :], PB[LATER[i // 2]][0:n, (i % 2) * D:(i % 2 + 1) * D],
                                                     w, h[0:n, i, :], ALU.mult, ALU.add).then_inc(acc_done[run], 1)

                if iters == 1:
                    body(0)
                else:
                    with dve.Fori(0, iters) as it:
                        dve.wait_ge(acc_done[run], it * (NT * experts))
                        body(it)
                dve.wait_ge(acc_done[run], iters * NT * experts)

            def statistics(r, n, p, out):
                dve.wait_ge(stat_t, r + 1)
                dve.tensor_reduce(red[0:n, r:r + 1], PB[6][0:n, 0:p], X, ALU.max).then_inc(red_ready, 1)
                dve.wait_ge(stat_b, r + 1)
                then(dve.tensor_copy(out, PB[7][:, 0:n]))

            def scale_of(name, top, negmin, factor=None):
                then(dve.tensor_tensor(col(name), top, negmin, ALU.add))
                if factor is not None:
                    then(dve.tensor_tensor(col(name), col(name), factor, ALU.mult))
                then(dve.tensor_scalar(col(name), col(name), 1.0 / QMAX, SMIN, ALU.mult, ALU.max))
                then(dve.reciprocal(col(name + "_inv"), col(name)))

            def zero_of(name, negmin, inv):
                then(dve.tensor_tensor(col(name + "_z"), negmin, inv, ALU.mult))
                then(dve.tensor_scalar(col(name + "_z"), col(name + "_z"), MAGIC, None, ALU.add))
                then(dve.tensor_scalar(col(name + "_lo"), col(name + "_z"), -1.0, 2 * MAGIC, ALU.mult, ALU.add))
                then(dve.tensor_scalar(col(name + "_hi"), col(name + "_lo"), QMAX, None, ALU.add))

            for name in ("s1", "s1_inv", "s1_z", "s1_lo", "s1_hi", "gmax", "gneg", "qk", "alpha", "sa", "sa_inv",
                         "sa_z", "sa_lo", "sa_hi", "ceil_t", "ceil_r", "x0", "inv_x0", "x0_30", "neg_x0", "floor_shift",
                         "neg_half_b", "b_t", "b_r", "c_t", "c_r", "half_b2", "poly_c", "so", "so_inv", "so_z", "so_lo",
                         "so_hi", "alpha_o", "omax", "oneg", "sy", "sy_inv", "sy_z", "sy_lo", "sy_hi", "ymax", "yneg"):
                col(name)
            for name in ("s2", "s2_inv", "s2_z", "s2_lo", "s2_hi"):
                col(name, 3)

            settle(dve.memset(mv[:], 1.0))
            settle(dve.memset(logits[:], 0.0))
            settle(dve.memset(v1[:], 1.0))
            settle(dve.memset(stat_o[:], -3.0e38))
            settle(dve.memset(stat_y[:], -3.0e38))
            dve.memset(eps_c[:], EPS).then_inc(eps_ready, 1)
            dve.wait_ge(consts_in, 64)
            dve.tensor_copy(ident_bf[:], ident[:]).then_inc(ident_ready, 1)
            dve.wait_ge(bias_in, 32)
            for i in range(4):
                dve.wait_ge(tok_mm, i + 1)
                settle(dve.tensor_tensor(h[:, i, :], PB[i][:, 0:D], tok_bias[:], ALU.add))
            dve.wait_ge(dve_done, steps[0])
            layernorm(0)
            for j in range(KC):
                for n in range(2):
                    dve.wait_ge(k0_mm, 2 * j + n + 1)
                    dve.tensor_scalar(half(k0, j, n), PB[4 + 2 * j + n][0:DC, 0:HALF].rearrange("p (b s) -> p b s", s=S),
                                      0.1, None, ALU.mult).then_inc(k0_ready, 1)
            for n in range(2):
                dve.wait_ge(s0_ready, n + 1)
                s = s0[:, 4 * n:4 * n + 4, :]
                dve.scalar_tensor_tensor(a0[:, 4 * n:4 * n + 4, :], s, 1.0, s, ALU.add, ALU.mult).then_inc(a0_ready, 1)
            for g in range(3):
                dve.wait_ge(y0_mm, g + 1)
                n, w = (128, 2) if g < 2 else (B, 1)
                hh = h[0:n, 2 * g:2 * g + w, :]
                settle(dve.scalar_tensor_tensor(hh, PB[2 + g][0:n, 0:w * D].rearrange("p (i d) -> p i d", d=D), 0.1, hh,
                                                ALU.mult, ALU.add))
            dve.wait_ge(dve_done, steps[0])
            layernorm(1)
            softmax(0, E0)
            for i in range(NT):
                pf = probs[:, i, 0:E0].unsqueeze(1).broadcast_to([128, E0, E0])
                pe_ = probs[:, i, 0:E0].unsqueeze(2).broadcast_to([128, E0, E0])
                settle(dve.tensor_tensor(cmp_a[:], pf, pe_, ALU.is_gt))
                then(dve.tensor_tensor(cmp_b[:], pf, pe_, ALU.is_equal))
                then(dve.tensor_tensor(cmp_b[:], cmp_b[:], before[:], ALU.mult))
                then(dve.tensor_tensor(cmp_a[:], cmp_a[:], cmp_b[:], ALU.add))
                then(dve.tensor_reduce(rank[:, i, :], cmp_a[:], X, ALU.add))
            then(dve.tensor_scalar(chosen[:, :, 0:E0], rank[:], 1.5, None, ALU.is_lt))
            combine(comb0, E0)
            dve.wait_ge(wq_in, 32)
            then(dve.tensor_reduce(wq_amax[:], wq_raw[:], X, ALU.max, apply_absolute_value=True))
            then(dve.tensor_scalar(wq_scale[:], wq_amax[:], 1.0 / 127.0, SMIN, ALU.mult, ALU.max))
            then(dve.reciprocal(wq_inv[:], wq_scale[:]))
            then(dve.tensor_tensor(wq_int[:], wq_raw[:], wq_inv[:].unsqueeze(2).broadcast_to([DC, 8, D]), ALU.mult))
            then(dve.tensor_scalar(wq_int[:], wq_int[:], MAGIC, MAGIC, ALU.add, ALU.subtract))
            dve.tensor_scalar(wq_int[:], wq_int[:], -128.0, 127.0, ALU.max, ALU.min).then_inc(wint_ready, 1)
            ffn(0, comb0)

            layernorm(2)
            for j in range(6):
                dve.wait_ge(qkv_ready, 2 * j + 2)
                settle(dve.tensor_reduce(stat_q[:, 0, j:j + 1], qkv[:, j], XY, ALU.max))
                last = dve.tensor_reduce(stat_q[:, 1, j:j + 1], qkv[:, j], XY, ALU.min, negate=True)
                if j < 5:
                    settle(last)
            dve.wait_ge(dve_done, steps[0])
            last.then_inc(stat_ready, 1)
            statistics(0, 12, DC, g_q[:])
            then(dve.tensor_reduce(ext[:], g_q[:].rearrange("p (a j) -> p a j", j=2), X, ALU.max))
            settle(dve.tensor_reduce(col("gmax"), ext[:, 0:3], X, ALU.max))
            then(dve.tensor_reduce(col("gneg"), ext[:, 3:6], X, ALU.max))
            scale_of("s1", col("gmax"), col("gneg"))
            zero_of("s1", col("gneg"), col("s1_inv"))
            then(dve.tensor_scalar(ext[:, 3:6], ext[:, 3:6], -1.0, None, ALU.mult))
            then(dve.tensor_scalar(ext_t[:], ext[:], col("s1_inv"), MAGIC, ALU.mult, ALU.add))
            then(dve.tensor_scalar(ext_c[:], ext_t[:], col("s1_lo"), col("s1_hi"), ALU.max, ALU.min))
            then(dve.tensor_scalar(ext_q[:], ext_c[:], MAGIC, col("s1"), ALU.subtract, ALU.mult))
            s2, s2i = col("s2"), col("s2_inv")
            then(dve.tensor_tensor(s2, ext_q[:, 0:3], ext_q[:, 3:6], ALU.subtract))
            then(dve.tensor_scalar(s2, s2, 1.0 / QMAX, SMIN, ALU.mult, ALU.max))
            then(dve.reciprocal(s2i, s2))
            then(dve.tensor_tensor(col("s2_z"), ext_q[:, 3:6], s2i, ALU.mult))
            then(dve.tensor_scalar(col("s2_z"), col("s2_z"), -1.0, MAGIC, ALU.mult, ALU.add))
            then(dve.tensor_scalar(col("s2_lo"), col("s2_z"), -1.0, 2 * MAGIC, ALU.mult, ALU.add))
            then(dve.tensor_scalar(col("s2_hi"), col("s2_lo"), QMAX, None, ALU.add))
            for part in (2, 0, 1):
                z = qkv[:, 2 * part:2 * part + 2]
                then(dve.tensor_scalar(z, z, colp("s1_inv", DC), MAGIC, ALU.mult, ALU.add))
                then(dve.tensor_scalar(z, z, colp("s1_lo", DC), colp("s1_hi", DC), ALU.max, ALU.min))
                then(dve.tensor_scalar(z, z, MAGIC, colp("s1", DC), ALU.subtract, ALU.mult))
                then(dve.tensor_scalar(z, z, colp("s2_inv", DC, part), MAGIC, ALU.mult, ALU.add))
                then(dve.tensor_scalar(z, z, colp("s2_lo", DC, part), colp("s2_hi", DC, part), ALU.max, ALU.min))
                last = dve.tensor_scalar(qkv_int[:, 2 * part:2 * part + 2], z, MAGIC, None, ALU.subtract)
                if part == 2:
                    last.then_inc(v_int_ready, 1)
                else:
                    then(last)
            for kc in range(KC):
                q = cls_cols(qkv_int[:, kc].rearrange("p b s -> p (b s)")).unsqueeze(3).broadcast_to([DC, 4, 2, SLOT])
                own = cls_mask[:, kc, :].unsqueeze(1).unsqueeze(1).broadcast_to([DC, 4, 2, SLOT])
                settle(dve.tensor_tensor(q_cls[:, kc].rearrange("p (i b) m -> p i b m", b=2), q, own, ALU.mult))
            for head in range(HC):
                last = dve.tensor_scalar(k_heads[:, :, :, head, :], qkv_int[:, 2:4], head_mask[:, head:head + 1], None,
                                         ALU.mult)
                if head < HC - 1:
                    settle(last)
            dve.wait_ge(dve_done, steps[0])
            last.then_inc(qk_ready, 1)
            for g in range(9):
                a, z = (HC * g, HC * g + HC) if g < 8 else (48, 50)
                dve.wait_ge(sc_ready, g + 1)
                settle(dve.tensor_reduce(row_hi[:, a:z], sc[:, a:z, :], X, ALU.max))
                settle(dve.tensor_reduce(row_lo[:, a:z], sc[:, a:z, :], X, ALU.min, negate=True))
            dve.wait_ge(dve_done, steps[0])
            then(dve.tensor_reduce(stat_s[:, 0:1], row_hi[:], X, ALU.max))
            dve.tensor_reduce(stat_s[:, 1:2], row_lo[:], X, ALU.max).then_inc(stat_ready, 1)
            statistics(1, 2, 128, g_s[:])
            then(dve.tensor_tensor(col("qk"), c[:, columns["s2"][0]:columns["s2"][0] + 1],
                                   c[:, columns["s2"][0] + 1:columns["s2"][0] + 2], ALU.mult))
            then(dve.tensor_scalar(col("qk"), col("qk"), float(HD) ** -0.5, None, ALU.mult))
            scale_of("sa", g_s[:, 0:1], g_s[:, 1:2], col("qk"))
            then(dve.tensor_tensor(col("alpha"), col("qk"), col("sa_inv"), ALU.mult))
            zero_of("sa", g_s[:, 1:2], col("alpha"))
            then(dve.tensor_scalar(col("ceil_t"), col("sa_inv"), LN2, None, ALU.mult))
            then(dve.tensor_scalar(col("ceil_r"), col("ceil_t"), MAGIC, MAGIC, ALU.add, ALU.subtract))
            then(dve.tensor_tensor(col("x0"), col("ceil_t"), col("ceil_r"), ALU.is_gt))
            then(dve.tensor_tensor(col("x0"), col("x0"), col("ceil_r"), ALU.add))
            then(dve.reciprocal(col("inv_x0"), col("x0")))
            settle(dve.tensor_scalar(col("floor_shift"), col("inv_x0"), 0.5, -0.5, ALU.mult, ALU.add))
            settle(dve.tensor_scalar(col("x0_30"), col("x0"), float(N_EXP), None, ALU.mult))
            settle(dve.tensor_scalar(col("neg_x0"), col("x0"), -1.0, None, ALU.mult))
            then(dve.tensor_scalar(col("b_t"), col("sa_inv"), EXP_B / EXP_A, None, ALU.mult))
            then(dve.tensor_scalar(col("b_r"), col("b_t"), MAGIC, MAGIC, ALU.add, ALU.subtract))
            then(dve.tensor_tensor(col("b_t"), col("b_r"), col("b_t"), ALU.is_gt))
            then(dve.tensor_tensor(col("b_r"), col("b_r"), col("b_t"), ALU.subtract))
            then(dve.tensor_tensor(col("c_t"), col("sa_inv"), col("sa_inv"), ALU.mult))
            then(dve.tensor_scalar(col("c_t"), col("c_t"), EXP_C / EXP_A, None, ALU.mult))
            then(dve.tensor_scalar(col("c_r"), col("c_t"), MAGIC, MAGIC, ALU.add, ALU.subtract))
            then(dve.tensor_tensor(col("c_t"), col("c_r"), col("c_t"), ALU.is_gt))
            then(dve.tensor_tensor(col("c_r"), col("c_r"), col("c_t"), ALU.subtract))
            then(dve.tensor_scalar(col("neg_half_b"), col("b_r"), -0.5, None, ALU.mult))
            then(dve.tensor_tensor(col("half_b2"), col("neg_half_b"), col("neg_half_b"), ALU.mult))
            then(dve.tensor_tensor(col("poly_c"), col("c_r"), col("half_b2"), ALU.subtract))
            then(dve.tensor_scalar(row_hi[:], row_hi[:], col("alpha"), MAGIC, ALU.mult, ALU.add))
            then(dve.tensor_scalar(row_hi[:], row_hi[:], col("sa_lo"), col("sa_hi"), ALU.max, ALU.min))
            for n, (a, z) in enumerate(CHUNKS):
                s = sc[:, a:z, :]
                top = row_hi[:, a:z].unsqueeze(2).broadcast_to([128, z - a, S])
                then(dve.tensor_scalar(s, s, col("alpha"), MAGIC, ALU.mult, ALU.add))
                then(dve.tensor_scalar(s, s, col("sa_lo"), col("sa_hi"), ALU.max, ALU.min))
                then(dve.tensor_tensor(s, top, s, ALU.subtract))
                dve.tensor_scalar(s, s, col("x0_30"), None, ALU.min).then_inc(x_ready, 1)
            for n, (a, z) in enumerate(CHUNKS):
                q = qexp[:, a:z, :]
                dve.wait_ge(y_ready, n + 1)
                dve.tensor_scalar(q, q, MAGIC, MAGIC, ALU.add, ALU.subtract).then_inc(qexp_ready, 1)
                dve.wait_ge(qexp_ready, n + 1)
                dve.scalar_tensor_tensor(rem[:, a:z, :], q, col("neg_x0"), sc[:, a:z, :], ALU.mult,
                                         ALU.add).then_inc(rem_ready, 1)
            for n, (a, z) in enumerate(CHUNKS):
                dve.wait_ge(sq_ready, n + 1)
                last = dve.scalar_tensor_tensor(sc[:, a:z, :], sc[:, a:z, :], col("poly_c"), pow2[:, a:z, :],
                                                ALU.add, ALU.mult)
                if n == 0:
                    last.then_inc(e_ready, 1)
            then(last)
            then(dve.tensor_reduce(cls_sum[:], sc[:, 48:50, :], X, ALU.add))
            then(dve.reciprocal(cls_sum[:], cls_sum[:]))
            dve.tensor_tensor(sc[:, 48:50, :], sc[:, 48:50, :], cls_sum[:].unsqueeze(2).broadcast_to([128, 2, S]),
                              ALU.mult).then_inc(e_ready, 1)
            for g in range(1, GROUPS, 2):
                n = min(4, ROWS - 4 * g)
                dve.wait_ge(et_mm, g + 1)
                dve.tensor_copy(e_t[:, 4 * g:4 * g + n, :],
                                PB[g % 6][0:S, 0:n * 128].rearrange("p (r q) -> p r q", q=128)).then_inc(et_dve, 1)
            for g in range(2):
                dve.wait_ge(pv_mm, g + 1)
                acc = PB[6 + g][:, 0:2 * NH * (HD + 1)].rearrange("p (i h d) -> p i h d", i=2, h=NH)
                inv = o_inv[:, 2 * g:2 * g + 2, :]
                then(dve.reciprocal(inv, acc[:, :, :, HD]))
                then(dve.tensor_tensor(o1[:, 2 * g:2 * g + 2], acc[:, :, :, 0:HD],
                                       inv.unsqueeze(3).broadcast_to([128, 2, NH, HD]), ALU.mult))
            dve.wait_ge(pvc_mm, 1)
            ocm = o_cls_m[:].rearrange("p (b j) h -> p b j h", j=KC)
            src = PB[0][0:DC, 0:B * KC * NH].rearrange("p (b j h) -> p b j h", b=B, j=KC)
            own = cls_mask[:, :, 0:NH].unsqueeze(1).broadcast_to([DC, B, KC, NH])
            then(dve.tensor_tensor(ocm, src, own, ALU.mult))
            then(dve.tensor_reduce(o_cls[:], o_cls_m[:], X, ALU.add))
            flat = o1[:].rearrange("p i h d -> p (i h d)")
            settle(dve.tensor_reduce(stat_o[:, 0:1], flat, X, ALU.max))
            settle(dve.tensor_reduce(stat_o[:, 1:2], flat, X, ALU.min, negate=True))
            settle(dve.tensor_reduce(stat_o[0:DC, 2:3], o_cls[:], X, ALU.max))
            last = dve.tensor_reduce(stat_o[0:DC, 3:4], o_cls[:], X, ALU.min, negate=True)
            dve.wait_ge(dve_done, steps[0])
            last.then_inc(stat_ready, 1)
            statistics(2, 4, 128, g_o[:])
            settle(dve.tensor_tensor(col("omax"), g_o[:, 0:1], g_o[:, 2:3], ALU.max))
            then(dve.tensor_tensor(col("oneg"), g_o[:, 1:2], g_o[:, 3:4], ALU.max))
            sv = c[:, columns["s2"][0] + 2:columns["s2"][0] + 3]
            scale_of("so", col("omax"), col("oneg"), sv)
            then(dve.tensor_tensor(col("alpha_o"), sv, col("so_inv"), ALU.mult))
            zero_of("so", col("oneg"), col("alpha_o"))
            then(dve.tensor_scalar(flat, flat, col("alpha_o"), MAGIC, ALU.mult, ALU.add))
            then(dve.tensor_scalar(flat, flat, col("so_lo"), col("so_hi"), ALU.max, ALU.min))
            dve.tensor_scalar(o1_int[:].rearrange("p i f -> p (i f)"), flat, MAGIC, None, ALU.subtract).then_inc(o1_ready, 1)
            then(dve.tensor_scalar(o_cls[:], o_cls[:], colp("alpha_o", DC), MAGIC, ALU.mult, ALU.add))
            then(dve.tensor_scalar(o_cls[:], o_cls[:], colp("so_lo", DC), colp("so_hi", DC), ALU.max, ALU.min))
            dve.tensor_scalar(o1_t[:, :, 512:520].rearrange("p j b -> p b j"),
                              o_cls[:].rearrange("p (b j) -> p b j", j=KC), MAGIC, None, ALU.subtract).then_inc(ocls_ready, 1)
            dve.wait_ge(wint_t_ready, 5)
            then(dve.tensor_scalar(proj_scale[:], proj_scale[:], col("so"), None, ALU.mult))
            dve.wait_ge(bq_in, 32)
            for g in range(3):
                dve.wait_ge(y1_mm, g + 1)
                n, w = (128, 2) if g < 2 else (B, 1)
                yy = y1[0:n, 2 * g:2 * g + w, :]
                then(dve.tensor_tensor(yy, PB[3 + g][0:n, 0:w * D].rearrange("p (i d) -> p i d", d=D),
                                       proj_scale[0:n, :].unsqueeze(1).broadcast_to([n, w, D]), ALU.mult))
                then(dve.tensor_tensor(yy, yy, b_proj[0:n, :].unsqueeze(1).broadcast_to([n, w, D]), ALU.add))
            patch_y, cls_y = y1[:, 0:4, :], y1[0:B, 4, :]
            settle(dve.tensor_reduce(stat_y[:, 0:1], patch_y, XY, ALU.max))
            settle(dve.tensor_reduce(stat_y[:, 1:2], patch_y, XY, ALU.min, negate=True))
            settle(dve.tensor_reduce(stat_y[0:B, 2:3], cls_y, X, ALU.max))
            last = dve.tensor_reduce(stat_y[0:B, 3:4], cls_y, X, ALU.min, negate=True)
            dve.wait_ge(dve_done, steps[0])
            last.then_inc(stat_ready, 1)
            statistics(3, 4, 128, g_y[:])
            settle(dve.tensor_tensor(col("ymax"), g_y[:, 0:1], g_y[:, 2:3], ALU.max))
            then(dve.tensor_tensor(col("yneg"), g_y[:, 1:2], g_y[:, 3:4], ALU.max))
            scale_of("sy", col("ymax"), col("yneg"))
            zero_of("sy", col("yneg"), col("sy_inv"))
            for p, y, hh in ((128, patch_y, h[:, 0:4, :]), (B, cls_y, h[0:B, 4, :])):
                then(dve.tensor_scalar(y, y, colp("sy_inv", p), MAGIC, ALU.mult, ALU.add))
                then(dve.tensor_scalar(y, y, colp("sy_lo", p), colp("sy_hi", p), ALU.max, ALU.min))
                then(dve.tensor_scalar(y, y, MAGIC, colp("sy", p), ALU.subtract, ALU.mult))
                then(dve.tensor_tensor(hh, hh, y, ALU.add))
            layernorm(3)
            softmax(1, E1)
            for i in range(NT):
                then(dve.max(top8[:, i, :], probs[:, i, :]))
                then(dve.match_replace(left[:, i, :], top8[:, i, :], probs[:, i, :], -1.0))
            then(dve.tensor_scalar(chosen[:], left[:], 0.0, None, ALU.is_lt))
            combine(comb1, E1)
            ffn(1, comb1)
            ffn(2, comb1)


def lay_out(np, x, cls_tok, L0_tok_w, L0_tok_b, L0_attn_Wq, L0_attn_Wk, L0_attn_Wv, L0_attn_Wo, L0_ffn_w_fc,
            L0_ffn_w_proj, L0_ffn_w_gate, L1_attn_w_qkv, L1_attn_b_qkv, L1_attn_w_proj, L1_attn_b_proj,
            L1_ffn_router_w, L1_ffn_w1, L1_ffn_w2):
    def chunks(w):
        return w.reshape(KC, DC, -1).transpose(1, 0, 2)

    feature = np.arange(DC) // HD
    column = np.arange(SLOT) % NH
    a = {
        "patches": x.reshape(B, 8, 32, 8, 32).transpose(2, 4, 0, 1, 3).reshape(TOKK, 128, B * PATCH),
        "w_tok": L0_tok_w.T.reshape(TOKK, 128, D),
        "tok_bias": L0_tok_b,
        "cls_tok": cls_tok.reshape(D),
        "w_l0": np.stack([chunks(w.T) for w in (L0_attn_Wq, L0_attn_Wk, L0_attn_Wv, L0_attn_Wo)], axis=1),
        "w_gate0": chunks(L0_ffn_w_gate),
        "w_gate1": chunks(L1_ffn_router_w.T),
        "fc0": L0_ffn_w_fc.reshape(KC, DC, T0 * 128, E0).transpose(3, 1, 0, 2),
        "pj0": L0_ffn_w_proj.reshape(T0, 128, D, E0).transpose(3, 1, 0, 2),
        "w_qkv": L1_attn_w_qkv.reshape(6, DC, D).transpose(1, 0, 2),
        "w_proj": L1_attn_w_proj.reshape(KC, DC, D).transpose(1, 0, 2),
        "b_qkv": L1_attn_b_qkv.reshape(6, DC).T,
        "b_proj": L1_attn_b_proj,
        "fc1": L1_ffn_w1.reshape(KC, DC, 6, 512).transpose(2, 1, 0, 3),
        "pj1": L1_ffn_w2.reshape(6, 4, 128, D).transpose(0, 2, 1, 3),
        "ident": np.eye(128, dtype=np.float32),
        "head_mask": (feature[:, None] == np.arange(HC)).astype(np.float32),
        "cls_mask": (feature[:, None, None] + HC * np.arange(KC)[:, None] == column).astype(np.float32),
        "before": np.broadcast_to(np.arange(E0) < np.arange(E0)[:, None], (128, E0, E0)).astype(np.float32),
    }
    return {k: np.ascontiguousarray(v) for k, v in a.items()}


def kernel(**inputs):
    import numpy as np
    import concourse.bacc as bacc
    from concourse.bass_utils import run_bass_kernel_spmd

    arrays = lay_out(np, **{k: np.asarray(v) for k, v in inputs.items()})
    nc = bacc.Bacc("TRN2", target_bir_lowering=False, num_devices=1)
    t = {k: nc.dram_tensor(k + "_dram", v.shape, mybir.dt.from_np(v.dtype), kind="ExternalInput").ap()
         for k, v in arrays.items()}
    t["out"] = nc.dram_tensor("out_dram", (B, S, D), F32, kind="ExternalOutput").ap()
    build(nc, t)
    r = run_bass_kernel_spmd(nc, [{k + "_dram": v for k, v in arrays.items()}], core_ids=[0])
    return r.results[0]["out_dram"]
```

```python
from contextlib import ExitStack

import concourse.bass as bass
from concourse import mybir

F32 = mybir.dt.float32
BF16 = mybir.dt.bfloat16
F32R = mybir.dt.float32r
ALU = mybir.AluOpType
ACT = mybir.ActivationFunctionType
X = mybir.AxisListType.X
XY = mybir.AxisListType.XY

B, D, PATCH = 8, 192, 64
S = PATCH + 1
KC, DC = 2, 96
NT = 5
HALF = 4 * S
NH, HD, HC = 12, 16, 6
TOKK = 8
EPS = 1e-5
HT = 128
MAGIC = 12582912.0
QMAX, SMIN = 255.0, 1e-8
LN2, EXP_A, EXP_B, EXP_C, N_EXP = 0.6931471805599453, 0.35815147, 0.96963238, 1.0, 30
E0, T0 = 8, 6
E1 = 16
ROWS = 50
GROUPS = 13
SLOT = 32


def build(nc, t):
    with ExitStack() as ctx:
        def sb(name, shape, dt=F32):
            return ctx.enter_context(nc.sbuf_tensor(name, shape, dt))

        def sem(name):
            return ctx.enter_context(nc.semaphore(name))

        PB = [ctx.enter_context(nc.psum_tensor(f"bank{i}", [128, 512], F32)) for i in range(8)]

        class Area:
            def __init__(self, name, words):
                self.raw, self.at, self.words = sb(name, [128, words]), 0, words

            def take(self, p, shape):
                n = 1
                for d in shape:
                    n *= d
                assert self.at + n <= self.words
                flat = self.raw[0:p, self.at:self.at + n]
                self.at += n
                names = "abcd"[:len(shape)]
                return flat.rearrange(f"p ({' '.join(names)}) -> p {' '.join(names)}", **dict(zip(names[1:], shape[1:])))

            def again(self):
                self.at = 0

        embed_area = Area("embed_area", ROWS * S + B * NH * (HD + 1) + 4 * D)
        patches = embed_area.take(128, [TOKK, B * PATCH])
        w_tok = embed_area.take(128, [TOKK, D])
        tok_bias = sb("tok_bias", [128, D])
        score_area = Area("score_area", ROWS * S)
        attn1_area = Area("attn1_area", 3 * KC * B * S + B * D + 2 * B * S + 8 * D)
        hidden_area = Area("hidden_area", ROWS * S)
        w_l0 = score_area.take(DC, [4, KC, D])
        w_gate0 = sb("w_gate0", [DC, KC, E0])
        w_gate1 = sb("w_gate1", [DC, KC, E1])
        ident = sb("ident", [128, 128])
        ident_bf = sb("ident_bf", [128, 128], BF16)
        head_mask = sb("head_mask", [DC, HC])
        cls_mask = sb("cls_mask", [DC, KC, SLOT])
        before = sb("before", [128, E0, E0])
        h = sb("h", [128, NT, D])
        xn = sb("xn", [128, NT, D])
        xt = sb("xt", [DC, KC, B * S])
        bn6 = sb("bn6", [128, NT, 6])
        mv = sb("mv", [128, NT, 2])
        var_eps = sb("var_eps", [128, NT])
        std = sb("std", [128, NT])
        rstd = sb("rstd", [128, NT])
        newton = sb("newton", [128, NT])
        eps_c = sb("eps_c", [128, 1])
        q0, k0, o0 = (attn1_area.take(DC, [KC, B, S]) for _ in range(3))
        v0 = attn1_area.take(S, [B, D])
        s0, a0 = (attn1_area.take(S, [B, S]) for _ in range(2))
        logits = sb("logits", [128, NT, E1])
        probs = sb("probs", [128, NT, E1])
        rmax = sb("rmax", [128, NT])
        rsum = sb("rsum", [128, NT])
        rinv = sb("rinv", [128, NT])
        cmp_a = sb("cmp_a", [128, E0, E0])
        cmp_b = sb("cmp_b", [128, E0, E0])
        rank = sb("rank", [128, NT, E0])
        top8 = sb("top8", [128, NT, 8])
        left = sb("left", [128, NT, E1])
        chosen = sb("chosen", [128, NT, E1])
        comb0 = sb("comb0", [128, NT, E0])
        comb1 = sb("comb1", [128, NT, E1])
        raw_area = Area("raw_area", 2 * (KC * T0 * HT + T0 * D))
        fc_raw = raw_area.take(DC, [2, KC, T0 * HT])
        pj_raw = raw_area.take(128, [2, T0, D])
        fc_hi = sb("fc_hi", [DC, 2, KC, T0 * HT], F32R)
        fc_lo = sb("fc_lo", [DC, 2, KC, T0 * HT], F32R)
        pj_hi = sb("pj_hi", [128, 2, T0, D], F32R)
        pj_lo = sb("pj_lo", [128, 2, T0, D], F32R)
        xt_hi = sb("xt_hi", [DC, KC, B * S], F32R)
        xt_lo = sb("xt_lo", [DC, KC, B * S], F32R)
        hid_hi = sb("hid_hi", [128, 2, B * S], F32R)
        hid_lo = sb("hid_lo", [128, 2, B * S], F32R)
        o0_cls = sb("o0_cls", [DC, KC, B])
        hid = hidden_area.take(128, [2, B * S])
        hid_w = hidden_area.take(128, [2, B * S])
        tok_w_b = hidden_area.take(128, [2, B * S])
        comb_r = sb("comb_r", [128, NT, 2 * E1], F32R)
        comb_t = sb("comb_t", [2 * E1, B * S])
        one_expert = sb("one_expert", [2 * E1, 2, B * S], F32R)
        pick0 = sb("pick0", [2 * E0, E0 + 2])
        pick1 = sb("pick1", [2 * E1, E1 + 2])
        ones_r = sb("ones_r", [2 * E1, 128], F32R)
        ones_f = sb("ones_f", [2 * E1, 128])
        zeros = sb("zeros", [128, HALF], BF16)
        wq_raw = attn1_area.take(DC, [8, D])
        wq_amax = sb("wq_amax", [DC, 8])
        wq_scale = sb("wq_scale", [DC, 8])
        wq_inv = sb("wq_inv", [DC, 8])
        wq_int = score_area.take(DC, [8, D])
        w_qkv_t = sb("w_qkv_t", [DC, KC, 6 * DC], F32R)
        w_proj_t = sb("w_proj_t", [DC, KC, D], BF16)
        b_qkv = sb("b_qkv", [DC, 6])
        b_proj = sb("b_proj", [128, D])
        proj_scale = sb("proj_scale", [128, D])
        attn1_area.again()
        qkv = attn1_area.take(DC, [6, B, S])
        qkv_int = sb("qkv_int", [DC, 6, B, S], BF16)
        k_heads = attn1_area.take(DC, [6, B * S]).rearrange("p a b -> p (a b)").bitcast(BF16).rearrange(
            "p (j b h s) -> p j b h s", j=KC, b=B, h=HC)
        q_cls = sb("q_cls", [DC, KC, B, SLOT], BF16)
        for area in (embed_area, raw_area, score_area, attn1_area, hidden_area):
            area.again()
        v1 = embed_area.take(S, [B, NH, HD + 1])
        rem = embed_area.take(128, [ROWS, S])
        pow2 = raw_area.take(128, [ROWS, S])
        v1_flat = raw_area.take(S, [B, D])
        o1 = embed_area.take(128, [4, NH, HD])
        sc = score_area.take(128, [ROWS, S])
        qexp = hidden_area.take(128, [ROWS, S])
        e_t = attn1_area.take(S, [ROWS, 128])
        row_hi = sb("row_hi", [128, ROWS])
        row_lo = sb("row_lo", [128, ROWS])
        cls_sum = sb("cls_sum", [128, 2])
        o_inv = sb("o_inv", [128, 4, NH])
        o1_int = sb("o1_int", [128, 4, NH * HD], BF16)
        o_cls_m = sb("o_cls_m", [DC, B * KC, NH])
        o_cls = sb("o_cls", [DC, B * KC])
        o1_t = sb("o1_t", [DC, KC, B * S], BF16)
        y1 = xn
        stat_q = sb("stat_q", [DC, 2, 6])
        stat_s = sb("stat_s", [128, 2])
        stat_o = sb("stat_o", [128, 4])
        stat_y = sb("stat_y", [128, 4])
        red = sb("red", [12, 4])
        g_q = sb("g_q", [128, 12])
        g_s = sb("g_s", [128, 2])
        g_o = sb("g_o", [128, 4])
        g_y = sb("g_y", [128, 4])
        ext = sb("ext", [128, 6])
        ext_t = sb("ext_t", [128, 6])
        ext_c = sb("ext_c", [128, 6])
        ext_q = sb("ext_q", [128, 6])
        c = sb("consts", [128, 64])
        columns = {}

        def col(name, n=1):
            if name not in columns:
                columns[name] = (sum(w for _, w in columns.values()), n)
                assert sum(w for _, w in columns.values()) <= 64
            at, w = columns[name]
            return c[:, at:at + w]

        def colp(name, p, i=0):
            at, _ = columns[name]
            return c[0:p, at + i:at + i + 1]

        tok_in = [sem(f"tok_in{k}") for k in range(TOKK)]
        bias_in = sem("bias_in")
        w_l0_in = sem("w_l0_in")
        consts_in = sem("consts_in")
        gates_in = sem("gates_in")
        wq_in = sem("wq_in")
        bq_in = sem("bq_in")
        raw_in = [sem(f"raw_in{s}") for s in range(2)]
        w_hi_done = [sem(f"w_hi_done{s}") for s in range(2)]
        w_lo_done = [sem(f"w_lo_done{s}") for s in range(2)]
        dve_done = sem("dve_done")
        act_done = sem("act_done")
        tok_mm = sem("tok_mm")
        ident_ready = sem("ident_ready")
        mv_ready = sem("mv_ready")
        eps_ready = sem("eps_ready")
        std_ready = sem("std_ready")
        xn_ready = sem("xn_ready")
        xt_mm = sem("xt_mm")
        xt_act = sem("xt_act")
        xt_dve = sem("xt_dve")
        q0_mm = sem("q0_mm")
        k0_mm = sem("k0_mm")
        q0_ready = sem("q0_ready")
        k0_ready = sem("k0_ready")
        v0_mm = sem("v0_mm")
        v0_ready = sem("v0_ready")
        s0_mm = sem("s0_mm")
        s0_ready = sem("s0_ready")
        a0_ready = sem("a0_ready")
        o0_mm = sem("o0_mm")
        o0_ready = sem("o0_ready")
        y0_mm = sem("y0_mm")
        gate_mm = sem("gate_mm")
        soft_in = sem("soft_in")
        soft_exp = sem("soft_exp")
        logits_out = sem("logits_out")
        comb_ready = sem("comb_ready")
        comb_mm = sem("comb_mm")
        comb_t_ready = sem("comb_t_ready")
        xhi_ready = sem("xhi_ready")
        xlo_ready = sem("xlo_ready")
        picked = [sem(f"picked{n}") for n in range(2)]
        entry_mm = [sem(f"entry_mm{n}") for n in range(2)]
        entry_out = [sem(f"entry_out{n}") for n in range(2)]
        weighted = [sem(f"weighted{n}") for n in range(2)]
        hid_hi_ready = [sem(f"hid_hi_ready{n}") for n in range(2)]
        hid_lo_ready = [sem(f"hid_lo_ready{n}") for n in range(2)]
        pj_mm = [sem(f"pj_mm{n}") for n in range(2)]
        sum_out = sem("sum_out")
        back_mm = sem("back_mm")
        h_done = sem("h_done")
        wint_ready = sem("wint_ready")
        wint_t_mm = sem("wint_t_mm")
        wint_t_ready = sem("wint_t_ready")
        pscale_mm = sem("pscale_mm")
        qkv_mm = sem("qkv_mm")
        qkv_ready = sem("qkv_ready")
        stat_ready = sem("stat_ready")
        stat_t = sem("stat_t")
        red_ready = sem("red_ready")
        stat_b = sem("stat_b")
        v_int_ready = sem("v_int_ready")
        qk_ready = sem("qk_ready")
        v1_ones = sem("v1_ones")
        v1_mm = sem("v1_mm")
        v1_ready = sem("v1_ready")
        sc_mm = sem("sc_mm")
        sc_ready = sem("sc_ready")
        x_ready = sem("x_ready")
        y_ready = sem("y_ready")
        qexp_ready = sem("qexp_ready")
        pow2_ready = sem("pow2_ready")
        rem_ready = sem("rem_ready")
        sq_ready = sem("sq_ready")
        e_ready = sem("e_ready")
        et_mm = sem("et_mm")
        et_act = sem("et_act")
        et_dve = sem("et_dve")
        pv_mm = sem("pv_mm")
        pvc_mm = sem("pvc_mm")
        o1_ready = sem("o1_ready")
        o1t_mm = sem("o1t_mm")
        o1t_ready = sem("o1t_ready")
        ocls_ready = sem("ocls_ready")
        y1_mm = sem("y1_mm")
        h_ready = sem("h_ready")
        out_done = sem("out_done")

        def tile_tokens(fm, kc, i):
            return fm[:, kc, i * 128:i * 128 + rows(i)]

        def pairs(cols):
            return cols.rearrange("p (i q) -> p i q", q=2 * S)

        def cls_cols(cols):
            return pairs(cols)[:, :, 0:2 * S:2 * S - 1]

        def patch_at(b):
            return 1 if b % 2 == 0 else 0

        def half(fm, kc, n):
            return fm[:, kc, 4 * n:4 * n + 4, :]

        def xt_half(kc, n):
            return xt[:, kc, n * HALF:(n + 1) * HALF]

        def xt_patches(r, j, i):
            if r % 2 == 0:
                return pairs(xt[:, j, :])[:, i:i + 2, 1:129]
            return xt[:, j, i * 128:(i + 2) * 128].rearrange("p (i q) -> p i q", i=2)

        def rows(i):
            return 128 if i < 4 else B

        CHUNKS = [(0, 26), (26, 50)]
        SUMS = [2, 3, 4, 5]
        PAIRS = [(0, 1), (6, 7)]

        class Run:
            def __init__(self, layer, tiles, per, iters, tiles0=0, entries0=0, experts0=0, load0=0):
                self.layer, self.tiles, self.per, self.iters = layer, tiles, per, iters
                self.unit = tiles // 2
                self.experts = tiles // per
                self.tiles0, self.entries0, self.experts0, self.load0 = tiles0, entries0, experts0, load0
                self.entries = []
                for e in range(self.experts):
                    self.entries.append(("w", e))
                    self.entries += [("h", e * per + j) for j in range(per)]
                self.entries[0], self.entries[1] = self.entries[1], self.entries[0]
                self.width = (T0 if layer == 0 else 4)

            def tile(self, it):
                return it * self.tiles + self.tiles0

            def entry(self, it):
                return it * len(self.entries) + self.entries0

            def expert(self, it):
                return it * self.experts + self.experts0

        RUNS = [[Run(0, 2 * T0, T0, E0 // 2)],
                [Run(1, 8, 1, 1, load0=4), Run(1, 8, 2, 1, 8, 16, 8, 5), Run(1, 8, 2, 1, 16, 28, 12, 6)]]

        def run_loop(eng, run, body):
            if run.iters == 1:
                body(0)
            else:
                with eng.Fori(0, run.iters) as it:
                    body(it)

        block = ctx.enter_context(nc.Block())

        @block.sync
        def _(sp):
            for k in range(TOKK):
                sp.dma_start(patches[:, k, :], t["patches"][k]).then_inc(tok_in[k], 16)
                sp.dma_start(w_tok[:, k, :], t["w_tok"][k]).then_inc(tok_in[k], 16)
            sp.dma_start(w_l0[:], t["w_l0"]).then_inc(w_l0_in, 16)
            def load(s, fc, pj, w):
                sp.dma_start(fc_raw[:, s, :, 0:w * HT], fc).then_inc(raw_in[s], 16)
                sp.dma_start(pj_raw[:, s, 0:w, :], pj).then_inc(raw_in[s], 16)

            def wait_split(s, n):
                sp.wait_ge(w_hi_done[s], 3 * n)
                sp.wait_ge(w_lo_done[s], 3 * n)

            for s in range(2):
                load(s, t["fc0"][s], t["pj0"][s], T0)
            with sp.Fori(1, E0 // 2) as it:
                for s in range(2):
                    wait_split(s, it)
                    load(s, t["fc0"][bass.ds(it * 2 + s, 1)].squeeze(0), t["pj0"][bass.ds(it * 2 + s, 1)].squeeze(0), T0)
            for n in range(3):
                for s in range(2):
                    wait_split(s, E0 // 2 + n)
                    if (n, s) == (0, 1):
                        sp.wait_ge(pvc_mm, 1)
                        sp.wait_ge(e_ready, 2)
                    load(s, t["fc1"][2 * n + s], t["pj1"][2 * n + s], 4)
            sp.wait_ge(h_done, 6)
            for b in range(B):
                lo = (b % 2) * PATCH
                sp.dma_start(t["out"][b, 1:S, :], h[lo:lo + PATCH, b // 2, :]).then_inc(out_done, 16)
            sp.dma_start(t["out"][:, 0, :], h[0:B, 4, :]).then_inc(out_done, 16)
            sp.wait_ge(out_done, 16 * (B + 1))

        @block.gpsimd
        def _(pool):
            pool.dma_start(wq_raw[:, 0:6, :], t["w_qkv"]).then_inc(wq_in, 16)
            pool.dma_start(wq_raw[:, 6:8, :], t["w_proj"]).then_inc(wq_in, 16)
            pool.dma_start(ident[:], t["ident"]).then_inc(consts_in, 16)
            pool.dma_start(head_mask[:], t["head_mask"]).then_inc(consts_in, 16)
            pool.dma_start(cls_mask[:], t["cls_mask"]).then_inc(consts_in, 16)
            pool.dma_start(before[:], t["before"]).then_inc(consts_in, 16)
            pool.dma_start(tok_bias[:], t["tok_bias"].partition_broadcast(128)).then_inc(bias_in, 16)
            pool.dma_start(h[0:B, 4, :], t["cls_tok"].partition_broadcast(B)).then_inc(bias_in, 16)
            pool.dma_start(pick0[:], t["pick0"]).then_inc(gates_in, 16)
            pool.dma_start(pick1[:], t["pick1"]).then_inc(gates_in, 16)
            pool.dma_start(w_gate0[:], t["w_gate0"]).then_inc(gates_in, 16)
            pool.dma_start(w_gate1[:], t["w_gate1"]).then_inc(gates_in, 16)
            pool.dma_start(b_qkv[:], t["b_qkv"]).then_inc(bq_in, 16)
            pool.dma_start(b_proj[:], t["b_proj"].partition_broadcast(128)).then_inc(bq_in, 16)

            def split_lo(s, n, w):
                for piece in range(3):
                    pool.wait_ge(w_hi_done[s], n * 3 + (piece - 2))
                    lo, raw, hi = [(fc[:, s, piece, 0:w * HT] if piece < 2 else pj[:, s, 0:w, :])
                                   for fc, pj in ((fc_lo, pj_lo), (fc_raw, pj_raw), (fc_hi, pj_hi))]
                    pool.tensor_tensor(lo, raw, hi.bitcast(F32), ALU.subtract).then_inc(w_lo_done[s], 1)

            with pool.Fori(1, E0 // 2 + 1) as n:
                for s in range(2):
                    split_lo(s, n, T0)
            for n in range(3):
                for s in range(2):
                    split_lo(s, E0 // 2 + 1 + n, 4)

        @block.tensor
        def _(pe):
            def wait_xt(r):
                pe.wait_ge(xt_act, 4 * (r + 1))
                pe.wait_ge(xt_dve, 2 * (r + 1))

            def transpose_x(r):
                for i in range(NT):
                    pe.wait_ge(xn_ready, NT * r + i + 1)
                    n = rows(i)
                    for j in range(KC):
                        at = (i % 2) * 256 + j * 128 if i < 4 else j * B
                        last = pe.transpose(PB[i // 2][0:DC, at:at + n], xn[0:n, i, j * DC:(j + 1) * DC],
                                            ident[0:n, 0:n])
                    last.then_inc(xt_mm, 1)

            def wait_split_x(n):
                pe.wait_ge(xhi_ready, 2 * n)
                pe.wait_ge(xlo_ready, 2 * n)

            def mm_kc(out, lhs, rhs, n=KC):
                for kc in range(n):
                    last = pe.matmul(out, lhs(kc), rhs(kc), start=(kc == 0), stop=(kc == n - 1))
                return last

            def gate(r, w, n):
                wait_xt(r)
                pe.wait_ge(gates_in, 64)
                for i in range(NT):
                    last = mm_kc(PB[3][0:rows(i), i * n:(i + 1) * n],
                                 lambda kc: tile_tokens(xt, kc, i), lambda kc: w[:, kc, :])
                last.then_inc(gate_mm, 1)

            def split3(out, lhs, rhs, start, stop, last_kc=KC):
                for n, (a, b) in enumerate(((0, 0), (0, 1), (1, 0))):
                    mm = pe.matmul(out, lhs[a], rhs[b], start=start and n == 0, stop=stop and n == 2,
                                   skip_group_check=True)
                return mm

            def comb_turn(layer, n_exp):
                pe.wait_ge(comb_ready, layer + 1)
                for i in range(NT):
                    n = rows(i)
                    out = PB[2][0:2 * n_exp, i * 128:(i + 1) * 128] if i < 4 else PB[3][0:2 * n_exp, 0:B]
                    last = pe.transpose(out, comb_r[0:n, i, 0:2 * n_exp].bitcast(F32), ident[0:n, 0:n])
                last.then_inc(comb_mm, 1)

            def clear_sums(layer):
                pe.wait_ge(comb_t_ready, 2 * (layer + 1))
                for k in SUMS:
                    mm = pe.matmul(PB[k][0:DC, 0:HALF], zeros[:, 0:DC], zeros[:], start=True, stop=True,
                                   skip_group_check=True)
                mm.then_inc(pj_mm[layer], 1)

            def ffn(run, n_exp):
                y = run.layer

                def entry(it, k):
                    kind, x = run.entries[k]
                    if kind == "w":
                        pe.wait_ge(picked[y], run.expert(it) + x + 1)
                    else:
                        s, j = x // run.unit, x % run.unit
                        if j == 0:
                            pe.wait_ge(w_lo_done[s], it * 3 + 3 * (run.load0 + 1))
                    for n in range(2):
                        if k >= 2:
                            pe.wait_ge(entry_out[y], 2 * run.entry(it) + (2 * k - 3 + n))
                        out = PB[PAIRS[k % 2][n]][:, 0:HALF]
                        if kind == "w":
                            mm = pe.matmul(out, ones_r[0:2 * n_exp, :],
                                           one_expert[0:2 * n_exp, x % 2, n * HALF:(n + 1) * HALF],
                                           start=True, stop=True)
                        else:
                            for kc in range(KC):
                                cols, tok = slice(j * HT, (j + 1) * HT), slice(n * HALF, (n + 1) * HALF)
                                mm = split3(out, (fc_hi[:, s, kc, cols], fc_lo[:, s, kc, cols]),
                                            (xt_hi[:, kc, tok], xt_lo[:, kc, tok]), kc == 0, kc == KC - 1)
                        mm.then_inc(entry_mm[y], 1)

                def project(it, g):
                    s, j = g // run.unit, g % run.unit
                    pe.wait_ge(hid_lo_ready[y], run.tile(it) + g + 1)
                    for c in range(KC):
                        for n in range(2):
                            cols, tok = slice(c * DC, (c + 1) * DC), slice(n * HALF, (n + 1) * HALF)
                            mm = split3(PB[SUMS[2 * c + n]][0:DC, 0:HALF], (pj_hi[:, s, j, cols], pj_lo[:, s, j, cols]),
                                        (hid_hi[:, g % 2, tok], hid_lo[:, g % 2, tok]), False, True)
                    mm.then_inc(pj_mm[y], 1)

                def body(it):
                    for k, (kind, x) in enumerate(run.entries):
                        entry(it, k)
                        if kind == "h" and x:
                            project(it, x - 1)
                    project(it, run.tiles - 1)

                run_loop(pe, run, body)

            def turn_back(layer):
                for i in range(NT):
                    pe.wait_ge(sum_out, 4 * (layer + 1))
                    for c in range(KC):
                        last = pe.transpose(PB[(0, 1, 6)[i // 2]][0:rows(i), (i % 2) * D + c * DC:(i % 2) * D + (c + 1) * DC],
                                            tile_tokens(xt, c, i), ident[0:DC, 0:DC])
                    if i % 2 or i == 4:
                        last.then_inc(back_mm, 1)

            def statistics(r, stat, n, p, out_cols):
                pe.wait_ge(stat_ready, r + 1)
                pe.transpose(PB[6][0:n, 0:p], stat, ident[0:p, 0:p]).then_inc(stat_t, 1)
                pe.wait_ge(red_ready, r + 1)
                pe.matmul(PB[7][:, 0:n], red[0:n, r:r + 1].broadcast_to([n, 128]), ident[0:n, 0:n],
                          start=True, stop=True).then_inc(stat_b, 1)

            for k in range(TOKK):
                pe.wait_ge(tok_in[k], 32)
                for i in range(4):
                    mm = pe.matmul(PB[i][:, 0:D], patches[:, k, i * 128:(i + 1) * 128], w_tok[:, k, :],
                                   start=(k == 0), stop=(k == TOKK - 1))
                    if k == TOKK - 1:
                        mm.then_inc(tok_mm, 1)
            pe.wait_ge(consts_in, 64)
            pe.wait_ge(wint_ready, 1)
            for hr in range(2):
                for kc in range(KC):
                    for j in range(4):
                        last = pe.transpose(PB[4 + 2 * hr + kc][0:DC, j * DC:(j + 1) * DC],
                                            wq_int[:, 4 * hr + j, kc * DC:(kc + 1) * DC], ident[0:DC, 0:DC])
                    if hr:
                        last = pe.matmul(PB[6 + kc][:, 4 * DC:5 * DC], wq_scale[:, 6 + kc:7 + kc].broadcast_to([DC, 128]),
                                         ident[0:DC, 0:DC], start=True, stop=True)
                    last.then_inc(wint_t_mm, 1)
            transpose_x(0)
            wait_xt(0)
            pe.wait_ge(w_l0_in, 16)
            pe.wait_ge(wint_t_ready, 6)
            for w, done in ((0, q0_mm), (1, k0_mm)):
                for j in range(KC):
                    for n in range(2):
                        mm_kc(PB[4 * w + 2 * j + n][0:DC, 0:HALF], lambda kc: w_l0[:, w, kc, j * DC:(j + 1) * DC],
                              lambda kc: xt_half(kc, n)).then_inc(done, 1)
            for b in range(B):
                if b % 2 == 0:
                    pe.wait_ge(q0_ready, b // 2 + 1)
                last = mm_kc(PB[b // 2][0:S, (b % 2) * D:(b % 2 + 1) * D], lambda kc: xt[:, kc, b * S:(b + 1) * S],
                             lambda kc: w_l0[:, 2, kc, :])
                if b % 2:
                    last.then_inc(v0_mm, 1)
            pe.wait_ge(q0_ready, 4)
            pe.wait_ge(k0_ready, 4)
            for b in range(B):
                last = mm_kc(PB[4 + b // 4][0:S, (b % 4) * S:(b % 4 + 1) * S], lambda kc: k0[:, kc, b, :],
                             lambda kc: q0[:, kc, b, :])
                if b % 4 == 3:
                    last.then_inc(s0_mm, 1)
            pe.wait_ge(v0_ready, 4)
            for n in range(2):
                pe.wait_ge(a0_ready, n + 1)
                for j in range(KC):
                    bank = PB[(6, 0)[n] + j]
                    for b in range(4 * n, 4 * n + 4):
                        last = pe.matmul(bank[0:DC, (b % 4) * S:(b % 4 + 1) * S], v0[:, b, j * DC:(j + 1) * DC],
                                         a0[:, b, :], start=True, stop=True)
                    last.then_inc(o0_mm, 1)
            pe.wait_ge(o0_ready, 5)
            o0_cols = o0.rearrange("p j b s -> p j (b s)")
            for i in range(NT):
                lhs = o0_cols[:, :, 2 * S * i + 1:2 * S * i + 129] if i < 4 else o0_cls
                last = mm_kc(PB[2 + i // 2][0:rows(i), (i % 2) * D:(i % 2 + 1) * D],
                             lambda kc: lhs[:, kc, :], lambda kc: w_l0[:, 3, kc, :])
                if i % 2 or i == 4:
                    last.then_inc(y0_mm, 1)
            transpose_x(1)
            gate(1, w_gate0, E0)
            comb_turn(0, E0)
            clear_sums(0)
            wait_split_x(1)
            for run in RUNS[0]:
                ffn(run, E0)
            turn_back(0)
            transpose_x(2)
            wait_split_x(2)
            for j in range(6):
                for n in range(2):
                    g = 2 * j + n
                    if g >= 8:
                        pe.wait_ge(qkv_ready, g - 7)
                    for kc in range(KC):
                        for part, x in enumerate((xt_hi, xt_lo)):
                            mm = pe.matmul(PB[g % 8][0:DC, 0:HALF], w_qkv_t[:, kc, j * DC:(j + 1) * DC],
                                           x[:, kc, n * HALF:(n + 1) * HALF], start=kc + part == 0, stop=kc + part == 2)
                    mm.then_inc(qkv_mm, 1)
            statistics(0, stat_q[:].rearrange("p a j -> p (a j)"), 12, DC, 12)
            pe.wait_ge(v_int_ready, 1)
            pe.wait_ge(ident_ready, 1)
            for b in range(B):
                for kc in range(KC):
                    out = PB[b // 4][:, :].bitcast(BF16)[0:S, (b % 4) * D + kc * DC:(b % 4) * D + (kc + 1) * DC]
                    last = pe.transpose(out, qkv_int[:, 4 + kc, b, :], ident_bf[0:DC, 0:DC])
                if b % 4 == 3:
                    last.then_inc(v1_mm, 1)
            pe.wait_ge(qk_ready, 1)
            for i in range(4):
                for kc in range(KC):
                    g = 2 * i + kc
                    if g >= 6:
                        pe.wait_ge(sc_ready, g - 5)
                    bank = PB[2 + g % 6]
                    for b in (2 * i, 2 * i + 1):
                        lo = (b % 2) * PATCH
                        last = pe.matmul(bank[lo:lo + PATCH, 0:HC * S], qkv_int[:, kc, b, patch_at(b):patch_at(b) + PATCH],
                                         k_heads[:, kc, b, :, :], start=True, stop=True)
                    last.then_inc(sc_mm, 1)
            pe.wait_ge(sc_ready, 3)
            for b in range(B):
                lo = SLOT * (b % 4)
                last = mm_kc(PB[4][lo:lo + SLOT, (b // 4) * S:(b // 4 + 1) * S], lambda kc: q_cls[:, kc, b, :],
                             lambda kc: qkv_int[:, 2 + kc, b, :])
            last.then_inc(sc_mm, 1)
            pe.wait_ge(sc_ready, 9)
            statistics(1, stat_s[:], 2, 128, 2)
            for g in range(GROUPS):
                n = min(4, ROWS - 4 * g)
                pe.wait_ge(e_ready, 1 if 4 * g + n <= CHUNKS[0][1] else 2)
                if g >= 6:
                    pe.wait_ge(et_dve if g % 2 else et_act, (g - 6) // 2 + 1)
                for r in range(4 * g, 4 * g + n):
                    last = pe.transpose(PB[g % 6][0:S, (r % 4) * 128:(r % 4 + 1) * 128], sc[:, r, :], ident[:])
                last.then_inc(et_mm, 1)
            pe.wait_ge(v1_ready, 4)
            for i in range(4):
                for head in range(NH):
                    r = i * NH + head
                    pe.wait_ge(et_dve if (r // 4) % 2 else et_act, (r // 4) // 2 + 1)
                    for b in (2 * i, 2 * i + 1):
                        lo = (b % 2) * PATCH
                        at = (i % 2) * NH * (HD + 1) + head * (HD + 1)
                        last = pe.matmul(PB[6 + i // 2][lo:lo + PATCH, at:at + HD + 1], e_t[:, r, lo:lo + PATCH],
                                         v1[:, b, head, :], start=True, stop=True)
                if i % 2:
                    last.then_inc(pv_mm, 1)
            pe.wait_ge(et_act, 7)
            for b in range(B):
                for kc in range(KC):
                    at = (2 * b + kc) * NH
                    last = pe.matmul(PB[0][0:DC, at:at + NH], v1_flat[:, b, kc * DC:(kc + 1) * DC],
                                     e_t[:, 48 + b // 4, SLOT * (b % 4):SLOT * (b % 4) + NH], start=True, stop=True)
            last.then_inc(pvc_mm, 1)
            statistics(2, stat_o[:], 4, 128, 4)
            pe.wait_ge(o1_ready, 1)
            for i in range(4):
                for kc in range(KC):
                    at = (i % 2) * 256 + kc * 128
                    last = pe.transpose(PB[1 + i // 2][:, :].bitcast(BF16)[0:DC, at:at + 128],
                                        o1_int[:, i, kc * DC:(kc + 1) * DC], ident_bf[:])
                if i % 2:
                    last.then_inc(o1t_mm, 1)
            pe.wait_ge(o1t_ready, 2)
            pe.wait_ge(ocls_ready, 1)
            for i in range(NT):
                last = mm_kc(PB[3 + i // 2][0:rows(i), (i % 2) * D:(i % 2 + 1) * D],
                             lambda kc: tile_tokens(o1_t, kc, i), lambda kc: w_proj_t[:, kc, :])
                if i % 2 or i == 4:
                    last.then_inc(y1_mm, 1)
            statistics(3, stat_y[:], 4, 128, 4)
            transpose_x(3)
            gate(3, w_gate1, E1)
            comb_turn(1, E1)
            clear_sums(1)
            wait_split_x(3)
            for run in RUNS[1]:
                ffn(run, E1)
            turn_back(1)

        @block.scalar
        def _(act):
            def layernorm(r):
                act.wait_ge(mv_ready, r + 1)
                if r == 0:
                    act.wait_ge(eps_ready, 1)
                act.activation(std[:], mv[:, :, 1], ACT.Sqrt, bias=eps_c[:]).then_inc(std_ready, 1)
                act.wait_ge(xt_mm, NT * r + 2)
                for j in range(KC):
                    src = PB[0][0:DC, :].rearrange("p (i j q) -> p i j q", i=2, j=2)[:, :, j]
                    act.activation(xt_patches(r, j, 0), src, ACT.Copy).then_inc(xt_act, 1)
                act.wait_ge(xt_mm, NT * r + 5)
                for j in range(KC):
                    to = xt[:, j, 512:520].rearrange("p (i b) -> p i b", b=2) if r % 2 else cls_cols(xt[:, j, :])
                    act.activation(to, PB[2][0:DC, j * B:(j + 1) * B].rearrange("p (i b) -> p i b", b=2),
                                   ACT.Copy).then_inc(xt_act, 1)
                if r:
                    act.wait_ge(xt_act, 4 * (r + 1))
                    act.wait_ge(xt_dve, 2 * (r + 1))
                    for j in range(KC):
                        act.activation(xt_hi[:, j, :], xt[:, j, :], ACT.Copy).then_inc(xhi_ready, 1)

            def softmax_exp(r, n):
                act.wait_ge(soft_in, r + 1)
                act.activation(probs[:, :, 0:n], logits[:, :, 0:n], ACT.Exp).then_inc(soft_exp, 1)

            def ffn(run):
                y = run.layer

                def body(it):
                    for k, (kind, x) in enumerate(run.entries):
                        for n in range(2):
                            act.wait_ge(entry_mm[y], 2 * run.entry(it) + (2 * k + n + 1))
                            src, tok = PB[PAIRS[k % 2][n]][:, 0:HALF], slice(n * HALF, (n + 1) * HALF)
                            if kind == "w":
                                act.activation(tok_w_b[:, x % 2, tok], src, ACT.Identity).then_inc(entry_out[y], 1)
                            else:
                                act.activation(hid[:, x % 2, tok], src, ACT.Gelu_apprx_tanh).then_inc(entry_out[y], 1)
                        if k == 1:
                            x = 0
                        if kind == "h" and k or k == 1:
                            act.wait_ge(weighted[y], run.tile(it) + x + 1)
                            if x >= 2:
                                act.wait_ge(pj_mm[y], run.tile(it) + x)
                            act.activation(hid_hi[:, x % 2, :], hid_w[:, x % 2, :], ACT.Copy).then_inc(hid_hi_ready[y], 1)

                run_loop(act, run, body)

            def comb_turned(layer, n_exp):
                act.wait_ge(comb_mm, layer + 1)
                act.activation(comb_t[0:2 * n_exp, 0:512], PB[2][0:2 * n_exp, :], ACT.Copy).then_inc(comb_t_ready, 1)
                act.activation(comb_t[0:2 * n_exp, 512:520], PB[3][0:2 * n_exp, 0:B], ACT.Copy).then_inc(comb_t_ready, 1)

            def sums_out(layer):
                act.wait_ge(pj_mm[layer], 1 + (E0 * T0, 24)[layer])
                for c in range(KC):
                    act.activation(xt[:, c, 0:HALF], PB[SUMS[2 * c]][0:DC, 0:HALF], ACT.Copy).then_inc(sum_out, 1)

            for kc in range(KC):
                act.wait_ge(wint_t_mm, kc + 1)
                act.activation(w_qkv_t[:, kc, 0:4 * DC], PB[4 + kc][0:DC, 0:4 * DC], ACT.Copy).then_inc(wint_t_ready, 1)
            for kc in range(KC):
                act.wait_ge(wint_t_mm, kc + 3)
                act.activation(w_qkv_t[:, kc, 4 * DC:6 * DC], PB[6 + kc][0:DC, 0:2 * DC], ACT.Copy).then_inc(act_done, 1)
                act.activation(w_proj_t[:, kc, :], PB[6 + kc][0:DC, 2 * DC:4 * DC], ACT.Copy).then_inc(wint_t_ready, 1)
                act.activation(proj_scale[:, kc * DC:(kc + 1) * DC], PB[6 + kc][:, 4 * DC:5 * DC],
                               ACT.Copy).then_inc(wint_t_ready, 1)
            act.wait_ge(act_done, 2)
            layernorm(0)
            for j in range(KC):
                for n in range(2):
                    act.wait_ge(q0_mm, 2 * j + n + 1)
                    act.activation(half(q0, j, n), PB[2 * j + n][0:DC, 0:HALF].rearrange("p (b s) -> p b s", s=S),
                                   ACT.Copy, scale=0.1).then_inc(q0_ready, 1)
            for g in range(4):
                act.wait_ge(v0_mm, g + 1)
                act.activation(v0[:, 2 * g:2 * g + 2, :], PB[g][0:S, 0:2 * D].rearrange("p (b d) -> p b d", d=D),
                               ACT.Copy).then_inc(v0_ready, 1)
            for n in range(2):
                act.wait_ge(s0_mm, n + 1)
                act.activation(s0[:, 4 * n:4 * n + 4, :], PB[4 + n][0:S, 0:HALF].rearrange("p (b s) -> p b s", s=S),
                               ACT.Copy, scale=0.1).then_inc(s0_ready, 1)
            for n in range(2):
                for j in range(KC):
                    act.wait_ge(o0_mm, 2 * n + j + 1)
                    act.activation(half(o0, j, n), PB[(6, 0)[n] + j][0:DC, 0:HALF].rearrange("p (b s) -> p b s", s=S),
                                   ACT.Copy).then_inc(o0_ready, 1)
            act.wait_ge(o0_ready, 4)
            for j in range(KC):
                last = act.activation(o0_cls[:, j, :].rearrange("p (i b) -> p i b", b=2),
                                      cls_cols(o0[:, j].rearrange("p b s -> p (b s)")), ACT.Copy)
                if j == 0:
                    last.then_inc(act_done, 1)
            act.wait_ge(act_done, 3)
            last.then_inc(o0_ready, 1)
            layernorm(1)
            softmax_exp(0, E0)
            comb_turned(0, E0)
            for run in RUNS[0]:
                ffn(run)
            sums_out(0)
            layernorm(2)
            act.wait_ge(bq_in, 32)
            for j in range(6):
                for n in range(2):
                    g = 2 * j + n
                    act.wait_ge(qkv_mm, g + 1)
                    act.activation(half(qkv, j, n), PB[g % 8][0:DC, 0:HALF].rearrange("p (b s) -> p b s", s=S),
                                   ACT.Identity, scale=wq_scale[:, j:j + 1], bias=b_qkv[:, j:j + 1]).then_inc(qkv_ready, 1)
            for n in range(2):
                act.wait_ge(v1_mm, n + 1)
                act.wait_ge(v1_ones, 1)
                if n == 0:
                    act.wait_ge(w_lo_done[0], 3 * (E0 // 2 + 1))
                    act.wait_ge(w_lo_done[1], 3 * (E0 // 2))
                src = PB[n][:, :].bitcast(BF16)[0:S, 0:4 * D].rearrange("p (b h d) -> p b h d", b=4, h=NH)
                act.activation(v1[:, 4 * n:4 * n + 4, :, 0:HD], src, ACT.Copy).then_inc(v1_ready, 1)
                act.activation(v1_flat[:, 4 * n:4 * n + 4, :].rearrange("p b (h d) -> p b h d", h=NH), src,
                               ACT.Copy).then_inc(v1_ready, 1)
            for g in range(8):
                act.wait_ge(sc_mm, g + 1)
                act.activation(sc[:, HC * g:HC * (g + 1), :], PB[2 + g % 6][:, 0:HC * S].rearrange("p (h s) -> p h s", s=S),
                               ACT.Copy).then_inc(sc_ready, 1)
            act.wait_ge(sc_mm, 9)
            act.activation(sc[:, 48:50, :], PB[4][:, 0:2 * S].rearrange("p (h s) -> p h s", s=S),
                           ACT.Copy).then_inc(sc_ready, 1)
            for n, (a, z) in enumerate(CHUNKS):
                act.wait_ge(x_ready, n + 1)
                act.activation(qexp[:, a:z, :], sc[:, a:z, :], ACT.Identity, scale=col("inv_x0"),
                               bias=col("floor_shift")).then_inc(y_ready, 1)
            for n, (a, z) in enumerate(CHUNKS):
                act.wait_ge(qexp_ready, n + 1)
                act.activation(pow2[:, a:z, :], qexp[:, a:z, :], ACT.Exp, scale=-LN2).then_inc(pow2_ready, 1)
                act.wait_ge(rem_ready, n + 1)
                act.activation(sc[:, a:z, :], rem[:, a:z, :], ACT.Square, bias=col("neg_half_b")).then_inc(sq_ready, 1)
            for g in range(0, GROUPS, 2):
                n = min(4, ROWS - 4 * g)
                act.wait_ge(et_mm, g + 1)
                act.activation(e_t[:, 4 * g:4 * g + n, :], PB[g % 6][0:S, 0:n * 128].rearrange("p (r q) -> p r q", q=128),
                               ACT.Copy).then_inc(et_act, 1)
            for g in range(2):
                act.wait_ge(o1t_mm, g + 1)
                src = PB[1 + g][:, :].bitcast(BF16)[0:DC, 0:512].rearrange("p (i j q) -> p i j q", i=2, j=2)
                for kc in range(KC):
                    last = act.activation(o1_t[:, kc, 256 * g:256 * (g + 1)].rearrange("p (i q) -> p i q", i=2),
                                          src[:, :, kc], ACT.Copy)
                    if kc == 0:
                        last.then_inc(act_done, 1)
                act.wait_ge(act_done, 4 + g)
                last.then_inc(o1t_ready, 1)
            layernorm(3)
            softmax_exp(1, E1)
            comb_turned(1, E1)
            for run in RUNS[1]:
                ffn(run)
            sums_out(1)

        @block.vector
        def _(dve):
            steps = [0]

            def then(ins):
                steps[0] += 1
                ins.then_inc(dve_done, 1)
                dve.wait_ge(dve_done, steps[0])

            def settle(ins):
                steps[0] += 1
                ins.then_inc(dve_done, 1)

            def layernorm(r):
                for i in range(NT):
                    settle(dve.bn_stats(bn6[0:rows(i), i, :], h[0:rows(i), i, :]))
                dve.wait_ge(dve_done, steps[0])
                for i in range(NT):
                    last = dve.bn_aggr(mv[0:rows(i), i, :], bn6[0:rows(i), i, :])
                    if i < NT - 1:
                        settle(last)
                dve.wait_ge(dve_done, steps[0])
                last.then_inc(mv_ready, 1)
                dve.wait_ge(mv_ready, r + 1)
                then(dve.tensor_scalar(var_eps[:], mv[:, :, 1], EPS, None, ALU.add))
                dve.wait_ge(std_ready, r + 1)
                then(dve.reciprocal(rstd[:], std[:]))
                then(dve.tensor_tensor(newton[:], rstd[:], rstd[:], ALU.mult))
                then(dve.tensor_tensor(newton[:], newton[:], var_eps[:], ALU.mult))
                then(dve.tensor_scalar(newton[:], newton[:], -0.5, 1.5, ALU.mult, ALU.add))
                then(dve.tensor_tensor(rstd[:], rstd[:], newton[:], ALU.mult))
                for i in range(NT):
                    n = rows(i)
                    dve.tensor_scalar(xn[0:n, i, :], h[0:n, i, :], mv[0:n, i, 0:1], rstd[0:n, i:i + 1],
                                      ALU.subtract, ALU.mult).then_inc(xn_ready, 1)
                dve.wait_ge(xt_mm, NT * r + 4)
                for j in range(KC):
                    src = PB[1][0:DC, :].rearrange("p (i j q) -> p i j q", i=2, j=2)[:, :, j]
                    dve.tensor_copy(xt_patches(r, j, 2), src).then_inc(xt_dve, 1)

            def split_x(r):
                for j in range(KC):
                    dve.wait_ge(xhi_ready, 2 * (r - 1) + j + 1)
                    dve.tensor_tensor(xt_lo[:, j, :], xt[:, j, :], xt_hi[:, j, :].bitcast(F32),
                                      ALU.subtract).then_inc(xlo_ready, 1)

            def softmax(r, n):
                dve.wait_ge(gate_mm, r + 1)
                settle(dve.tensor_copy(logits[:, 0:4, 0:n], PB[3][:, 0:4 * n].rearrange("p (i e) -> p i e", e=n)))
                then(dve.tensor_copy(logits[0:B, 4, 0:n], PB[3][0:B, 4 * n:5 * n]))
                split_x(2 * r + 1)
                lg, pr = logits[:, :, 0:n], probs[:, :, 0:n]
                then(dve.tensor_reduce(rmax[:], lg, X, ALU.max))
                dve.tensor_tensor(lg, lg, rmax[:].unsqueeze(2).broadcast_to([128, NT, n]), ALU.subtract).then_inc(soft_in, 1)
                dve.wait_ge(soft_exp, r + 1)
                then(dve.tensor_reduce(rsum[:], pr, X, ALU.add))
                then(dve.reciprocal(rinv[:], rsum[:]))
                then(dve.tensor_tensor(pr, pr, rinv[:].unsqueeze(2).broadcast_to([128, NT, n]), ALU.mult))

            def combine(out, n):
                pr, ch = probs[:, :, 0:n], chosen[:, :, 0:n]
                then(dve.tensor_tensor(ch, ch, pr, ALU.mult))
                then(dve.tensor_reduce(rsum[:], ch, X, ALU.add))
                then(dve.reciprocal(rinv[:], rsum[:]))
                then(dve.tensor_tensor(out[:], ch, rinv[:].unsqueeze(2).broadcast_to([128, NT, n]), ALU.mult))
                then(dve.tensor_copy(comb_r[:, :, 0:n], out[:]))
                dve.tensor_tensor(comb_r[:, :, n:2 * n], out[:], comb_r[:, :, 0:n].bitcast(F32),
                                  ALU.subtract).then_inc(comb_ready, 1)

            def pick(layer, n_exp, e):
                src, cols = comb_t[0:2 * n_exp, :], (pick0, pick1)[layer]
                w = cols[:, e:e + 1] if isinstance(e, int) else cols[:, bass.ds(e, 1)]
                return dve.tensor_scalar(one_expert[0:2 * n_exp, e_slot[0], :], src, w, None, ALU.mult)

            e_slot = [0]

            def split_hi(s, piece, w, n):
                if piece == 0:
                    dve.wait_ge(raw_in[s], 32 * n)
                if piece < 2:
                    ins = dve.tensor_copy(fc_hi[:, s, piece, 0:w * HT], fc_raw[:, s, piece, 0:w * HT])
                else:
                    ins = dve.tensor_copy(pj_hi[:, s, 0:w, :], pj_raw[:, s, 0:w, :])
                ins.then_inc(w_hi_done[s], 1)

            def ffn(run, n_exp, final=False):
                y = run.layer

                def body(it):
                    for k, (kind, x) in enumerate(run.entries):
                        if kind == "w":
                            continue
                        e, s, j = x // run.per, x // run.unit, x % run.unit
                        dve.wait_ge(entry_out[y], 2 * run.entry(it) + 2 * max(k + 1, 2))
                        dve.tensor_tensor(hid_w[:, x % 2, :], hid[:, x % 2, :], tok_w_b[:, e % 2, :],
                                          ALU.mult).then_inc(weighted[y], 1)
                        dve.wait_ge(hid_hi_ready[y], run.tile(it) + x + 1)
                        dve.tensor_tensor(hid_lo[:, x % 2, :], hid_w[:, x % 2, :], hid_hi[:, x % 2, :].bitcast(F32),
                                          ALU.subtract).then_inc(hid_lo_ready[y], 1)
                        if x % run.per == 0:
                            e_slot[0] = e % 2
                            pick(y, n_exp, run.expert(it) + (e + 2)).then_inc(picked[y], 1)
                        if j <= 1 and not (final and s == 1):
                            if j == 0:
                                dve.wait_ge(pj_mm[y], run.tile(it) + (run.unit * s + 1))
                            for piece in ((0, 1), (2,))[j]:
                                split_hi(1 - s, piece, run.width, it + (run.load0 + 1 + s))

                run_loop(dve, run, body)

            def start_picks(layer, n_exp):
                dve.wait_ge(comb_t_ready, 2 * (layer + 1))
                for e in range(2):
                    e_slot[0] = e
                    pick(layer, n_exp, e).then_inc(picked[layer], 1)

            def add_sums(layer):
                dve.wait_ge(pj_mm[layer], 1 + (E0 * T0, 24)[layer])
                for c in range(KC):
                    dve.tensor_copy(xt[:, c, HALF:2 * HALF], PB[SUMS[2 * c + 1]][0:DC, 0:HALF]).then_inc(sum_out, 1)
                for g in range(3):
                    dve.wait_ge(back_mm, 3 * layer + g + 1)
                    n, w = (128, 2) if g < 2 else (B, 1)
                    hh = h[0:n, 2 * g:2 * g + w, :]
                    dve.tensor_tensor(hh, hh, PB[(0, 1, 6)[g]][0:n, 0:w * D].rearrange("p (i d) -> p i d", d=D),
                                      ALU.add).then_inc(h_done, 1)
                dve.wait_ge(h_done, 3 * (layer + 1))

            def statistics(r, n, p, out):
                dve.wait_ge(stat_t, r + 1)
                dve.tensor_reduce(red[0:n, r:r + 1], PB[6][0:n, 0:p], X, ALU.max).then_inc(red_ready, 1)
                dve.wait_ge(stat_b, r + 1)
                then(dve.tensor_copy(out, PB[7][:, 0:n]))

            def scale_of(name, top, negmin, factor=None):
                then(dve.tensor_tensor(col(name), top, negmin, ALU.add))
                if factor is not None:
                    then(dve.tensor_tensor(col(name), col(name), factor, ALU.mult))
                then(dve.tensor_scalar(col(name), col(name), 1.0 / QMAX, SMIN, ALU.mult, ALU.max))
                then(dve.reciprocal(col(name + "_inv"), col(name)))

            def zero_of(name, negmin, inv):
                then(dve.tensor_tensor(col(name + "_z"), negmin, inv, ALU.mult))
                then(dve.tensor_scalar(col(name + "_z"), col(name + "_z"), MAGIC, None, ALU.add))
                then(dve.tensor_scalar(col(name + "_lo"), col(name + "_z"), -1.0, 2 * MAGIC, ALU.mult, ALU.add))
                then(dve.tensor_scalar(col(name + "_hi"), col(name + "_lo"), QMAX, None, ALU.add))

            for name in ("s1", "s1_inv", "s1_z", "s1_lo", "s1_hi", "gmax", "gneg", "qk", "alpha", "sa", "sa_inv",
                         "sa_z", "sa_lo", "sa_hi", "ceil_t", "ceil_r", "x0", "inv_x0", "x0_30", "neg_x0", "floor_shift",
                         "neg_half_b", "b_t", "b_r", "c_t", "c_r", "half_b2", "poly_c", "so", "so_inv", "so_z", "so_lo",
                         "so_hi", "alpha_o", "omax", "oneg", "sy", "sy_inv", "sy_z", "sy_lo", "sy_hi", "ymax", "yneg"):
                col(name)
            for name in ("s2", "s2_inv", "s2_z", "s2_lo", "s2_hi"):
                col(name, 3)

            settle(dve.memset(mv[:], 1.0))
            settle(dve.memset(logits[:], 0.0))
            settle(dve.memset(ones_f[:], 1.0))
            settle(dve.memset(zeros[:], 0.0))
            settle(dve.memset(stat_o[:], -3.0e38))
            settle(dve.memset(stat_y[:], -3.0e38))
            dve.memset(eps_c[:], EPS).then_inc(eps_ready, 1)
            dve.wait_ge(consts_in, 64)
            dve.tensor_copy(ident_bf[:], ident[:]).then_inc(ident_ready, 1)
            dve.wait_ge(dve_done, steps[0])
            settle(dve.tensor_copy(ones_r[:], ones_f[:]))
            dve.wait_ge(wq_in, 32)
            then(dve.tensor_reduce(wq_amax[:], wq_raw[:], X, ALU.max, apply_absolute_value=True))
            then(dve.tensor_scalar(wq_scale[:], wq_amax[:], 1.0 / 127.0, SMIN, ALU.mult, ALU.max))
            then(dve.reciprocal(wq_inv[:], wq_scale[:]))
            then(dve.tensor_tensor(wq_int[:], wq_raw[:], wq_inv[:].unsqueeze(2).broadcast_to([DC, 8, D]), ALU.mult))
            then(dve.tensor_scalar(wq_int[:], wq_int[:], MAGIC, MAGIC, ALU.add, ALU.subtract))
            dve.tensor_scalar(wq_int[:], wq_int[:], -128.0, 127.0, ALU.max, ALU.min).then_inc(wint_ready, 1)
            for piece in range(3):
                split_hi(0, piece, T0, 1)
            dve.wait_ge(bias_in, 32)
            for i in range(4):
                dve.wait_ge(tok_mm, i + 1)
                settle(dve.tensor_tensor(h[:, i, :], PB[i][:, 0:D], tok_bias[:], ALU.add))
            dve.wait_ge(dve_done, steps[0])
            layernorm(0)
            for j in range(KC):
                for n in range(2):
                    dve.wait_ge(k0_mm, 2 * j + n + 1)
                    dve.tensor_scalar(half(k0, j, n), PB[4 + 2 * j + n][0:DC, 0:HALF].rearrange("p (b s) -> p b s", s=S),
                                      0.1, None, ALU.mult).then_inc(k0_ready, 1)
            for n in range(2):
                dve.wait_ge(s0_ready, n + 1)
                s = s0[:, 4 * n:4 * n + 4, :]
                dve.scalar_tensor_tensor(a0[:, 4 * n:4 * n + 4, :], s, 1.0, s, ALU.add, ALU.mult).then_inc(a0_ready, 1)
            for g in range(3):
                dve.wait_ge(y0_mm, g + 1)
                n, w = (128, 2) if g < 2 else (B, 1)
                hh = h[0:n, 2 * g:2 * g + w, :]
                settle(dve.scalar_tensor_tensor(hh, PB[2 + g][0:n, 0:w * D].rearrange("p (i d) -> p i d", d=D), 0.1, hh,
                                                ALU.mult, ALU.add))
            dve.wait_ge(dve_done, steps[0])
            layernorm(1)
            softmax(0, E0)
            for i in range(NT):
                pf = probs[:, i, 0:E0].unsqueeze(1).broadcast_to([128, E0, E0])
                pe_ = probs[:, i, 0:E0].unsqueeze(2).broadcast_to([128, E0, E0])
                settle(dve.tensor_tensor(cmp_a[:], pf, pe_, ALU.is_gt))
                then(dve.tensor_tensor(cmp_b[:], pf, pe_, ALU.is_equal))
                then(dve.tensor_tensor(cmp_b[:], cmp_b[:], before[:], ALU.mult))
                then(dve.tensor_tensor(cmp_a[:], cmp_a[:], cmp_b[:], ALU.add))
                then(dve.tensor_reduce(rank[:, i, :], cmp_a[:], X, ALU.add))
            then(dve.tensor_scalar(chosen[:, :, 0:E0], rank[:], 1.5, None, ALU.is_lt))
            combine(comb0, E0)
            start_picks(0, E0)
            for run in RUNS[0]:
                ffn(run, E0)
            add_sums(0)

            layernorm(2)
            split_x(2)
            dve.memset(v1[:], 1.0).then_inc(v1_ones, 1)
            for j in range(6):
                dve.wait_ge(qkv_ready, 2 * j + 2)
                settle(dve.tensor_reduce(stat_q[:, 0, j:j + 1], qkv[:, j], XY, ALU.max))
                last = dve.tensor_reduce(stat_q[:, 1, j:j + 1], qkv[:, j], XY, ALU.min, negate=True)
                if j < 5:
                    settle(last)
            dve.wait_ge(dve_done, steps[0])
            last.then_inc(stat_ready, 1)
            statistics(0, 12, DC, g_q[:])
            then(dve.tensor_reduce(ext[:], g_q[:].rearrange("p (a j) -> p a j", j=2), X, ALU.max))
            settle(dve.tensor_reduce(col("gmax"), ext[:, 0:3], X, ALU.max))
            then(dve.tensor_reduce(col("gneg"), ext[:, 3:6], X, ALU.max))
            scale_of("s1", col("gmax"), col("gneg"))
            zero_of("s1", col("gneg"), col("s1_inv"))
            then(dve.tensor_scalar(ext[:, 3:6], ext[:, 3:6], -1.0, None, ALU.mult))
            then(dve.tensor_scalar(ext_t[:], ext[:], col("s1_inv"), MAGIC, ALU.mult, ALU.add))
            then(dve.tensor_scalar(ext_c[:], ext_t[:], col("s1_lo"), col("s1_hi"), ALU.max, ALU.min))
            then(dve.tensor_scalar(ext_q[:], ext_c[:], MAGIC, col("s1"), ALU.subtract, ALU.mult))
            s2, s2i = col("s2"), col("s2_inv")
            then(dve.tensor_tensor(s2, ext_q[:, 0:3], ext_q[:, 3:6], ALU.subtract))
            then(dve.tensor_scalar(s2, s2, 1.0 / QMAX, SMIN, ALU.mult, ALU.max))
            then(dve.reciprocal(s2i, s2))
            then(dve.tensor_tensor(col("s2_z"), ext_q[:, 3:6], s2i, ALU.mult))
            then(dve.tensor_scalar(col("s2_z"), col("s2_z"), -1.0, MAGIC, ALU.mult, ALU.add))
            then(dve.tensor_scalar(col("s2_lo"), col("s2_z"), -1.0, 2 * MAGIC, ALU.mult, ALU.add))
            then(dve.tensor_scalar(col("s2_hi"), col("s2_lo"), QMAX, None, ALU.add))
            for part in (2, 0, 1):
                z = qkv[:, 2 * part:2 * part + 2]
                then(dve.tensor_scalar(z, z, colp("s1_inv", DC), MAGIC, ALU.mult, ALU.add))
                then(dve.tensor_scalar(z, z, colp("s1_lo", DC), colp("s1_hi", DC), ALU.max, ALU.min))
                then(dve.tensor_scalar(z, z, MAGIC, colp("s1", DC), ALU.subtract, ALU.mult))
                then(dve.tensor_scalar(z, z, colp("s2_inv", DC, part), MAGIC, ALU.mult, ALU.add))
                then(dve.tensor_scalar(z, z, colp("s2_lo", DC, part), colp("s2_hi", DC, part), ALU.max, ALU.min))
                last = dve.tensor_scalar(qkv_int[:, 2 * part:2 * part + 2], z, MAGIC, None, ALU.subtract)
                if part == 2:
                    last.then_inc(v_int_ready, 1)
                else:
                    then(last)
            for kc in range(KC):
                q = cls_cols(qkv_int[:, kc].rearrange("p b s -> p (b s)")).unsqueeze(3).broadcast_to([DC, 4, 2, SLOT])
                own = cls_mask[:, kc, :].unsqueeze(1).unsqueeze(1).broadcast_to([DC, 4, 2, SLOT])
                settle(dve.tensor_tensor(q_cls[:, kc].rearrange("p (i b) m -> p i b m", b=2), q, own, ALU.mult))
            for head in range(HC):
                last = dve.tensor_scalar(k_heads[:, :, :, head, :], qkv_int[:, 2:4], head_mask[:, head:head + 1], None,
                                         ALU.mult)
                if head < HC - 1:
                    settle(last)
            dve.wait_ge(dve_done, steps[0])
            last.then_inc(qk_ready, 1)
            for g in range(9):
                a, z = (HC * g, HC * g + HC) if g < 8 else (48, 50)
                dve.wait_ge(sc_ready, g + 1)
                settle(dve.tensor_reduce(row_hi[:, a:z], sc[:, a:z, :], X, ALU.max))
                settle(dve.tensor_reduce(row_lo[:, a:z], sc[:, a:z, :], X, ALU.min, negate=True))
            dve.wait_ge(dve_done, steps[0])
            then(dve.tensor_reduce(stat_s[:, 0:1], row_hi[:], X, ALU.max))
            dve.tensor_reduce(stat_s[:, 1:2], row_lo[:], X, ALU.max).then_inc(stat_ready, 1)
            statistics(1, 2, 128, g_s[:])
            then(dve.tensor_tensor(col("qk"), c[:, columns["s2"][0]:columns["s2"][0] + 1],
                                   c[:, columns["s2"][0] + 1:columns["s2"][0] + 2], ALU.mult))
            then(dve.tensor_scalar(col("qk"), col("qk"), float(HD) ** -0.5, None, ALU.mult))
            scale_of("sa", g_s[:, 0:1], g_s[:, 1:2], col("qk"))
            then(dve.tensor_tensor(col("alpha"), col("qk"), col("sa_inv"), ALU.mult))
            zero_of("sa", g_s[:, 1:2], col("alpha"))
            then(dve.tensor_scalar(col("ceil_t"), col("sa_inv"), LN2, None, ALU.mult))
            then(dve.tensor_scalar(col("ceil_r"), col("ceil_t"), MAGIC, MAGIC, ALU.add, ALU.subtract))
            then(dve.tensor_tensor(col("x0"), col("ceil_t"), col("ceil_r"), ALU.is_gt))
            then(dve.tensor_tensor(col("x0"), col("x0"), col("ceil_r"), ALU.add))
            then(dve.reciprocal(col("inv_x0"), col("x0")))
            settle(dve.tensor_scalar(col("floor_shift"), col("inv_x0"), 0.5, -0.5, ALU.mult, ALU.add))
            settle(dve.tensor_scalar(col("x0_30"), col("x0"), float(N_EXP), None, ALU.mult))
            settle(dve.tensor_scalar(col("neg_x0"), col("x0"), -1.0, None, ALU.mult))
            then(dve.tensor_scalar(col("b_t"), col("sa_inv"), EXP_B / EXP_A, None, ALU.mult))
            then(dve.tensor_scalar(col("b_r"), col("b_t"), MAGIC, MAGIC, ALU.add, ALU.subtract))
            then(dve.tensor_tensor(col("b_t"), col("b_r"), col("b_t"), ALU.is_gt))
            then(dve.tensor_tensor(col("b_r"), col("b_r"), col("b_t"), ALU.subtract))
            then(dve.tensor_tensor(col("c_t"), col("sa_inv"), col("sa_inv"), ALU.mult))
            then(dve.tensor_scalar(col("c_t"), col("c_t"), EXP_C / EXP_A, None, ALU.mult))
            then(dve.tensor_scalar(col("c_r"), col("c_t"), MAGIC, MAGIC, ALU.add, ALU.subtract))
            then(dve.tensor_tensor(col("c_t"), col("c_r"), col("c_t"), ALU.is_gt))
            then(dve.tensor_tensor(col("c_r"), col("c_r"), col("c_t"), ALU.subtract))
            then(dve.tensor_scalar(col("neg_half_b"), col("b_r"), -0.5, None, ALU.mult))
            then(dve.tensor_tensor(col("half_b2"), col("neg_half_b"), col("neg_half_b"), ALU.mult))
            then(dve.tensor_tensor(col("poly_c"), col("c_r"), col("half_b2"), ALU.subtract))
            then(dve.tensor_scalar(row_hi[:], row_hi[:], col("alpha"), MAGIC, ALU.mult, ALU.add))
            then(dve.tensor_scalar(row_hi[:], row_hi[:], col("sa_lo"), col("sa_hi"), ALU.max, ALU.min))
            for n, (a, z) in enumerate(CHUNKS):
                s = sc[:, a:z, :]
                top = row_hi[:, a:z].unsqueeze(2).broadcast_to([128, z - a, S])
                then(dve.tensor_scalar(s, s, col("alpha"), MAGIC, ALU.mult, ALU.add))
                then(dve.tensor_scalar(s, s, col("sa_lo"), col("sa_hi"), ALU.max, ALU.min))
                then(dve.tensor_tensor(s, top, s, ALU.subtract))
                dve.tensor_scalar(s, s, col("x0_30"), None, ALU.min).then_inc(x_ready, 1)
            for n, (a, z) in enumerate(CHUNKS):
                q = qexp[:, a:z, :]
                dve.wait_ge(y_ready, n + 1)
                dve.tensor_scalar(q, q, MAGIC, MAGIC, ALU.add, ALU.subtract).then_inc(qexp_ready, 1)
                dve.wait_ge(qexp_ready, n + 1)
                dve.scalar_tensor_tensor(rem[:, a:z, :], q, col("neg_x0"), sc[:, a:z, :], ALU.mult,
                                         ALU.add).then_inc(rem_ready, 1)
            for n, (a, z) in enumerate(CHUNKS):
                dve.wait_ge(sq_ready, n + 1)
                last = dve.scalar_tensor_tensor(sc[:, a:z, :], sc[:, a:z, :], col("poly_c"), pow2[:, a:z, :],
                                                ALU.add, ALU.mult)
                if n == 0:
                    last.then_inc(e_ready, 1)
            then(last)
            then(dve.tensor_reduce(cls_sum[:], sc[:, 48:50, :], X, ALU.add))
            then(dve.reciprocal(cls_sum[:], cls_sum[:]))
            dve.tensor_tensor(sc[:, 48:50, :], sc[:, 48:50, :], cls_sum[:].unsqueeze(2).broadcast_to([128, 2, S]),
                              ALU.mult).then_inc(e_ready, 1)
            for g in range(1, GROUPS, 2):
                n = min(4, ROWS - 4 * g)
                dve.wait_ge(et_mm, g + 1)
                dve.tensor_copy(e_t[:, 4 * g:4 * g + n, :],
                                PB[g % 6][0:S, 0:n * 128].rearrange("p (r q) -> p r q", q=128)).then_inc(et_dve, 1)
            for g in range(2):
                dve.wait_ge(pv_mm, g + 1)
                acc = PB[6 + g][:, 0:2 * NH * (HD + 1)].rearrange("p (i h d) -> p i h d", i=2, h=NH)
                inv = o_inv[:, 2 * g:2 * g + 2, :]
                then(dve.reciprocal(inv, acc[:, :, :, HD]))
                then(dve.tensor_tensor(o1[:, 2 * g:2 * g + 2], acc[:, :, :, 0:HD],
                                       inv.unsqueeze(3).broadcast_to([128, 2, NH, HD]), ALU.mult))
            dve.wait_ge(pvc_mm, 1)
            ocm = o_cls_m[:].rearrange("p (b j) h -> p b j h", j=KC)
            src = PB[0][0:DC, 0:B * KC * NH].rearrange("p (b j h) -> p b j h", b=B, j=KC)
            own = cls_mask[:, :, 0:NH].unsqueeze(1).broadcast_to([DC, B, KC, NH])
            then(dve.tensor_tensor(ocm, src, own, ALU.mult))
            then(dve.tensor_reduce(o_cls[:], o_cls_m[:], X, ALU.add))
            flat = o1[:].rearrange("p i h d -> p (i h d)")
            settle(dve.tensor_reduce(stat_o[:, 0:1], flat, X, ALU.max))
            settle(dve.tensor_reduce(stat_o[:, 1:2], flat, X, ALU.min, negate=True))
            settle(dve.tensor_reduce(stat_o[0:DC, 2:3], o_cls[:], X, ALU.max))
            last = dve.tensor_reduce(stat_o[0:DC, 3:4], o_cls[:], X, ALU.min, negate=True)
            dve.wait_ge(dve_done, steps[0])
            last.then_inc(stat_ready, 1)
            statistics(2, 4, 128, g_o[:])
            settle(dve.tensor_tensor(col("omax"), g_o[:, 0:1], g_o[:, 2:3], ALU.max))
            then(dve.tensor_tensor(col("oneg"), g_o[:, 1:2], g_o[:, 3:4], ALU.max))
            sv = c[:, columns["s2"][0] + 2:columns["s2"][0] + 3]
            scale_of("so", col("omax"), col("oneg"), sv)
            then(dve.tensor_tensor(col("alpha_o"), sv, col("so_inv"), ALU.mult))
            zero_of("so", col("oneg"), col("alpha_o"))
            then(dve.tensor_scalar(flat, flat, col("alpha_o"), MAGIC, ALU.mult, ALU.add))
            then(dve.tensor_scalar(flat, flat, col("so_lo"), col("so_hi"), ALU.max, ALU.min))
            dve.tensor_scalar(o1_int[:].rearrange("p i f -> p (i f)"), flat, MAGIC, None, ALU.subtract).then_inc(o1_ready, 1)
            then(dve.tensor_scalar(o_cls[:], o_cls[:], colp("alpha_o", DC), MAGIC, ALU.mult, ALU.add))
            then(dve.tensor_scalar(o_cls[:], o_cls[:], colp("so_lo", DC), colp("so_hi", DC), ALU.max, ALU.min))
            dve.tensor_scalar(o1_t[:, :, 512:520].rearrange("p j b -> p b j"),
                              o_cls[:].rearrange("p (b j) -> p b j", j=KC), MAGIC, None, ALU.subtract).then_inc(ocls_ready, 1)
            dve.wait_ge(wint_t_ready, 6)
            then(dve.tensor_scalar(proj_scale[:], proj_scale[:], col("so"), None, ALU.mult))
            dve.wait_ge(bq_in, 32)
            for g in range(3):
                dve.wait_ge(y1_mm, g + 1)
                n, w = (128, 2) if g < 2 else (B, 1)
                yy = y1[0:n, 2 * g:2 * g + w, :]
                then(dve.tensor_tensor(yy, PB[3 + g][0:n, 0:w * D].rearrange("p (i d) -> p i d", d=D),
                                       proj_scale[0:n, :].unsqueeze(1).broadcast_to([n, w, D]), ALU.mult))
                then(dve.tensor_tensor(yy, yy, b_proj[0:n, :].unsqueeze(1).broadcast_to([n, w, D]), ALU.add))
            patch_y, cls_y = y1[:, 0:4, :], y1[0:B, 4, :]
            settle(dve.tensor_reduce(stat_y[:, 0:1], patch_y, XY, ALU.max))
            settle(dve.tensor_reduce(stat_y[:, 1:2], patch_y, XY, ALU.min, negate=True))
            settle(dve.tensor_reduce(stat_y[0:B, 2:3], cls_y, X, ALU.max))
            last = dve.tensor_reduce(stat_y[0:B, 3:4], cls_y, X, ALU.min, negate=True)
            dve.wait_ge(dve_done, steps[0])
            last.then_inc(stat_ready, 1)
            statistics(3, 4, 128, g_y[:])
            settle(dve.tensor_tensor(col("ymax"), g_y[:, 0:1], g_y[:, 2:3], ALU.max))
            then(dve.tensor_tensor(col("yneg"), g_y[:, 1:2], g_y[:, 3:4], ALU.max))
            scale_of("sy", col("ymax"), col("yneg"))
            zero_of("sy", col("yneg"), col("sy_inv"))
            for p, y, hh in ((128, patch_y, h[:, 0:4, :]), (B, cls_y, h[0:B, 4, :])):
                then(dve.tensor_scalar(y, y, colp("sy_inv", p), MAGIC, ALU.mult, ALU.add))
                then(dve.tensor_scalar(y, y, colp("sy_lo", p), colp("sy_hi", p), ALU.max, ALU.min))
                then(dve.tensor_scalar(y, y, MAGIC, colp("sy", p), ALU.subtract, ALU.mult))
                then(dve.tensor_tensor(hh, hh, y, ALU.add))
            layernorm(3)
            softmax(1, E1)
            for i in range(NT):
                then(dve.max(top8[:, i, :], probs[:, i, :]))
                then(dve.match_replace(left[:, i, :], top8[:, i, :], probs[:, i, :], -1.0))
            then(dve.tensor_scalar(chosen[:], left[:], 0.0, None, ALU.is_lt))
            combine(comb1, E1)
            start_picks(1, E1)
            for run in RUNS[1]:
                ffn(run, E1, final=run is RUNS[1][-1])
            add_sums(1)


def lay_out(np, x, cls_tok, L0_tok_w, L0_tok_b, L0_attn_Wq, L0_attn_Wk, L0_attn_Wv, L0_attn_Wo, L0_ffn_w_fc,
            L0_ffn_w_proj, L0_ffn_w_gate, L1_attn_w_qkv, L1_attn_b_qkv, L1_attn_w_proj, L1_attn_b_proj,
            L1_ffn_router_w, L1_ffn_w1, L1_ffn_w2):
    def chunks(w):
        return w.reshape(KC, DC, -1).transpose(1, 0, 2)

    feature = np.arange(DC) // HD
    column = np.arange(SLOT) % NH
    a = {
        "patches": x.reshape(B, 8, 32, 8, 32).transpose(2, 4, 0, 1, 3).reshape(TOKK, 128, B * PATCH),
        "w_tok": L0_tok_w.T.reshape(TOKK, 128, D),
        "tok_bias": L0_tok_b,
        "cls_tok": cls_tok.reshape(D),
        "w_l0": np.stack([chunks(w.T) for w in (L0_attn_Wq, L0_attn_Wk, L0_attn_Wv, L0_attn_Wo)], axis=1),
        "w_gate0": chunks(L0_ffn_w_gate),
        "w_gate1": chunks(L1_ffn_router_w.T),
        "fc0": L0_ffn_w_fc.reshape(KC, DC, T0 * 128, E0).transpose(3, 1, 0, 2),
        "pj0": L0_ffn_w_proj.reshape(T0, 128, D, E0).transpose(3, 1, 0, 2),
        "w_qkv": L1_attn_w_qkv.reshape(6, DC, D).transpose(1, 0, 2),
        "w_proj": L1_attn_w_proj.reshape(KC, DC, D).transpose(1, 0, 2),
        "b_qkv": L1_attn_b_qkv.reshape(6, DC).T,
        "b_proj": L1_attn_b_proj,
        "fc1": L1_ffn_w1.reshape(KC, DC, 6, 512).transpose(2, 1, 0, 3),
        "pj1": L1_ffn_w2.reshape(6, 4, 128, D).transpose(0, 2, 1, 3),
        "pick0": np.eye(E0, E0 + 2, dtype=np.float32)[np.arange(2 * E0) % E0],
        "pick1": np.eye(E1, E1 + 2, dtype=np.float32)[np.arange(2 * E1) % E1],
        "ident": np.eye(128, dtype=np.float32),
        "head_mask": (feature[:, None] == np.arange(HC)).astype(np.float32),
        "cls_mask": (feature[:, None, None] + HC * np.arange(KC)[:, None] == column).astype(np.float32),
        "before": np.broadcast_to(np.arange(E0) < np.arange(E0)[:, None], (128, E0, E0)).astype(np.float32),
    }
    return {k: np.ascontiguousarray(v) for k, v in a.items()}


def kernel(**inputs):
    import numpy as np
    import concourse.bacc as bacc
    from concourse.bass_utils import run_bass_kernel_spmd

    arrays = lay_out(np, **{k: np.asarray(v) for k, v in inputs.items()})
    nc = bacc.Bacc("TRN2", target_bir_lowering=False, num_devices=1)
    t = {k: nc.dram_tensor(k + "_dram", v.shape, mybir.dt.from_np(v.dtype), kind="ExternalInput").ap()
         for k, v in arrays.items()}
    t["out"] = nc.dram_tensor("out_dram", (B, S, D), F32, kind="ExternalOutput").ap()
    build(nc, t)
    r = run_bass_kernel_spmd(nc, [{k + "_dram": v for k, v in arrays.items()}], core_ids=[0])
    return r.results[0]["out_dram"]
```

```python
from contextlib import ExitStack

import concourse.bass as bass
from concourse import mybir

F32 = mybir.dt.float32
BF16 = mybir.dt.bfloat16
F32R = mybir.dt.float32r
ALU = mybir.AluOpType
ACT = mybir.ActivationFunctionType
X = mybir.AxisListType.X
XY = mybir.AxisListType.XY

B, D, PATCH = 8, 192, 64
S = PATCH + 1
KC, DC = 2, 96
NT = 5
HALF = 4 * S
NH, HD, HC = 12, 16, 6
TOKK = 8
EPS = 1e-5
HT = 128
MAGIC = 12582912.0
QMAX, SMIN = 255.0, 1e-8
LN2, EXP_A, EXP_B, EXP_C, N_EXP = 0.6931471805599453, 0.35815147, 0.96963238, 1.0, 30
E0, T0 = 8, 6
E1 = 16
ROWS = 50
GROUPS = 13
SLOT = 32


def build(nc, t):
    with ExitStack() as ctx:
        def sb(name, shape, dt=F32):
            return ctx.enter_context(nc.sbuf_tensor(name, shape, dt))

        def sem(name):
            return ctx.enter_context(nc.semaphore(name))

        PB = [ctx.enter_context(nc.psum_tensor(f"bank{i}", [128, 512], F32)) for i in range(8)]

        class Area:
            def __init__(self, name, words):
                self.raw, self.at, self.words = sb(name, [128, words]), 0, words

            def take(self, p, shape):
                n = 1
                for d in shape:
                    n *= d
                assert self.at + n <= self.words
                flat = self.raw[0:p, self.at:self.at + n]
                self.at += n
                names = "abcd"[:len(shape)]
                return flat.rearrange(f"p ({' '.join(names)}) -> p {' '.join(names)}", **dict(zip(names[1:], shape[1:])))

            def again(self):
                self.at = 0

        embed_area = Area("embed_area", ROWS * S + B * NH * (HD + 1) + 4 * D)
        patches = embed_area.take(128, [TOKK, B * PATCH])
        w_tok = embed_area.take(128, [TOKK, D])
        tok_bias = sb("tok_bias", [128, D])
        score_area = Area("score_area", ROWS * S)
        attn1_area = Area("attn1_area", 3 * KC * B * S + B * D + 2 * B * S + 8 * D)
        hidden_area = Area("hidden_area", ROWS * S)
        w_l0 = score_area.take(DC, [4, KC, D])
        w_gate0 = sb("w_gate0", [DC, KC, E0])
        w_gate1 = sb("w_gate1", [DC, KC, E1])
        ident = sb("ident", [128, 128])
        ident_bf = sb("ident_bf", [128, 128], BF16)
        head_mask = sb("head_mask", [DC, HC])
        cls_mask = sb("cls_mask", [DC, KC, SLOT])
        before = sb("before", [128, E0, E0])
        h = sb("h", [128, NT, D])
        xn = sb("xn", [128, NT, D])
        xt = sb("xt", [DC, KC, B * S])
        bn6 = sb("bn6", [128, NT, 6])
        mv = sb("mv", [128, NT, 2])
        var_eps = sb("var_eps", [128, NT])
        std = sb("std", [128, NT])
        rstd = sb("rstd", [128, NT])
        newton = sb("newton", [128, NT])
        eps_c = sb("eps_c", [128, 1])
        q0, k0, o0 = (attn1_area.take(DC, [KC, B, S]) for _ in range(3))
        v0 = attn1_area.take(S, [B, D])
        s0, a0 = (attn1_area.take(S, [B, S]) for _ in range(2))
        logits = sb("logits", [128, NT, E1])
        probs = sb("probs", [128, NT, E1])
        rmax = sb("rmax", [128, NT])
        rsum = sb("rsum", [128, NT])
        rinv = sb("rinv", [128, NT])
        cmp_a = sb("cmp_a", [128, NT, E0, E0])
        cmp_b = sb("cmp_b", [128, NT, E0, E0])
        rank = sb("rank", [128, NT, E0])
        top8 = sb("top8", [128, NT, 8])
        left = sb("left", [128, NT, E1])
        chosen = sb("chosen", [128, NT, E1])
        comb0 = sb("comb0", [128, NT, E0])
        comb1 = sb("comb1", [128, NT, E1])
        raw_area = Area("raw_area", 2 * (KC * T0 * HT + T0 * D))
        fc_raw = raw_area.take(DC, [2, KC, T0 * HT])
        pj_raw = raw_area.take(128, [2, T0, D])
        fc_hi = sb("fc_hi", [DC, 2, KC, T0 * HT], F32R)
        fc_lo = sb("fc_lo", [DC, 2, KC, T0 * HT], F32R)
        pj_hi = sb("pj_hi", [128, 2, T0, D], F32R)
        pj_lo = sb("pj_lo", [128, 2, T0, D], F32R)
        xt_hi = sb("xt_hi", [DC, KC, B * S], F32R)
        xt_lo = sb("xt_lo", [DC, KC, B * S], F32R)
        hid_hi = sb("hid_hi", [128, 2, B * S], F32R)
        hid_lo = sb("hid_lo", [128, 2, B * S], F32R)
        o0_cls = sb("o0_cls", [DC, KC, B])
        hid = hidden_area.take(128, [2, B * S])
        hid_w = hidden_area.take(128, [2, B * S])
        tok_w_b = hidden_area.take(128, [2, B * S])
        comb_r = sb("comb_r", [128, NT, 2 * E1], F32R)
        comb_t = sb("comb_t", [2 * E1, B * S])
        one_expert = sb("one_expert", [2 * E1, 2, B * S], F32R)
        pick0 = sb("pick0", [2 * E0, E0 + 2])
        pick1 = sb("pick1", [2 * E1, E1 + 2])
        ones_r = sb("ones_r", [2 * E1, 128], F32R)
        ones_f = sb("ones_f", [2 * E1, 128])
        zeros = sb("zeros", [128, HALF], BF16)
        wq_raw = attn1_area.take(DC, [8, D])
        wq_amax = sb("wq_amax", [DC, 8])
        wq_scale = sb("wq_scale", [DC, 8])
        wq_inv = sb("wq_inv", [DC, 8])
        wq_int = score_area.take(DC, [8, D])
        w_qkv_t = sb("w_qkv_t", [DC, KC, 6 * DC], F32R)
        w_proj_t = sb("w_proj_t", [DC, KC, D], BF16)
        b_qkv = sb("b_qkv", [DC, 6])
        b_proj = sb("b_proj", [128, D])
        proj_scale = sb("proj_scale", [128, D])
        attn1_area.again()
        qkv = attn1_area.take(DC, [6, B, S])
        qkv_int = sb("qkv_int", [DC, 6, B, S], BF16)
        k_heads = attn1_area.take(DC, [6, B * S]).rearrange("p a b -> p (a b)").bitcast(BF16).rearrange(
            "p (j b h s) -> p j b h s", j=KC, b=B, h=HC)
        q_cls = sb("q_cls", [DC, KC, B, SLOT], BF16)
        for area in (embed_area, raw_area, score_area, attn1_area, hidden_area):
            area.again()
        v1 = embed_area.take(S, [B, NH, HD + 1])
        neg_n = embed_area.take(128, [ROWS, S // 2 + 1]).rearrange("p r s -> p (r s)").bitcast(BF16)[:, 0:ROWS * S].rearrange(
            "p (r s) -> p r s", s=S)
        pow2 = raw_area.take(128, [ROWS, S])
        v1_flat = raw_area.take(S, [B, D])
        o1 = embed_area.take(128, [4, NH, HD])
        sc = score_area.take(128, [ROWS, S])
        qexp = hidden_area.take(128, [ROWS, S])
        e_t = attn1_area.take(S, [ROWS, 128])
        row_hi = sb("row_hi", [128, ROWS])
        row_lo = sb("row_lo", [128, ROWS])
        cls_sum = sb("cls_sum", [128, 2])
        o_inv = sb("o_inv", [128, 4, NH, 2])
        o1_int = sb("o1_int", [128, 4, NH * HD], BF16)
        o_cls_m = sb("o_cls_m", [DC, B * KC, NH])
        o_cls = sb("o_cls", [DC, B * KC])
        o1_t = sb("o1_t", [DC, KC, B * S], BF16)
        y1 = xn
        stat_q = sb("stat_q", [DC, 2, 6])
        stat_s = sb("stat_s", [128, 2])
        stat_o = sb("stat_o", [128, 10])
        stat_y = sb("stat_y", [128, 4])
        red = sb("red", [12, 4])
        g_q = sb("g_q", [128, 12])
        g_s = sb("g_s", [128, 2])
        g_o = sb("g_o", [128, 10])
        g_y = sb("g_y", [128, 4])
        ext = sb("ext", [128, 6])
        ext_t = sb("ext_t", [128, 6])
        ext_c = sb("ext_c", [128, 6])
        ext_q = sb("ext_q", [128, 6])
        c = sb("consts", [128, 64])
        columns = {}

        def col(name, n=1):
            if name not in columns:
                columns[name] = (sum(w for _, w in columns.values()), n)
                assert sum(w for _, w in columns.values()) <= 64
            at, w = columns[name]
            return c[:, at:at + w]

        def colp(name, p, i=0):
            at, _ = columns[name]
            return c[0:p, at + i:at + i + 1]

        for name in ("s1", "s1_inv", "s1_z", "s1_lo", "s1_hi", "gmax", "gneg", "qk", "alpha", "sa", "sa_inv", "sa_z", "sa_lo",
                     "sa_hi", "ceil_t", "ceil_r", "x0", "neg_inv_x0", "neg_x0_30", "floor_shift", "half_b", "b_t",
                     "b_r", "c_t", "c_r", "half_b2", "poly_c", "so", "so_inv", "so_z", "so_lo", "so_hi", "alpha_o", "omax",
                     "oneg", "sy", "sy_inv", "sy_z", "sy_lo", "sy_hi", "ymax", "yneg", "magic"):
            col(name)
        for name in ("s2", "s2_inv", "s2_z", "s2_lo", "s2_hi", "ratio"):
            col(name, 3)

        tok_in = [sem(f"tok_in{k}") for k in range(TOKK)]
        bias_in = sem("bias_in")
        w_l0_in = sem("w_l0_in")
        consts_in = sem("consts_in")
        gates_in = sem("gates_in")
        wq_in = sem("wq_in")
        bq_in = sem("bq_in")
        raw_in = [sem(f"raw_in{s}") for s in range(2)]
        w_hi_done = [sem(f"w_hi_done{s}") for s in range(2)]
        w_lo_done = [sem(f"w_lo_done{s}") for s in range(2)]
        dve_done = sem("dve_done")
        act_done = sem("act_done")
        tok_mm = sem("tok_mm")
        ident_ready = sem("ident_ready")
        mv_ready = sem("mv_ready")
        eps_ready = sem("eps_ready")
        std_ready = sem("std_ready")
        rstd_ready = sem("rstd_ready")
        xn_ready = sem("xn_ready")
        xt_mm = sem("xt_mm")
        xt_act = sem("xt_act")
        xt_dve = sem("xt_dve")
        q0_mm = sem("q0_mm")
        k0_mm = sem("k0_mm")
        q0_ready = sem("q0_ready")
        k0_ready = sem("k0_ready")
        v0_mm = sem("v0_mm")
        v0_ready = sem("v0_ready")
        s0_mm = sem("s0_mm")
        s0_ready = sem("s0_ready")
        a0_ready = sem("a0_ready")
        o0_mm = sem("o0_mm")
        o0_ready = sem("o0_ready")
        y0_mm = sem("y0_mm")
        gate_mm = sem("gate_mm")
        soft_in = sem("soft_in")
        soft_exp = sem("soft_exp")
        logits_out = sem("logits_out")
        comb_ready = sem("comb_ready")
        comb_mm = sem("comb_mm")
        comb_t_ready = sem("comb_t_ready")
        xhi_ready = sem("xhi_ready")
        xlo_ready = sem("xlo_ready")
        picked = [sem(f"picked{n}") for n in range(2)]
        entry_mm = [sem(f"entry_mm{n}") for n in range(2)]
        entry_out = [sem(f"entry_out{n}") for n in range(2)]
        weighted = [sem(f"weighted{n}") for n in range(2)]
        hid_hi_ready = [sem(f"hid_hi_ready{n}") for n in range(2)]
        hid_lo_ready = [sem(f"hid_lo_ready{n}") for n in range(2)]
        pj_mm = [sem(f"pj_mm{n}") for n in range(2)]
        sum_act = sem("sum_act")
        sum_dve = sem("sum_dve")
        back_mm = sem("back_mm")
        h_done = sem("h_done")
        wint_ready = sem("wint_ready")
        wint_t_mm = sem("wint_t_mm")
        wint_t_ready = sem("wint_t_ready")
        pscale_mm = sem("pscale_mm")
        qkv_mm = sem("qkv_mm")
        qkv_ready = sem("qkv_ready")
        stat_ready = sem("stat_ready")
        stat_t = sem("stat_t")
        red_ready = sem("red_ready")
        stat_b = sem("stat_b")
        s2_ready = sem("s2_ready")
        v_act = sem("v_act")
        v_dve = sem("v_dve")
        n_ready = sem("n_ready")
        t_ready = sem("t_ready")
        alpha_ready = sem("alpha_ready")
        inv_x0_ready = sem("inv_x0_ready")
        poly_ready = sem("poly_ready")
        v_int_ready = sem("v_int_ready")
        qk_ready = sem("qk_ready")
        v1_ones = sem("v1_ones")
        v1_mm = sem("v1_mm")
        v1_ready = sem("v1_ready")
        sc_mm = sem("sc_mm")
        sc_ready = sem("sc_ready")
        y_ready = sem("y_ready")
        qexp_ready = sem("qexp_ready")
        pow2_ready = sem("pow2_ready")
        rem_ready = sem("rem_ready")
        sq_ready = sem("sq_ready")
        e_ready = sem("e_ready")
        et_mm = sem("et_mm")
        et_act = sem("et_act")
        et_dve = sem("et_dve")
        pv_mm = sem("pv_mm")
        pvc_mm = sem("pvc_mm")
        o1_ready = sem("o1_ready")
        o1t_mm = sem("o1t_mm")
        o1t_ready = sem("o1t_ready")
        ocls_ready = sem("ocls_ready")
        y1_mm = sem("y1_mm")
        h_ready = sem("h_ready")
        out_done = sem("out_done")

        def tile_tokens(fm, kc, i):
            return fm[:, kc, i * 128:i * 128 + rows(i)]

        def pairs(cols):
            return cols.rearrange("p (i q) -> p i q", q=2 * S)

        def cls_cols(cols):
            return pairs(cols)[:, :, 0:2 * S:2 * S - 1]

        def patch_at(b):
            return 1 if b % 2 == 0 else 0

        def half(fm, kc, n):
            return fm[:, kc, 4 * n:4 * n + 4, :]

        def xt_half(kc, n):
            return xt[:, kc, n * HALF:(n + 1) * HALF]

        def xt_patches(r, j, i):
            if r % 2 == 0:
                return pairs(xt[:, j, :])[:, i:i + 2, 1:129]
            return xt[:, j, i * 128:(i + 2) * 128].rearrange("p (i q) -> p i q", i=2)

        def rows(i):
            return 128 if i < 4 else B

        CHUNKS = [(0, 12), (12, 24), (24, 36), (36, 50)]
        SUMS = [2, 3, 4, 5]
        PAIRS = [(0, 1), (6, 7)]

        class Run:
            def __init__(self, layer, tiles, per, iters, tiles0=0, entries0=0, experts0=0, load0=0):
                self.layer, self.tiles, self.per, self.iters = layer, tiles, per, iters
                self.unit = tiles // 2
                self.experts = tiles // per
                self.tiles0, self.entries0, self.experts0, self.load0 = tiles0, entries0, experts0, load0
                self.entries = []
                for e in range(self.experts):
                    self.entries.append(("w", e))
                    self.entries += [("h", e * per + j) for j in range(per)]
                self.entries[0], self.entries[1] = self.entries[1], self.entries[0]
                self.width = (T0 if layer == 0 else 4)

            def tile(self, it):
                return it * self.tiles + self.tiles0

            def entry(self, it):
                return it * len(self.entries) + self.entries0

            def expert(self, it):
                return it * self.experts + self.experts0

        RUNS = [[Run(0, 2 * T0, T0, E0 // 2)],
                [Run(1, 8, 1, 1, load0=4), Run(1, 8, 2, 1, 8, 16, 8, 5), Run(1, 8, 2, 1, 16, 28, 12, 6)]]

        def run_rounds(eng, layer, start, body):
            runs = RUNS[layer]
            start(runs[0], 0)
            if layer == 0:
                run = runs[0]
                with eng.Fori(0, run.iters - 1) as it:
                    body(run, it, (run, it + 1))
                body(run, run.iters - 1, None)
            else:
                for n, run in enumerate(runs):
                    body(run, 0, (runs[n + 1], 0) if n + 1 < len(runs) else None)

        block = ctx.enter_context(nc.Block())

        @block.sync
        def _(sp):
            for k in range(TOKK):
                sp.dma_start(patches[:, k, :], t["patches"][k]).then_inc(tok_in[k], 16)
                sp.dma_start(w_tok[:, k, :], t["w_tok"][k]).then_inc(tok_in[k], 16)
            sp.dma_start(w_l0[:], t["w_l0"]).then_inc(w_l0_in, 16)
            def load(s, fc, pj, w):
                sp.dma_start(fc_raw[:, s, :, 0:w * HT], fc).then_inc(raw_in[s], 16)
                sp.dma_start(pj_raw[:, s, 0:w, :], pj).then_inc(raw_in[s], 16)

            def wait_split(s, n):
                sp.wait_ge(w_hi_done[s], 3 * n)
                sp.wait_ge(w_lo_done[s], 3 * n)

            for s in range(2):
                load(s, t["fc0"][s], t["pj0"][s], T0)
            with sp.Fori(1, E0 // 2) as it:
                for s in range(2):
                    wait_split(s, it)
                    load(s, t["fc0"][bass.ds(it * 2 + s, 1)].squeeze(0), t["pj0"][bass.ds(it * 2 + s, 1)].squeeze(0), T0)
            for n in range(3):
                for s in range(2):
                    wait_split(s, E0 // 2 + n)
                    if (n, s) == (0, 1):
                        sp.wait_ge(pvc_mm, 1)
                        sp.wait_ge(e_ready, len(CHUNKS))
                    load(s, t["fc1"][2 * n + s], t["pj1"][2 * n + s], 4)
            for b in range(B):
                lo = (b % 2) * PATCH
                if b % 4 == 0:
                    sp.wait_ge(h_done, 4 + b // 4)
                sp.dma_start(t["out"][b, 1:S, :], h[lo:lo + PATCH, b // 2, :]).then_inc(out_done, 16)
            sp.wait_ge(h_done, 6)
            sp.dma_start(t["out"][:, 0, :], h[0:B, 4, :]).then_inc(out_done, 16)
            sp.wait_ge(out_done, 16 * (B + 1))

        @block.gpsimd
        def _(pool):
            pool.dma_start(wq_raw[:, 0:6, :], t["w_qkv"]).then_inc(wq_in, 16)
            pool.dma_start(wq_raw[:, 6:8, :], t["w_proj"]).then_inc(wq_in, 16)
            pool.dma_start(ident[:], t["ident"]).then_inc(consts_in, 16)
            pool.dma_start(head_mask[:], t["head_mask"]).then_inc(consts_in, 16)
            pool.dma_start(cls_mask[:], t["cls_mask"]).then_inc(consts_in, 16)
            pool.dma_start(before[:], t["before"]).then_inc(consts_in, 16)
            pool.dma_start(tok_bias[:], t["tok_bias"].partition_broadcast(128)).then_inc(bias_in, 16)
            pool.dma_start(h[0:B, 4, :], t["cls_tok"].partition_broadcast(B)).then_inc(bias_in, 16)
            pool.dma_start(pick0[:], t["pick0"]).then_inc(gates_in, 16)
            pool.dma_start(pick1[:], t["pick1"]).then_inc(gates_in, 16)
            pool.dma_start(w_gate0[:], t["w_gate0"]).then_inc(gates_in, 16)
            pool.dma_start(w_gate1[:], t["w_gate1"]).then_inc(gates_in, 16)
            pool.dma_start(b_qkv[:], t["b_qkv"]).then_inc(bq_in, 16)
            pool.dma_start(b_proj[:], t["b_proj"].partition_broadcast(128)).then_inc(bq_in, 16)

            def split_lo(s, n, w):
                for piece in range(3):
                    pool.wait_ge(w_hi_done[s], n * 3 + (piece - 2))
                    lo, raw, hi = [(fc[:, s, piece, 0:w * HT] if piece < 2 else pj[:, s, 0:w, :])
                                   for fc, pj in ((fc_lo, pj_lo), (fc_raw, pj_raw), (fc_hi, pj_hi))]
                    pool.tensor_tensor(lo, raw, hi.bitcast(F32), ALU.subtract).then_inc(w_lo_done[s], 1)

            split_lo(0, 1, T0)
            split_lo(1, 1, T0)
            with pool.Fori(2, E0 // 2 + 1) as n:
                for s in range(2):
                    split_lo(s, n, T0)
            split_lo(0, E0 // 2 + 1, 4)
            for s, n in ((1, 0), (0, 1), (1, 1), (0, 2), (1, 2)):
                split_lo(s, E0 // 2 + 1 + n, 4)

        @block.tensor
        def _(pe):
            def wait_xt(r):
                pe.wait_ge(xt_act, 4 * (r + 1))
                pe.wait_ge(xt_dve, 2 * (r + 1))

            def transpose_x(r):
                for i in range(NT):
                    pe.wait_ge(xn_ready, NT * r + i + 1)
                    n = rows(i)
                    for j in range(KC):
                        at = (i % 2) * 256 + j * 128 if i < 4 else j * B
                        last = pe.transpose(PB[i // 2][0:DC, at:at + n], xn[0:n, i, j * DC:(j + 1) * DC],
                                            ident[0:n, 0:n])
                    last.then_inc(xt_mm, 1)

            def wait_split_x(n):
                pe.wait_ge(xhi_ready, 2 * n)
                pe.wait_ge(xlo_ready, 2 * n)

            def mm_kc(out, lhs, rhs, n=KC):
                for kc in range(n):
                    last = pe.matmul(out, lhs(kc), rhs(kc), start=(kc == 0), stop=(kc == n - 1))
                return last

            def gate(r, w, n):
                wait_xt(r)
                pe.wait_ge(gates_in, 64)
                for i in range(NT):
                    last = mm_kc(PB[3][0:rows(i), i * n:(i + 1) * n],
                                 lambda kc: tile_tokens(xt, kc, i), lambda kc: w[:, kc, :])
                last.then_inc(gate_mm, 1)

            def split3(out, lhs, rhs, start, stop, last_kc=KC):
                for n, (a, b) in enumerate(((0, 0), (0, 1), (1, 0))):
                    mm = pe.matmul(out, lhs[a], rhs[b], start=start and n == 0, stop=stop and n == 2,
                                   skip_group_check=True)
                return mm

            def comb_turn(layer, n_exp):
                pe.wait_ge(comb_ready, layer + 1)
                for i in range(NT):
                    n = rows(i)
                    out = PB[2][0:2 * n_exp, i * 128:(i + 1) * 128] if i < 4 else PB[3][0:2 * n_exp, 0:B]
                    last = pe.transpose(out, comb_r[0:n, i, 0:2 * n_exp].bitcast(F32), ident[0:n, 0:n])
                last.then_inc(comb_mm, 1)

            def clear_sums(layer):
                pe.wait_ge(comb_t_ready, 2 * (layer + 1))
                for k in SUMS:
                    mm = pe.matmul(PB[k][0:DC, 0:HALF], zeros[:, 0:DC], zeros[:], start=True, stop=True,
                                   skip_group_check=True)
                mm.then_inc(pj_mm[layer], 1)

            def ffn(y, n_exp):

                def entry(run, it, k, first=False):
                    kind, x = run.entries[k]
                    if kind == "w":
                        pe.wait_ge(picked[y], run.expert(it) + (x + 1))
                    else:
                        s, j = x // run.unit, x % run.unit
                        if j == 0:
                            pe.wait_ge(w_lo_done[s], it * 3 + 3 * (run.load0 + 1))
                    for n in range(2):
                        if not first:
                            pe.wait_ge(entry_out[y], 2 * run.entry(it) + (2 * k - 3 + n))
                        out = PB[PAIRS[k % 2][n]][:, 0:HALF]
                        if kind == "w":
                            mm = pe.matmul(out, ones_r[0:2 * n_exp, :],
                                           one_expert[0:2 * n_exp, x % 2, n * HALF:(n + 1) * HALF],
                                           start=True, stop=True)
                        else:
                            for kc in range(KC):
                                cols, tok = slice(j * HT, (j + 1) * HT), slice(n * HALF, (n + 1) * HALF)
                                mm = split3(out, (fc_hi[:, s, kc, cols], fc_lo[:, s, kc, cols]),
                                            (xt_hi[:, kc, tok], xt_lo[:, kc, tok]), kc == 0, kc == KC - 1)
                        mm.then_inc(entry_mm[y], 1)

                def project(run, it, g):
                    s, j = g // run.unit, g % run.unit
                    pe.wait_ge(hid_lo_ready[y], run.tile(it) + (g + 1))
                    for c in range(KC):
                        for n in range(2):
                            cols, tok = slice(c * DC, (c + 1) * DC), slice(n * HALF, (n + 1) * HALF)
                            mm = split3(PB[SUMS[2 * c + n]][0:DC, 0:HALF], (pj_hi[:, s, j, cols], pj_lo[:, s, j, cols]),
                                        (hid_hi[:, g % 2, tok], hid_lo[:, g % 2, tok]), False, True)
                    mm.then_inc(pj_mm[y], 1)

                def start(run, it, first=True):
                    for k in range(2):
                        entry(run, it, k, first)

                def body(run, it, following):
                    for k in range(2, len(run.entries)):
                        entry(run, it, k)
                        if run.entries[k][0] == "h":
                            project(run, it, run.entries[k][1] - 1)
                    if following:
                        start(*following, first=False)
                    project(run, it, run.tiles - 1)

                run_rounds(pe, y, start, body)

            def turn_back(layer):
                for i in range(NT):
                    pe.wait_ge(sum_act, 2 * (layer + 1))
                    if i >= 2:
                        pe.wait_ge(sum_dve, 2 * (layer + 1))
                    for c in range(KC):
                        last = pe.transpose(PB[(0, 1, 6)[i // 2]][0:rows(i), (i % 2) * D + c * DC:(i % 2) * D + (c + 1) * DC],
                                            tile_tokens(xt, c, i), ident[0:DC, 0:DC])
                    if i % 2 or i == 4:
                        last.then_inc(back_mm, 1)

            def statistics(r, stat, n, p, out_cols):
                pe.wait_ge(stat_ready, r + 1)
                pe.transpose(PB[6][0:n, 0:p], stat, ident[0:p, 0:p]).then_inc(stat_t, 1)
                pe.wait_ge(red_ready, r + 1)
                pe.matmul(PB[7][:, 0:n], red[0:n, r:r + 1].broadcast_to([n, 128]), ident[0:n, 0:n],
                          start=True, stop=True).then_inc(stat_b, 1)

            for k in range(TOKK):
                pe.wait_ge(tok_in[k], 32)
                for i in range(4):
                    mm = pe.matmul(PB[i][:, 0:D], patches[:, k, i * 128:(i + 1) * 128], w_tok[:, k, :],
                                   start=(k == 0), stop=(k == TOKK - 1))
                    if k == TOKK - 1:
                        mm.then_inc(tok_mm, 1)
            pe.wait_ge(consts_in, 64)
            pe.wait_ge(wint_ready, 1)
            for hr in range(2):
                for kc in range(KC):
                    for j in range(4):
                        last = pe.transpose(PB[4 + 2 * hr + kc][0:DC, j * DC:(j + 1) * DC],
                                            wq_int[:, 4 * hr + j, kc * DC:(kc + 1) * DC], ident[0:DC, 0:DC])
                    if hr:
                        last = pe.matmul(PB[6 + kc][:, 4 * DC:5 * DC], wq_scale[:, 6 + kc:7 + kc].broadcast_to([DC, 128]),
                                         ident[0:DC, 0:DC], start=True, stop=True)
                    last.then_inc(wint_t_mm, 1)
            transpose_x(0)
            wait_xt(0)
            pe.wait_ge(w_l0_in, 16)
            pe.wait_ge(wint_t_ready, 6)
            for w, done in ((0, q0_mm), (1, k0_mm)):
                for j in range(KC):
                    for n in range(2):
                        mm_kc(PB[4 * w + 2 * j + n][0:DC, 0:HALF], lambda kc: w_l0[:, w, kc, j * DC:(j + 1) * DC],
                              lambda kc: xt_half(kc, n)).then_inc(done, 1)
            for b in range(B):
                if b % 2 == 0:
                    pe.wait_ge(q0_ready, b // 2 + 1)
                last = mm_kc(PB[b // 2][0:S, (b % 2) * D:(b % 2 + 1) * D], lambda kc: xt[:, kc, b * S:(b + 1) * S],
                             lambda kc: w_l0[:, 2, kc, :])
                if b % 2:
                    last.then_inc(v0_mm, 1)
            pe.wait_ge(q0_ready, 4)
            pe.wait_ge(k0_ready, 4)
            for b in range(B):
                last = mm_kc(PB[4 + b // 4][0:S, (b % 4) * S:(b % 4 + 1) * S], lambda kc: k0[:, kc, b, :],
                             lambda kc: q0[:, kc, b, :])
                if b % 4 == 3:
                    last.then_inc(s0_mm, 1)
            pe.wait_ge(v0_ready, 4)
            for n in range(2):
                pe.wait_ge(a0_ready, n + 1)
                for j in range(KC):
                    bank = PB[(6, 0)[n] + j]
                    for b in range(4 * n, 4 * n + 4):
                        last = pe.matmul(bank[0:DC, (b % 4) * S:(b % 4 + 1) * S], v0[:, b, j * DC:(j + 1) * DC],
                                         a0[:, b, :], start=True, stop=True)
                    last.then_inc(o0_mm, 1)
            pe.wait_ge(o0_ready, 5)
            o0_cols = o0.rearrange("p j b s -> p j (b s)")
            for i in range(NT):
                lhs = o0_cols[:, :, 2 * S * i + 1:2 * S * i + 129] if i < 4 else o0_cls
                last = mm_kc(PB[2 + i // 2][0:rows(i), (i % 2) * D:(i % 2 + 1) * D],
                             lambda kc: lhs[:, kc, :], lambda kc: w_l0[:, 3, kc, :])
                if i % 2 or i == 4:
                    last.then_inc(y0_mm, 1)
            transpose_x(1)
            gate(1, w_gate0, E0)
            comb_turn(0, E0)
            clear_sums(0)
            wait_split_x(1)
            ffn(0, E0)
            turn_back(0)
            transpose_x(2)
            wait_split_x(2)
            for j in range(6):
                for n in range(2):
                    g = 2 * j + n
                    if g >= 8:
                        pe.wait_ge(qkv_ready, g - 7)
                    for kc in range(KC):
                        for part, x in enumerate((xt_hi, xt_lo)):
                            mm = pe.matmul(PB[g % 8][0:DC, 0:HALF], w_qkv_t[:, kc, j * DC:(j + 1) * DC],
                                           x[:, kc, n * HALF:(n + 1) * HALF], start=kc + part == 0, stop=kc + part == 2)
                    mm.then_inc(qkv_mm, 1)
            statistics(0, stat_q[:].rearrange("p a j -> p (a j)"), 12, DC, 12)
            def turn_v():
                pe.wait_ge(v_int_ready, 1)
                pe.wait_ge(ident_ready, 1)
                for b in range(B):
                    for kc in range(KC):
                        out = PB[b // 4][:, :].bitcast(BF16)[0:S, (b % 4) * D + kc * DC:(b % 4) * D + (kc + 1) * DC]
                        last = pe.transpose(out, qkv_int[:, 4 + kc, b, :], ident_bf[0:DC, 0:DC])
                    if b % 4 == 3:
                        last.then_inc(v1_mm, 1)

            pe.wait_ge(qk_ready, 1)
            for i in range(4):
                for kc in range(KC):
                    g = 2 * i + kc
                    if g >= 6:
                        pe.wait_ge(sc_ready, g - 5)
                    bank = PB[2 + g % 6]
                    for b in (2 * i, 2 * i + 1):
                        lo = (b % 2) * PATCH
                        last = pe.matmul(bank[lo:lo + PATCH, 0:HC * S], qkv_int[:, kc, b, patch_at(b):patch_at(b) + PATCH],
                                         k_heads[:, kc, b, :, :], start=True, stop=True)
                    last.then_inc(sc_mm, 1)
            pe.wait_ge(sc_ready, 3)
            for b in range(B):
                lo = SLOT * (b % 4)
                last = mm_kc(PB[4][lo:lo + SLOT, (b // 4) * S:(b // 4 + 1) * S], lambda kc: q_cls[:, kc, b, :],
                             lambda kc: qkv_int[:, 2 + kc, b, :])
            last.then_inc(sc_mm, 1)
            turn_v()
            pe.wait_ge(sc_ready, 9)
            statistics(1, stat_s[:], 2, 128, 2)
            def turn_rows(c):
                pe.wait_ge(e_ready, c + 1)
                for g in range(3 * c, 3 * c + 3 if c < 3 else GROUPS):
                    if g >= 4:
                        pe.wait_ge(et_dve if g % 2 else et_act, (g - 4) // 2 + 1)
                    for r in range(4 * g, min(4 * g + 4, ROWS)):
                        last = pe.transpose(PB[g % 4][0:S, (r % 4) * 128:(r % 4 + 1) * 128], sc[:, r, :], ident[:])
                    last.then_inc(et_mm, 1)

            def times_v(i):
                for head in range(NH):
                    r = i * NH + head
                    pe.wait_ge(et_dve if (r // 4) % 2 else et_act, (r // 4) // 2 + 1)
                    at = head * 2 * (HD + 1)
                    last = pe.matmul(PB[4 + i][:, at:at + 2 * (HD + 1)], e_t[:, r, :], v1[:, 2 * i:2 * i + 2, head, :],
                                     start=True, stop=True)
                last.then_inc(pv_mm, 1)

            pe.wait_ge(v1_ready, 4)
            turn_rows(0)
            for i in range(1, 4):
                turn_rows(i)
                times_v(i - 1)
            times_v(3)
            pe.wait_ge(et_act, 7)
            for b in range(B):
                for kc in range(KC):
                    at = (2 * b + kc) * NH
                    last = pe.matmul(PB[0][0:DC, at:at + NH], v1_flat[:, b, kc * DC:(kc + 1) * DC],
                                     e_t[:, 48 + b // 4, SLOT * (b % 4):SLOT * (b % 4) + NH], start=True, stop=True)
            last.then_inc(pvc_mm, 1)
            statistics(2, stat_o[:], 10, 128, 10)
            pe.wait_ge(o1_ready, 1)
            for i in range(4):
                for kc in range(KC):
                    at = (i % 2) * 256 + kc * 128
                    last = pe.transpose(PB[1 + i // 2][:, :].bitcast(BF16)[0:DC, at:at + 128],
                                        o1_int[:, i, kc * DC:(kc + 1) * DC], ident_bf[:])
                if i % 2:
                    last.then_inc(o1t_mm, 1)
            pe.wait_ge(o1t_ready, 2)
            pe.wait_ge(ocls_ready, 1)
            for i in range(NT):
                last = mm_kc(PB[3 + i // 2][0:rows(i), (i % 2) * D:(i % 2 + 1) * D],
                             lambda kc: tile_tokens(o1_t, kc, i), lambda kc: w_proj_t[:, kc, :])
                if i % 2 or i == 4:
                    last.then_inc(y1_mm, 1)
            statistics(3, stat_y[:], 4, 128, 4)
            transpose_x(3)
            gate(3, w_gate1, E1)
            comb_turn(1, E1)
            clear_sums(1)
            wait_split_x(3)
            ffn(1, E1)
            turn_back(1)

        @block.scalar
        def _(act):
            def layernorm(r):
                act.wait_ge(mv_ready, r + 1)
                if r == 0:
                    act.wait_ge(eps_ready, 1)
                act.activation(std[:], mv[:, :, 1], ACT.Sqrt, bias=eps_c[:]).then_inc(std_ready, 1)
                act.wait_ge(xt_mm, NT * r + 2)
                for j in range(KC):
                    src = PB[0][0:DC, :].rearrange("p (i j q) -> p i j q", i=2, j=2)[:, :, j]
                    act.activation(xt_patches(r, j, 0), src, ACT.Copy).then_inc(xt_act, 1)
                act.wait_ge(xt_mm, NT * r + 5)
                for j in range(KC):
                    to = xt[:, j, 512:520].rearrange("p (i b) -> p i b", b=2) if r % 2 else cls_cols(xt[:, j, :])
                    act.activation(to, PB[2][0:DC, j * B:(j + 1) * B].rearrange("p (i b) -> p i b", b=2),
                                   ACT.Copy).then_inc(xt_act, 1)
                if r:
                    act.wait_ge(xt_act, 4 * (r + 1))
                    act.wait_ge(xt_dve, 2 * (r + 1))
                    for j in range(KC):
                        act.activation(xt_hi[:, j, :], xt[:, j, :], ACT.Copy).then_inc(xhi_ready, 1)

            def softmax_exp(r, n):
                act.wait_ge(soft_in, r + 1)
                act.activation(probs[:, :, 0:n], logits[:, :, 0:n], ACT.Exp).then_inc(soft_exp, 1)

            def ffn(y):
                def entry(run, it, k):
                    kind, x = run.entries[k]
                    for n in range(2):
                        act.wait_ge(entry_mm[y], 2 * run.entry(it) + (2 * k + n + 1))
                        src, tok = PB[PAIRS[k % 2][n]][:, 0:HALF], slice(n * HALF, (n + 1) * HALF)
                        if kind == "w":
                            act.activation(tok_w_b[:, x % 2, tok], src, ACT.Identity).then_inc(entry_out[y], 1)
                        else:
                            act.activation(hid[:, x % 2, tok], src, ACT.Gelu_apprx_tanh).then_inc(entry_out[y], 1)

                def hi_part(run, it, x):
                    act.wait_ge(weighted[y], run.tile(it) + (x + 1))
                    act.activation(hid_hi[:, x % 2, :], hid_w[:, x % 2, :], ACT.Copy).then_inc(hid_hi_ready[y], 1)

                def start(run, it):
                    entry(run, it, 0)
                    entry(run, it, 1)
                    hi_part(run, it, 0)

                def body(run, it, following):
                    for k in range(2, len(run.entries)):
                        entry(run, it, k)
                        if run.entries[k][0] == "h":
                            hi_part(run, it, run.entries[k][1])
                    if following:
                        start(*following)

                run_rounds(act, y, start, body)

            def comb_turned(layer, n_exp):
                act.wait_ge(comb_mm, layer + 1)
                act.activation(comb_t[0:2 * n_exp, 0:512], PB[2][0:2 * n_exp, :], ACT.Copy).then_inc(comb_t_ready, 1)
                act.activation(comb_t[0:2 * n_exp, 512:520], PB[3][0:2 * n_exp, 0:B], ACT.Copy).then_inc(comb_t_ready, 1)

            def sums_out(layer):
                act.wait_ge(pj_mm[layer], 1 + (E0 * T0, 24)[layer])
                for c in range(KC):
                    act.activation(xt[:, c, 0:HALF], PB[SUMS[2 * c]][0:DC, 0:HALF], ACT.Copy).then_inc(sum_act, 1)

            for kc in range(KC):
                act.wait_ge(wint_t_mm, kc + 1)
                act.activation(w_qkv_t[:, kc, 0:4 * DC], PB[4 + kc][0:DC, 0:4 * DC], ACT.Copy).then_inc(wint_t_ready, 1)
            for kc in range(KC):
                act.wait_ge(wint_t_mm, kc + 3)
                act.activation(w_qkv_t[:, kc, 4 * DC:6 * DC], PB[6 + kc][0:DC, 0:2 * DC], ACT.Copy).then_inc(act_done, 1)
                act.activation(w_proj_t[:, kc, :], PB[6 + kc][0:DC, 2 * DC:4 * DC], ACT.Copy).then_inc(wint_t_ready, 1)
                act.activation(proj_scale[:, kc * DC:(kc + 1) * DC], PB[6 + kc][:, 4 * DC:5 * DC],
                               ACT.Copy).then_inc(wint_t_ready, 1)
            act.wait_ge(act_done, 2)
            layernorm(0)
            for j in range(KC):
                for n in range(2):
                    act.wait_ge(q0_mm, 2 * j + n + 1)
                    act.activation(half(q0, j, n), PB[2 * j + n][0:DC, 0:HALF].rearrange("p (b s) -> p b s", s=S),
                                   ACT.Copy, scale=0.1).then_inc(q0_ready, 1)
            for g in range(4):
                act.wait_ge(v0_mm, g + 1)
                act.activation(v0[:, 2 * g:2 * g + 2, :], PB[g][0:S, 0:2 * D].rearrange("p (b d) -> p b d", d=D),
                               ACT.Copy).then_inc(v0_ready, 1)
            for n in range(2):
                act.wait_ge(s0_mm, n + 1)
                act.activation(s0[:, 4 * n:4 * n + 4, :], PB[4 + n][0:S, 0:HALF].rearrange("p (b s) -> p b s", s=S),
                               ACT.Copy, scale=0.1).then_inc(s0_ready, 1)
            for n in range(2):
                for j in range(KC):
                    act.wait_ge(o0_mm, 2 * n + j + 1)
                    act.activation(half(o0, j, n), PB[(6, 0)[n] + j][0:DC, 0:HALF].rearrange("p (b s) -> p b s", s=S),
                                   ACT.Copy).then_inc(o0_ready, 1)
            act.wait_ge(o0_ready, 4)
            for j in range(KC):
                last = act.activation(o0_cls[:, j, :].rearrange("p (i b) -> p i b", b=2),
                                      cls_cols(o0[:, j].rearrange("p b s -> p (b s)")), ACT.Copy)
                if j == 0:
                    last.then_inc(act_done, 1)
            act.wait_ge(act_done, 3)
            last.then_inc(o0_ready, 1)
            layernorm(1)
            softmax_exp(0, E0)
            comb_turned(0, E0)
            ffn(0)
            sums_out(0)
            layernorm(2)
            act.wait_ge(bq_in, 32)
            for j in range(6):
                for n in range(2):
                    g = 2 * j + n
                    act.wait_ge(qkv_mm, g + 1)
                    act.activation(half(qkv, j, n), PB[g % 8][0:DC, 0:HALF].rearrange("p (b s) -> p b s", s=S),
                                   ACT.Identity, scale=wq_scale[:, j:j + 1], bias=b_qkv[:, j:j + 1]).then_inc(qkv_ready, 1)
            v = qkv[:, 4:6]
            act.wait_ge(s2_ready, 1)
            act.activation(v, v, ACT.Copy, scale=colp("s1_inv", DC)).then_inc(v_act, 1)
            act.wait_ge(v_dve, 1)
            act.activation(v, v, ACT.Copy, bias=MAGIC).then_inc(v_act, 1)
            act.wait_ge(v_act, 2)
            act.activation(v, v, ACT.Copy, bias=-MAGIC).then_inc(v_act, 1)
            act.wait_ge(v_act, 3)
            act.activation(v, v, ACT.Copy, scale=colp("ratio", DC, 2)).then_inc(v_act, 1)
            act.wait_ge(v_dve, 2)
            act.activation(v, v, ACT.Copy, bias=MAGIC).then_inc(v_act, 1)
            act.wait_ge(v_act, 5)
            act.activation(qkv_int[:, 4:6], v, ACT.Copy, bias=-MAGIC).then_inc(v_int_ready, 1)
            for g in range(8):
                act.wait_ge(sc_mm, g + 1)
                act.activation(sc[:, HC * g:HC * (g + 1), :], PB[2 + g % 6][:, 0:HC * S].rearrange("p (h s) -> p h s", s=S),
                               ACT.Copy).then_inc(sc_ready, 1)
            act.wait_ge(sc_mm, 9)
            act.activation(sc[:, 48:50, :], PB[4][:, 0:2 * S].rearrange("p (h s) -> p h s", s=S),
                           ACT.Copy).then_inc(sc_ready, 1)
            for n in range(2):
                act.wait_ge(v1_mm, n + 1)
                act.wait_ge(v1_ones, 1)
                if n == 0:
                    act.wait_ge(w_lo_done[0], 3 * (E0 // 2 + 1))
                    act.wait_ge(w_lo_done[1], 3 * (E0 // 2))
                src = PB[n][:, :].bitcast(BF16)[0:S, 0:4 * D].rearrange("p (b h d) -> p b h d", b=4, h=NH)
                act.activation(v1[:, 4 * n:4 * n + 4, :, 0:HD], src, ACT.Copy).then_inc(v1_ready, 1)
                act.activation(v1_flat[:, 4 * n:4 * n + 4, :].rearrange("p b (h d) -> p b h d", h=NH), src,
                               ACT.Copy).then_inc(v1_ready, 1)
            act.wait_ge(alpha_ready, 1)
            for n, (a, z) in enumerate(CHUNKS):
                act.activation(sc[:, a:z, :], sc[:, a:z, :], ACT.Identity, scale=col("alpha"),
                               bias=col("magic")).then_inc(t_ready, 1)

            def quotient(n):
                a, z = CHUNKS[n]
                act.wait_ge(n_ready, n + 1)
                act.activation(qexp[:, a:z, :], neg_n[:, a:z, :], ACT.Identity, scale=col("neg_inv_x0"),
                               bias=col("floor_shift")).then_inc(y_ready, 1)

            def power(n):
                a, z = CHUNKS[n]
                act.wait_ge(qexp_ready, n + 1)
                act.activation(pow2[:, a:z, :], qexp[:, a:z, :], ACT.Exp, scale=-LN2).then_inc(pow2_ready, 1)

            def square(n):
                a, z = CHUNKS[n]
                act.wait_ge(rem_ready, n + 1)
                act.activation(sc[:, a:z, :], sc[:, a:z, :], ACT.Square, bias=col("half_b")).then_inc(sq_ready, 1)

            act.wait_ge(inv_x0_ready, 1)
            quotient(0)
            for n in range(1, len(CHUNKS)):
                quotient(n)
                power(n - 1)
            power(len(CHUNKS) - 1)
            act.wait_ge(poly_ready, 1)
            for n in range(len(CHUNKS)):
                square(n)
            for g in range(0, GROUPS, 2):
                n = min(4, ROWS - 4 * g)
                act.wait_ge(et_mm, g + 1)
                act.activation(e_t[:, 4 * g:4 * g + n, :], PB[g % 4][0:S, 0:n * 128].rearrange("p (r q) -> p r q", q=128),
                               ACT.Copy).then_inc(et_act, 1)
            for g in range(2):
                act.wait_ge(o1t_mm, g + 1)
                src = PB[1 + g][:, :].bitcast(BF16)[0:DC, 0:512].rearrange("p (i j q) -> p i j q", i=2, j=2)
                for kc in range(KC):
                    last = act.activation(o1_t[:, kc, 256 * g:256 * (g + 1)].rearrange("p (i q) -> p i q", i=2),
                                          src[:, :, kc], ACT.Copy)
                    if kc == 0:
                        last.then_inc(act_done, 1)
                act.wait_ge(act_done, 4 + g)
                last.then_inc(o1t_ready, 1)
            layernorm(3)
            softmax_exp(1, E1)
            comb_turned(1, E1)
            ffn(1)
            sums_out(1)

        @block.vector
        def _(dve):
            steps = [0]

            def then(ins):
                steps[0] += 1
                ins.then_inc(dve_done, 1)
                dve.wait_ge(dve_done, steps[0])

            def settle(ins):
                steps[0] += 1
                ins.then_inc(dve_done, 1)

            def layernorm(r):
                for i in range(NT):
                    settle(dve.bn_stats(bn6[0:rows(i), i, :], h[0:rows(i), i, :]))
                dve.wait_ge(dve_done, steps[0])
                for i in range(NT):
                    last = dve.bn_aggr(mv[0:rows(i), i, :], bn6[0:rows(i), i, :])
                    if i < NT - 1:
                        settle(last)
                dve.wait_ge(dve_done, steps[0])
                last.then_inc(mv_ready, 1)
                dve.wait_ge(mv_ready, r + 1)
                then(dve.tensor_scalar(var_eps[:], mv[:, :, 1], EPS, None, ALU.add))
                dve.wait_ge(std_ready, r + 1)
                then(dve.reciprocal(rstd[:], std[:]))
                then(dve.scalar_tensor_tensor(newton[:], rstd[:], -0.5, rstd[:], ALU.mult, ALU.mult))
                then(dve.tensor_tensor(newton[:], newton[:], var_eps[:], ALU.mult))
                dve.scalar_tensor_tensor(rstd[:], newton[:], 1.5, rstd[:], ALU.add, ALU.mult).then_inc(rstd_ready, 1)
                dve.wait_ge(rstd_ready, r + 1)
                for i in range(NT):
                    n = rows(i)
                    dve.tensor_scalar(xn[0:n, i, :], h[0:n, i, :], mv[0:n, i, 0:1], rstd[0:n, i:i + 1],
                                      ALU.subtract, ALU.mult).then_inc(xn_ready, 1)
                dve.wait_ge(xt_mm, NT * r + 4)
                for j in range(KC):
                    src = PB[1][0:DC, :].rearrange("p (i j q) -> p i j q", i=2, j=2)[:, :, j]
                    dve.tensor_copy(xt_patches(r, j, 2), src).then_inc(xt_dve, 1)

            def split_x(r):
                for j in range(KC):
                    dve.wait_ge(xhi_ready, 2 * (r - 1) + j + 1)
                    dve.tensor_tensor(xt_lo[:, j, :], xt[:, j, :], xt_hi[:, j, :].bitcast(F32),
                                      ALU.subtract).then_inc(xlo_ready, 1)

            def softmax(r, n):
                dve.wait_ge(gate_mm, r + 1)
                settle(dve.tensor_copy(logits[:, 0:4, 0:n], PB[3][:, 0:4 * n].rearrange("p (i e) -> p i e", e=n)))
                then(dve.tensor_copy(logits[0:B, 4, 0:n], PB[3][0:B, 4 * n:5 * n]))
                split_x(2 * r + 1)
                lg, pr = logits[:, :, 0:n], probs[:, :, 0:n]
                then(dve.tensor_reduce(rmax[:], lg, X, ALU.max))
                dve.tensor_tensor(lg, lg, rmax[:].unsqueeze(2).broadcast_to([128, NT, n]), ALU.subtract).then_inc(soft_in, 1)
                dve.wait_ge(soft_exp, r + 1)
                then(dve.tensor_reduce(rsum[:], pr, X, ALU.add))
                then(dve.reciprocal(rinv[:], rsum[:]))
                then(dve.tensor_tensor(pr, pr, rinv[:].unsqueeze(2).broadcast_to([128, NT, n]), ALU.mult))

            def combine(out, n):
                pr, ch = probs[:, :, 0:n], chosen[:, :, 0:n]
                then(dve.tensor_tensor(ch, ch, pr, ALU.mult))
                then(dve.tensor_reduce(rsum[:], ch, X, ALU.add))
                then(dve.reciprocal(rinv[:], rsum[:]))
                then(dve.tensor_tensor(out[:], ch, rinv[:].unsqueeze(2).broadcast_to([128, NT, n]), ALU.mult))
                then(dve.tensor_copy(comb_r[:, :, 0:n], out[:]))
                dve.tensor_tensor(comb_r[:, :, n:2 * n], out[:], comb_r[:, :, 0:n].bitcast(F32),
                                  ALU.subtract).then_inc(comb_ready, 1)

            def pick(layer, n_exp, e, slot):
                src, cols = comb_t[0:2 * n_exp, :], (pick0, pick1)[layer]
                w = cols[:, e:e + 1] if isinstance(e, int) else cols[:, bass.ds(e, 1)]
                return dve.tensor_scalar(one_expert[0:2 * n_exp, slot, :], src, w, None, ALU.mult)

            def split_hi(s, piece, w, n):
                if piece == 0:
                    dve.wait_ge(raw_in[s], 32 * n)
                if piece < 2:
                    ins = dve.tensor_copy(fc_hi[:, s, piece, 0:w * HT], fc_raw[:, s, piece, 0:w * HT])
                else:
                    ins = dve.tensor_copy(pj_hi[:, s, 0:w, :], pj_raw[:, s, 0:w, :])
                ins.then_inc(w_hi_done[s], 1)

            def ffn(y, n_exp):
                def tile(run, it, x):
                    e, s, j = x // run.per, x // run.unit, x % run.unit
                    k = run.entries.index(("h", x))
                    dve.wait_ge(entry_out[y], 2 * run.entry(it) + 2 * max(k + 1, 2))
                    dve.tensor_tensor(hid_w[:, x % 2, :], hid[:, x % 2, :], tok_w_b[:, e % 2, :],
                                      ALU.mult).then_inc(weighted[y], 1)
                    dve.wait_ge(hid_hi_ready[y], run.tile(it) + (x + 1))
                    dve.tensor_tensor(hid_lo[:, x % 2, :], hid_w[:, x % 2, :], hid_hi[:, x % 2, :].bitcast(F32),
                                      ALU.subtract).then_inc(hid_lo_ready[y], 1)
                    if x % run.per == 0:
                        pick(y, n_exp, run.expert(it) + (e + 2), e % 2).then_inc(picked[y], 1)
                    if j <= 1 and not (run is RUNS[1][-1] and s == 1):
                        if j == 0:
                            dve.wait_ge(pj_mm[y], run.tile(it) + (run.unit * s + 1))
                        for piece in ((0, 1), (2,))[j]:
                            split_hi(1 - s, piece, run.width, it + (run.load0 + 1 + s))

                def start(run, it):
                    tile(run, it, 0)

                def body(run, it, following):
                    for x in range(1, run.tiles):
                        tile(run, it, x)
                    if following:
                        start(*following)

                run_rounds(dve, y, start, body)

            def start_picks(layer, n_exp):
                dve.wait_ge(comb_t_ready, 2 * (layer + 1))
                for e in range(2):
                    pick(layer, n_exp, e, e).then_inc(picked[layer], 1)

            def add_sums(layer):
                dve.wait_ge(pj_mm[layer], 1 + (E0 * T0, 24)[layer])
                for c in range(KC):
                    dve.tensor_copy(xt[:, c, HALF:2 * HALF], PB[SUMS[2 * c + 1]][0:DC, 0:HALF]).then_inc(sum_dve, 1)
                for g in range(3):
                    dve.wait_ge(back_mm, 3 * layer + g + 1)
                    n, w = (128, 2) if g < 2 else (B, 1)
                    hh = h[0:n, 2 * g:2 * g + w, :]
                    dve.tensor_tensor(hh, hh, PB[(0, 1, 6)[g]][0:n, 0:w * D].rearrange("p (i d) -> p i d", d=D),
                                      ALU.add).then_inc(h_done, 1)
                dve.wait_ge(h_done, 3 * (layer + 1))

            def statistics(r, n, p, out):
                dve.wait_ge(stat_t, r + 1)
                dve.tensor_reduce(red[0:n, r:r + 1], PB[6][0:n, 0:p], X, ALU.max).then_inc(red_ready, 1)
                dve.wait_ge(stat_b, r + 1)
                then(dve.tensor_copy(out, PB[7][:, 0:n]))

            def scale_of(name, top, negmin, factor=None):
                if factor is None:
                    then(dve.tensor_scalar(col(name), top, negmin, 1.0 / QMAX, ALU.add, ALU.mult))
                    then(dve.tensor_scalar(col(name), col(name), SMIN, None, ALU.max))
                else:
                    then(dve.scalar_tensor_tensor(col(name), top, negmin, factor, ALU.add, ALU.mult))
                    then(dve.tensor_scalar(col(name), col(name), 1.0 / QMAX, SMIN, ALU.mult, ALU.max))
                then(dve.reciprocal(col(name + "_inv"), col(name)))

            def zero_of(name, negmin, inv):
                then(dve.tensor_scalar(col(name + "_z"), negmin, inv, MAGIC, ALU.mult, ALU.add))
                settle(dve.tensor_scalar(col(name + "_lo"), col(name + "_z"), MAGIC, -1.0, ALU.subtract, ALU.mult))
                then(dve.tensor_scalar(col(name + "_hi"), col(name + "_z"), -1.0, MAGIC + QMAX, ALU.mult, ALU.add))

            settle(dve.memset(mv[:], 1.0))
            settle(dve.memset(col("magic"), MAGIC))
            settle(dve.memset(xn[:, 4, :], 0.0))
            settle(dve.memset(logits[:], 0.0))
            settle(dve.memset(ones_f[:], 1.0))
            settle(dve.memset(zeros[:], 0.0))
            settle(dve.memset(stat_o[:], -3.0e38))
            settle(dve.memset(stat_y[:], -3.0e38))
            dve.memset(eps_c[:], EPS).then_inc(eps_ready, 1)
            dve.wait_ge(consts_in, 64)
            dve.tensor_copy(ident_bf[:], ident[:]).then_inc(ident_ready, 1)
            dve.wait_ge(dve_done, steps[0])
            settle(dve.tensor_copy(ones_r[:], ones_f[:]))
            dve.wait_ge(wq_in, 32)
            then(dve.tensor_reduce(wq_amax[:], wq_raw[:], X, ALU.max, apply_absolute_value=True))
            then(dve.tensor_scalar(wq_scale[:], wq_amax[:], 1.0 / 127.0, SMIN, ALU.mult, ALU.max))
            then(dve.reciprocal(wq_inv[:], wq_scale[:]))
            then(dve.tensor_tensor(wq_int[:], wq_raw[:], wq_inv[:].unsqueeze(2).broadcast_to([DC, 8, D]), ALU.mult))
            then(dve.tensor_scalar(wq_int[:], wq_int[:], MAGIC, MAGIC, ALU.add, ALU.subtract))
            dve.tensor_scalar(wq_int[:], wq_int[:], -128.0, 127.0, ALU.max, ALU.min).then_inc(wint_ready, 1)
            dve.wait_ge(bias_in, 32)
            for i in range(4):
                dve.wait_ge(tok_mm, i + 1)
                settle(dve.tensor_tensor(h[:, i, :], PB[i][:, 0:D], tok_bias[:], ALU.add))
            dve.wait_ge(dve_done, steps[0])
            layernorm(0)
            for j in range(KC):
                for n in range(2):
                    dve.wait_ge(k0_mm, 2 * j + n + 1)
                    dve.tensor_scalar(half(k0, j, n), PB[4 + 2 * j + n][0:DC, 0:HALF].rearrange("p (b s) -> p b s", s=S),
                                      0.1, None, ALU.mult).then_inc(k0_ready, 1)
            for piece in range(3):
                split_hi(0, piece, T0, 1)
            for n in range(2):
                dve.wait_ge(s0_ready, n + 1)
                s = s0[:, 4 * n:4 * n + 4, :]
                dve.scalar_tensor_tensor(a0[:, 4 * n:4 * n + 4, :], s, 1.0, s, ALU.add, ALU.mult).then_inc(a0_ready, 1)
            for g in range(3):
                dve.wait_ge(y0_mm, g + 1)
                n, w = (128, 2) if g < 2 else (B, 1)
                hh = h[0:n, 2 * g:2 * g + w, :]
                settle(dve.scalar_tensor_tensor(hh, PB[2 + g][0:n, 0:w * D].rearrange("p (i d) -> p i d", d=D), 0.1, hh,
                                                ALU.mult, ALU.add))
            dve.wait_ge(dve_done, steps[0])
            layernorm(1)
            softmax(0, E0)
            shape = [128, NT, E0, E0]
            rival = probs[:, :, 0:E0].unsqueeze(2).broadcast_to(shape)
            own = probs[:, :, 0:E0].unsqueeze(3).broadcast_to(shape)
            settle(dve.tensor_tensor(cmp_a[:], rival, own, ALU.is_gt))
            then(dve.tensor_tensor(cmp_b[:], rival, own, ALU.is_equal))
            then(dve.tensor_tensor(cmp_b[:], cmp_b[:], before[:].unsqueeze(1).broadcast_to(shape), ALU.mult))
            then(dve.tensor_tensor(cmp_a[:], cmp_a[:], cmp_b[:], ALU.add))
            then(dve.tensor_reduce(rank[:], cmp_a[:], X, ALU.add))
            then(dve.tensor_scalar(chosen[:, :, 0:E0], rank[:], 1.5, None, ALU.is_lt))
            combine(comb0, E0)
            start_picks(0, E0)
            ffn(0, E0)
            add_sums(0)

            layernorm(2)
            split_x(2)
            dve.memset(v1[:], 1.0).then_inc(v1_ones, 1)
            for j in range(6):
                dve.wait_ge(qkv_ready, 2 * j + 2)
                settle(dve.tensor_reduce(stat_q[:, 0, j:j + 1], qkv[:, j], XY, ALU.max))
                last = dve.tensor_reduce(stat_q[:, 1, j:j + 1], qkv[:, j], XY, ALU.min, negate=True)
                if j < 5:
                    settle(last)
            dve.wait_ge(dve_done, steps[0])
            last.then_inc(stat_ready, 1)
            statistics(0, 12, DC, g_q[:])
            then(dve.tensor_reduce(ext[:], g_q[:].rearrange("p (a j) -> p a j", j=2), X, ALU.max))
            settle(dve.tensor_reduce(col("gmax"), ext[:, 0:3], X, ALU.max))
            then(dve.tensor_reduce(col("gneg"), ext[:, 3:6], X, ALU.max))
            scale_of("s1", col("gmax"), col("gneg"))
            zero_of("s1", col("gneg"), col("s1_inv"))
            then(dve.tensor_scalar(ext[:, 3:6], ext[:, 3:6], -1.0, None, ALU.mult))
            then(dve.tensor_scalar(ext_t[:], ext[:], col("s1_inv"), col("s1_lo"), ALU.mult, ALU.max))
            then(dve.tensor_scalar(ext_c[:], ext_t[:], col("s1_hi"), MAGIC, ALU.min, ALU.add))
            then(dve.tensor_scalar(ext_q[:], ext_c[:], MAGIC, col("s1"), ALU.subtract, ALU.mult))
            s2, s2i = col("s2"), col("s2_inv")
            then(dve.tensor_tensor(s2, ext_q[:, 0:3], ext_q[:, 3:6], ALU.subtract))
            then(dve.tensor_scalar(s2, s2, 1.0 / QMAX, SMIN, ALU.mult, ALU.max))
            then(dve.reciprocal(s2i, s2))
            settle(dve.tensor_scalar(col("ratio"), s2i, col("s1"), None, ALU.mult))
            then(dve.tensor_tensor(col("s2_z"), ext_q[:, 3:6], s2i, ALU.mult))
            then(dve.tensor_scalar(col("s2_z"), col("s2_z"), -1.0, MAGIC, ALU.mult, ALU.add))
            then(dve.tensor_scalar(col("s2_lo"), col("s2_z"), MAGIC, -1.0, ALU.subtract, ALU.mult))
            dve.tensor_scalar(col("s2_hi"), col("s2_z"), -1.0, MAGIC + QMAX, ALU.mult, ALU.add).then_inc(s2_ready, 1)
            dve.wait_ge(s2_ready, 1)
            z = qkv[:, 0:4]
            then(dve.tensor_scalar(z, z, colp("s1_inv", DC), colp("s1_lo", DC), ALU.mult, ALU.max))
            then(dve.tensor_scalar(z, z, colp("s1_hi", DC), MAGIC, ALU.min, ALU.add))
            for part in range(2):
                z = qkv[:, 2 * part:2 * part + 2]
                settle(dve.tensor_scalar(z, z, MAGIC, colp("ratio", DC, part), ALU.subtract, ALU.mult))
            dve.wait_ge(dve_done, steps[0])
            for part in range(2):
                z = qkv[:, 2 * part:2 * part + 2]
                settle(dve.tensor_scalar(z, z, colp("s2_lo", DC, part), colp("s2_hi", DC, part), ALU.max, ALU.min))
            dve.wait_ge(dve_done, steps[0])
            then(dve.tensor_scalar(qkv_int[:, 0:4], qkv[:, 0:4], MAGIC, MAGIC, ALU.add, ALU.subtract))
            v = qkv[:, 4:6]
            dve.wait_ge(v_act, 1)
            dve.tensor_scalar(v, v, colp("s1_lo", DC), colp("s1_hi", DC), ALU.max, ALU.min).then_inc(v_dve, 1)
            for kc in range(KC):
                q = cls_cols(qkv_int[:, kc].rearrange("p b s -> p (b s)")).unsqueeze(3).broadcast_to([DC, 4, 2, SLOT])
                own = cls_mask[:, kc, :].unsqueeze(1).unsqueeze(1).broadcast_to([DC, 4, 2, SLOT])
                settle(dve.tensor_tensor(q_cls[:, kc].rearrange("p (i b) m -> p i b m", b=2), q, own, ALU.mult))
            for head in range(HC):
                last = dve.tensor_scalar(k_heads[:, :, :, head, :], qkv_int[:, 2:4], head_mask[:, head:head + 1], None,
                                         ALU.mult)
                if head < HC - 1:
                    settle(last)
            dve.wait_ge(dve_done, steps[0])
            last.then_inc(qk_ready, 1)
            dve.wait_ge(v_act, 4)
            dve.tensor_scalar(v, v, colp("s2_lo", DC, 2), colp("s2_hi", DC, 2), ALU.max, ALU.min).then_inc(v_dve, 1)
            for g in range(9):
                a, z = (HC * g, HC * g + HC) if g < 8 else (48, 50)
                dve.wait_ge(sc_ready, g + 1)
                settle(dve.tensor_reduce(row_hi[:, a:z], sc[:, a:z, :], X, ALU.max))
                settle(dve.tensor_reduce(row_lo[:, a:z], sc[:, a:z, :], X, ALU.min, negate=True))
            dve.wait_ge(dve_done, steps[0])
            then(dve.tensor_reduce(stat_s[:, 0:1], row_hi[:], X, ALU.max))
            dve.tensor_reduce(stat_s[:, 1:2], row_lo[:], X, ALU.max).then_inc(stat_ready, 1)
            statistics(1, 2, 128, g_s[:])
            then(dve.tensor_tensor(col("qk"), c[:, columns["s2"][0]:columns["s2"][0] + 1],
                                   c[:, columns["s2"][0] + 1:columns["s2"][0] + 2], ALU.mult))
            then(dve.tensor_scalar(col("qk"), col("qk"), float(HD) ** -0.5, None, ALU.mult))
            scale_of("sa", g_s[:, 0:1], g_s[:, 1:2], col("qk"))
            dve.tensor_tensor(col("alpha"), col("qk"), col("sa_inv"), ALU.mult).then_inc(alpha_ready, 1)
            dve.wait_ge(alpha_ready, 1)
            zero_of("sa", g_s[:, 1:2], col("alpha"))
            settle(dve.tensor_scalar(col("sa_lo"), col("sa_lo"), MAGIC, None, ALU.add))
            settle(dve.tensor_scalar(col("sa_hi"), col("sa_hi"), MAGIC, None, ALU.add))
            then(dve.tensor_scalar(row_hi[:], row_hi[:], col("alpha"), MAGIC, ALU.mult, ALU.add))
            then(dve.tensor_scalar(row_hi[:], row_hi[:], col("sa_lo"), col("sa_hi"), ALU.max, ALU.min))
            def ts(out, a, x, y, op0, op1):
                return lambda: dve.tensor_scalar(col(out), col(a), x, y, op0, op1)

            def tt(out, a, b, op):
                return lambda: dve.tensor_tensor(col(out), col(a), col(b), op)

            x0_steps = [
                ts("ceil_t", "sa_inv", LN2, None, ALU.mult, ALU.bypass),
                ts("ceil_r", "ceil_t", MAGIC, MAGIC, ALU.add, ALU.subtract),
                tt("x0", "ceil_t", "ceil_r", ALU.is_gt),
                tt("x0", "x0", "ceil_r", ALU.add),
                lambda: dve.reciprocal(col("neg_inv_x0"), col("x0")),
                ts("neg_inv_x0", "neg_inv_x0", -1.0, None, ALU.mult, ALU.bypass),
            ]
            poly_steps = [
                ts("b_t", "sa_inv", EXP_B / EXP_A, None, ALU.mult, ALU.bypass),
                ts("b_r", "b_t", MAGIC, MAGIC, ALU.add, ALU.subtract),
                tt("b_t", "b_r", "b_t", ALU.is_gt),
                tt("b_r", "b_r", "b_t", ALU.subtract),
                tt("c_t", "sa_inv", "sa_inv", ALU.mult),
                ts("c_t", "c_t", EXP_C / EXP_A, None, ALU.mult, ALU.bypass),
                ts("c_r", "c_t", MAGIC, MAGIC, ALU.add, ALU.subtract),
                tt("c_t", "c_r", "c_t", ALU.is_gt),
                tt("c_r", "c_r", "c_t", ALU.subtract),
                ts("half_b", "b_r", 0.5, None, ALU.mult, ALU.bypass),
                tt("half_b2", "half_b", "half_b", ALU.mult),
            ]
            for step in x0_steps:
                then(step())
            settle(dve.tensor_scalar(col("neg_x0_30"), col("x0"), -float(N_EXP), None, ALU.mult))
            dve.tensor_scalar(col("floor_shift"), col("neg_inv_x0"), -0.5, -0.5, ALU.mult, ALU.add).then_inc(inv_x0_ready, 1)
            for n, (a, z) in enumerate(CHUNKS):
                s = sc[:, a:z, :]
                top = row_hi[:, a:z].unsqueeze(2).broadcast_to([128, z - a, S])
                dve.wait_ge(t_ready, n + 1)
                settle(dve.scalar_tensor_tensor(neg_n[:, a:z, :], s, col("sa_lo"), top, ALU.max, ALU.subtract))
                clipped = steps[0]
                if poly_steps:
                    settle(poly_steps.pop(0)())
                dve.wait_ge(dve_done, clipped)
                dve.tensor_scalar(neg_n[:, a:z, :], neg_n[:, a:z, :], 0.0, col("neg_x0_30"), ALU.min,
                                  ALU.max).then_inc(n_ready, 1)
                if poly_steps:
                    dve.wait_ge(dve_done, steps[0])
                    then(poly_steps.pop(0)())
            for n, (a, z) in enumerate(CHUNKS):
                dve.wait_ge(y_ready, n + 1)
                dve.tensor_scalar(qexp[:, a:z, :], qexp[:, a:z, :], MAGIC, MAGIC, ALU.add,
                                  ALU.subtract).then_inc(qexp_ready, 1)
                for step in poly_steps[:1]:
                    then(poly_steps.pop(0)())
                dve.wait_ge(qexp_ready, n + 1)
                dve.scalar_tensor_tensor(sc[:, a:z, :], qexp[:, a:z, :], col("x0"), neg_n[:, a:z, :], ALU.mult,
                                         ALU.add).then_inc(rem_ready, 1)
            while poly_steps:
                then(poly_steps.pop(0)())
            dve.tensor_tensor(col("poly_c"), col("c_r"), col("half_b2"), ALU.subtract).then_inc(poly_ready, 1)
            dve.wait_ge(poly_ready, 1)
            for n, (a, z) in enumerate(CHUNKS):
                dve.wait_ge(sq_ready, n + 1)
                last = dve.scalar_tensor_tensor(sc[:, a:z, :], sc[:, a:z, :], col("poly_c"), pow2[:, a:z, :],
                                                ALU.add, ALU.mult)
                if n < len(CHUNKS) - 1:
                    last.then_inc(e_ready, 1)
            then(last)
            then(dve.tensor_reduce(cls_sum[:], sc[:, 48:50, :], X, ALU.add))
            then(dve.reciprocal(cls_sum[:], cls_sum[:]))
            dve.tensor_tensor(sc[:, 48:50, :], sc[:, 48:50, :], cls_sum[:].unsqueeze(2).broadcast_to([128, 2, S]),
                              ALU.mult).then_inc(e_ready, 1)
            for g in range(1, GROUPS, 2):
                n = min(4, ROWS - 4 * g)
                dve.wait_ge(et_mm, g + 1)
                dve.tensor_copy(e_t[:, 4 * g:4 * g + n, :],
                                PB[g % 4][0:S, 0:n * 128].rearrange("p (r q) -> p r q", q=128)).then_inc(et_dve, 1)
            for i in range(4):
                dve.wait_ge(pv_mm, i + 1)
                acc = PB[4 + i][:, 0:2 * NH * (HD + 1)].rearrange("p (h b d) -> p h b d", h=NH, b=2)
                then(dve.reciprocal(o_inv[:, i], acc[:, :, :, HD]))
                for b in range(2):
                    lo = PATCH * b
                    settle(dve.tensor_tensor(o1[lo:lo + PATCH, i], acc[lo:lo + PATCH, :, b, 0:HD],
                                             o_inv[lo:lo + PATCH, i, :, b].unsqueeze(2).broadcast_to([PATCH, NH, HD]),
                                             ALU.mult))
                dve.wait_ge(dve_done, steps[0])
                settle(dve.tensor_reduce(stat_o[:, i:i + 1], o1[:, i], XY, ALU.max))
                settle(dve.tensor_reduce(stat_o[:, 5 + i:6 + i], o1[:, i], XY, ALU.min, negate=True))
            dve.wait_ge(pvc_mm, 1)
            ocm = o_cls_m[:].rearrange("p (b j) h -> p b j h", j=KC)
            src = PB[0][0:DC, 0:B * KC * NH].rearrange("p (b j h) -> p b j h", b=B, j=KC)
            own = cls_mask[:, :, 0:NH].unsqueeze(1).broadcast_to([DC, B, KC, NH])
            then(dve.tensor_tensor(ocm, src, own, ALU.mult))
            then(dve.tensor_reduce(o_cls[:], o_cls_m[:], X, ALU.add))
            flat = o1[:].rearrange("p i h d -> p (i h d)")
            settle(dve.tensor_reduce(stat_o[0:DC, 4:5], o_cls[:], X, ALU.max))
            last = dve.tensor_reduce(stat_o[0:DC, 9:10], o_cls[:], X, ALU.min, negate=True)
            dve.wait_ge(dve_done, steps[0])
            last.then_inc(stat_ready, 1)
            statistics(2, 10, 128, g_o[:])
            settle(dve.tensor_reduce(col("omax"), g_o[:, 0:5], X, ALU.max))
            then(dve.tensor_reduce(col("oneg"), g_o[:, 5:10], X, ALU.max))
            sv = c[:, columns["s2"][0] + 2:columns["s2"][0] + 3]
            scale_of("so", col("omax"), col("oneg"), sv)
            then(dve.tensor_tensor(col("alpha_o"), sv, col("so_inv"), ALU.mult))
            zero_of("so", col("oneg"), col("alpha_o"))
            settle(dve.tensor_scalar(o_cls[:], o_cls[:], colp("alpha_o", DC), colp("so_lo", DC), ALU.mult, ALU.max))
            then(dve.tensor_scalar(flat, flat, col("alpha_o"), col("so_lo"), ALU.mult, ALU.max))
            settle(dve.tensor_scalar(o_cls[:], o_cls[:], colp("so_hi", DC), MAGIC, ALU.min, ALU.add))
            then(dve.tensor_scalar(flat, flat, col("so_hi"), MAGIC, ALU.min, ALU.add))
            dve.tensor_scalar(o1_int[:].rearrange("p i f -> p (i f)"), flat, MAGIC, None, ALU.subtract).then_inc(o1_ready, 1)
            dve.tensor_scalar(o1_t[:, :, 512:520].rearrange("p j b -> p b j"),
                              o_cls[:].rearrange("p (b j) -> p b j", j=KC), MAGIC, None, ALU.subtract).then_inc(ocls_ready, 1)
            dve.wait_ge(wint_t_ready, 6)
            then(dve.tensor_scalar(proj_scale[:], proj_scale[:], col("so"), None, ALU.mult))
            dve.wait_ge(bq_in, 32)
            for g in range(3):
                dve.wait_ge(y1_mm, g + 1)
                n, w = (128, 2) if g < 2 else (B, 1)
                yy = y1[0:n, 2 * g:2 * g + w, :]
                then(dve.tensor_tensor(yy, PB[3 + g][0:n, 0:w * D].rearrange("p (i d) -> p i d", d=D),
                                       proj_scale[0:n, :].unsqueeze(1).broadcast_to([n, w, D]), ALU.mult))
                then(dve.tensor_tensor(yy, yy, b_proj[0:n, :].unsqueeze(1).broadcast_to([n, w, D]), ALU.add))
            patch_y, cls_y = y1[:, 0:4, :], y1[0:B, 4, :]
            settle(dve.tensor_reduce(stat_y[:, 0:1], patch_y, XY, ALU.max))
            settle(dve.tensor_reduce(stat_y[:, 1:2], patch_y, XY, ALU.min, negate=True))
            settle(dve.tensor_reduce(stat_y[0:B, 2:3], cls_y, X, ALU.max))
            last = dve.tensor_reduce(stat_y[0:B, 3:4], cls_y, X, ALU.min, negate=True)
            dve.wait_ge(dve_done, steps[0])
            last.then_inc(stat_ready, 1)
            statistics(3, 4, 128, g_y[:])
            settle(dve.tensor_tensor(col("ymax"), g_y[:, 0:1], g_y[:, 2:3], ALU.max))
            then(dve.tensor_tensor(col("yneg"), g_y[:, 1:2], g_y[:, 3:4], ALU.max))
            scale_of("sy", col("ymax"), col("yneg"))
            zero_of("sy", col("yneg"), col("sy_inv"))
            y = y1[:]
            then(dve.tensor_scalar(y, y, col("sy_inv"), col("sy_lo"), ALU.mult, ALU.max))
            then(dve.tensor_scalar(y, y, col("sy_hi"), MAGIC, ALU.min, ALU.add))
            then(dve.tensor_scalar(y, y, MAGIC, col("sy"), ALU.subtract, ALU.mult))
            settle(dve.tensor_tensor(h[0:B, 4, :], h[0:B, 4, :], cls_y, ALU.add))
            then(dve.tensor_tensor(h[:, 0:4, :], h[:, 0:4, :], patch_y, ALU.add))
            layernorm(3)
            softmax(1, E1)
            for i in range(NT):
                settle(dve.max(top8[:, i, :], probs[:, i, :]))
            dve.wait_ge(dve_done, steps[0])
            for i in range(NT):
                settle(dve.match_replace(left[:, i, :], top8[:, i, :], probs[:, i, :], -1.0))
            dve.wait_ge(dve_done, steps[0])
            then(dve.tensor_scalar(chosen[:], left[:], 0.0, None, ALU.is_lt))
            combine(comb1, E1)
            start_picks(1, E1)
            ffn(1, E1)
            add_sums(1)


def lay_out(np, x, cls_tok, L0_tok_w, L0_tok_b, L0_attn_Wq, L0_attn_Wk, L0_attn_Wv, L0_attn_Wo, L0_ffn_w_fc,
            L0_ffn_w_proj, L0_ffn_w_gate, L1_attn_w_qkv, L1_attn_b_qkv, L1_attn_w_proj, L1_attn_b_proj,
            L1_ffn_router_w, L1_ffn_w1, L1_ffn_w2):
    def chunks(w):
        return w.reshape(KC, DC, -1).transpose(1, 0, 2)

    feature = np.arange(DC) // HD
    column = np.arange(SLOT) % NH
    a = {
        "patches": x.reshape(B, 8, 32, 8, 32).transpose(2, 4, 0, 1, 3).reshape(TOKK, 128, B * PATCH),
        "w_tok": L0_tok_w.T.reshape(TOKK, 128, D),
        "tok_bias": L0_tok_b,
        "cls_tok": cls_tok.reshape(D),
        "w_l0": np.stack([chunks(w.T) for w in (L0_attn_Wq, L0_attn_Wk, L0_attn_Wv, L0_attn_Wo)], axis=1),
        "w_gate0": chunks(L0_ffn_w_gate),
        "w_gate1": chunks(L1_ffn_router_w.T),
        "fc0": L0_ffn_w_fc.reshape(KC, DC, T0 * 128, E0).transpose(3, 1, 0, 2),
        "pj0": L0_ffn_w_proj.reshape(T0, 128, D, E0).transpose(3, 1, 0, 2),
        "w_qkv": L1_attn_w_qkv.reshape(6, DC, D).transpose(1, 0, 2),
        "w_proj": L1_attn_w_proj.reshape(KC, DC, D).transpose(1, 0, 2),
        "b_qkv": L1_attn_b_qkv.reshape(6, DC).T,
        "b_proj": L1_attn_b_proj,
        "fc1": L1_ffn_w1.reshape(KC, DC, 6, 512).transpose(2, 1, 0, 3),
        "pj1": L1_ffn_w2.reshape(6, 4, 128, D).transpose(0, 2, 1, 3),
        "pick0": np.eye(E0, E0 + 2, dtype=np.float32)[np.arange(2 * E0) % E0],
        "pick1": np.eye(E1, E1 + 2, dtype=np.float32)[np.arange(2 * E1) % E1],
        "ident": np.eye(128, dtype=np.float32),
        "head_mask": (feature[:, None] == np.arange(HC)).astype(np.float32),
        "cls_mask": (feature[:, None, None] + HC * np.arange(KC)[:, None] == column).astype(np.float32),
        "before": np.broadcast_to(np.arange(E0) < np.arange(E0)[:, None], (128, E0, E0)).astype(np.float32),
    }
    return {k: np.ascontiguousarray(v) for k, v in a.items()}


def kernel(**inputs):
    import numpy as np
    import concourse.bacc as bacc
    from concourse.bass_utils import run_bass_kernel_spmd

    arrays = lay_out(np, **{k: np.asarray(v) for k, v in inputs.items()})
    nc = bacc.Bacc("TRN2", target_bir_lowering=False, num_devices=1)
    t = {k: nc.dram_tensor(k + "_dram", v.shape, mybir.dt.from_np(v.dtype), kind="ExternalInput").ap()
         for k, v in arrays.items()}
    t["out"] = nc.dram_tensor("out_dram", (B, S, D), F32, kind="ExternalOutput").ap()
    build(nc, t)
    r = run_bass_kernel_spmd(nc, [{k + "_dram": v for k, v in arrays.items()}], core_ids=[0])
    return r.results[0]["out_dram"]
```
